# Optimizing a Trainium2 kernel written in Bass

```python
import numpy as np
import jax
import jax.numpy as jnp

def _softmax(x, axis=-1):
    return jax.nn.softmax(x, axis=axis)

def _gelu(x):
    return jax.nn.gelu(x, approximate=True)

def _silu(x):
    return jax.nn.silu(x)

def _sigmoid(x):
    return jax.nn.sigmoid(x)

def _layernorm(x, axis=-1, eps=1e-05):
    m = jnp.mean(x, axis=axis, keepdims=True)
    v = jnp.var(x, axis=axis, keepdims=True)
    return (x - m) / jnp.sqrt(v + eps)

def _scatter_add(tgt, idx, src, axis=0):
    return tgt.at[idx].add(src)

def _segment_sum(src, seg, n):
    return jax.ops.segment_sum(src, seg, n)
kernel_name = 'mk_gnn_preln_d4_gnn_r32_689bed'

def setup_inputs(seed: int=0):
    np.random.seed(seed)
    _w = jnp.asarray

    def _rec_inputs():
        import jax
        import jax.numpy as jnp
        _gk = jax.random.key(seed)
        x = -0.0009044 + 1 * jax.random.normal(jax.random.fold_in(_gk, 1), (3125, 16), jnp.float32)
        src = jax.random.randint(jax.random.fold_in(_gk, 2), (100000,), 0, 3125, jnp.int32)
        dst = jnp.minimum((3125 * jax.random.uniform(jax.random.fold_in(_gk, 3), (100000,)) ** 2.0).astype(jnp.int32), 99999)
        _o = jnp.argsort(dst, stable=True)
        src = src[_o]
        dst = dst[_o]
        edge_attr_16 = 0.000254407 + 0.99978 * jax.random.normal(jax.random.fold_in(_gk, 12), (100000, 16), jnp.float32)
        edge_attr_8 = -5.3897e-05 + 0.999841 * jax.random.normal(jax.random.fold_in(_gk, 13), (100000, 8), jnp.float32)
        edge_type_8 = jax.random.randint(jax.random.fold_in(_gk, 15), (100000,), 0, 8, jnp.int32)
        node_vec1 = -0.00472126 + 0.997171 * jax.random.normal(jax.random.fold_in(_gk, 16), (3125, 1), jnp.float32)
        return (x, src, dst, edge_attr_16, edge_attr_8, edge_type_8, node_vec1)
    x, src, dst, edge_attr_16, edge_attr_8, edge_type_8, node_vec1 = _rec_inputs()

    def _L0_gnn_setup():
        import jax, jax.numpy as jnp
        import numpy as np
        N_NODES = 3125
        N_EDGES = 15625
        IND = 16
        OUT = 16
        EDGE_DIM = 16
        HID = IND * OUT
        BN_EPS = 1e-05
        key = jax.random.key(seed)
        ks = jax.random.split(key, 12)
        x = jax.random.normal(ks[0], (N_NODES, IND), dtype=jnp.float32)
        edge_index = jax.random.randint(ks[1], (2, N_EDGES), 0, N_NODES, dtype=jnp.int64)
        edge_attr = jax.random.normal(ks[2], (N_EDGES, EDGE_DIM), dtype=jnp.float32)
        W1 = jax.random.normal(ks[3], (EDGE_DIM, HID), dtype=jnp.float32) * (1.0 / np.sqrt(EDGE_DIM))
        b1 = jnp.zeros((HID,), dtype=jnp.float32)
        W2 = jax.random.normal(ks[4], (HID, HID), dtype=jnp.float32) * (1.0 / np.sqrt(HID))
        b2 = jnp.zeros((HID,), dtype=jnp.float32)
        root = jax.random.normal(ks[5], (IND, OUT), dtype=jnp.float32) * (1.0 / np.sqrt(IND))
        bias = jnp.zeros((OUT,), dtype=jnp.float32)
        gamma = jnp.ones((OUT,), dtype=jnp.float32)
        beta = jnp.zeros((OUT,), dtype=jnp.float32)
        return {'x': x, 'edge_index': edge_index, 'edge_attr': edge_attr, 'W1': W1, 'b1': b1, 'W2': W2, 'b2': b2, 'root': root, 'bias': bias, 'gamma': gamma, 'beta': beta}
    _L0_gnn_all = _L0_gnn_setup()
    _L0_gnn_in = {k: v for k, v in _L0_gnn_all.items() if k in ('W1', 'b1', 'W2', 'b2', 'root', 'bias', 'gamma', 'beta')}
    del _L0_gnn_all

    def _L1_gnn_setup():
        import jax, jax.numpy as jnp
        import numpy as np
        N_NODES = 3125
        N_EDGES = 100000
        D_NODE = 16
        D_EDGE = 8
        D_HIDDEN = 16
        key = jax.random.key(seed)
        ks = jax.random.split(key, 8)
        node_features = jax.random.normal(ks[0], (N_NODES, D_NODE), dtype=jnp.float32)
        edge_attr_e3nn = jax.random.normal(ks[1], (N_EDGES, D_EDGE), dtype=jnp.float32)
        node_attr_scalar_raw = jax.random.normal(ks[2], (N_NODES, 1), dtype=jnp.float32)
        W_msg_tp = jax.random.normal(ks[3], (D_NODE, D_EDGE, D_HIDDEN), dtype=jnp.float32)
        W_msg_lin = jax.random.normal(ks[4], (D_HIDDEN, D_HIDDEN), dtype=jnp.float32)
        W_upd_tp = jax.random.normal(ks[5], (D_NODE, D_HIDDEN, D_HIDDEN), dtype=jnp.float32)
        W_upd_lin = jax.random.normal(ks[6], (D_HIDDEN, D_NODE), dtype=jnp.float32)
        edge_index = jax.random.randint(ks[7], (2, N_EDGES), 0, N_NODES, dtype=jnp.int64)
        return {'node_features': node_features, 'edge_attr_e3nn': edge_attr_e3nn, 'node_attr_scalar_raw': node_attr_scalar_raw, 'W_msg_tp': W_msg_tp, 'W_msg_lin': W_msg_lin, 'W_upd_tp': W_upd_tp, 'W_upd_lin': W_upd_lin, 'edge_index': edge_index}
    _L1_gnn_all = _L1_gnn_setup()
    _L1_gnn_in = {k: v for k, v in _L1_gnn_all.items() if k in ('W_msg_tp', 'W_msg_lin', 'W_upd_tp', 'W_upd_lin')}
    del _L1_gnn_all

    def _L2_gnn_setup():
        import jax, jax.numpy as jnp
        import numpy as np
        NUM_ENTITIES = 3125
        NUM_RELATIONS = 8
        NUM_CLASSES = 16
        HIDDEN = 16
        NUM_EDGES = 100000

        def rgcn_conv(x, src, dst, edge_type, W, root, bias):
            num_nodes = x.shape[0]
            x_src = x[src]
            msg = jnp.zeros((src.shape[0], W.shape[2]), x.dtype)
            for r in range(NUM_RELATIONS):
                msg = msg + jnp.where((edge_type == r)[:, None], x_src @ W[r], jnp.zeros((), x.dtype))
            cnt = jnp.zeros((num_nodes, NUM_RELATIONS), x.dtype).at[dst, edge_type].add(1.0)
            norm = 1.0 / jnp.maximum(cnt[dst, edge_type], 1.0)
            agg = jax.ops.segment_sum(msg * norm[:, None], dst, num_segments=num_nodes)
            return agg + x @ root + bias
        key = jax.random.key(seed)
        ks = jax.random.split(key, 9)
        s = 1.0 / np.sqrt(HIDDEN)
        edge_index = jax.random.randint(ks[0], (2, NUM_EDGES), 0, NUM_ENTITIES, dtype=jnp.int32)
        edge_type = jax.random.randint(ks[1], (NUM_EDGES,), 0, NUM_RELATIONS, dtype=jnp.int32)
        return {'embed': jax.random.normal(ks[2], (NUM_ENTITIES, HIDDEN), jnp.float32), 'W1': jax.random.normal(ks[3], (NUM_RELATIONS, HIDDEN, HIDDEN), jnp.float32) * s, 'root1': jax.random.normal(ks[4], (HIDDEN, HIDDEN), jnp.float32) * s, 'b1': jnp.zeros((HIDDEN,), jnp.float32), 'W2': jax.random.normal(ks[5], (NUM_RELATIONS, HIDDEN, NUM_CLASSES), jnp.float32) * s, 'root2': jax.random.normal(ks[6], (HIDDEN, NUM_CLASSES), jnp.float32) * s, 'b2': jnp.zeros((NUM_CLASSES,), jnp.float32), 'edge_index': edge_index, 'edge_type': edge_type}
    _L2_gnn_all = _L2_gnn_setup()
    _L2_gnn_in = {k: v for k, v in _L2_gnn_all.items() if k in ('W1', 'root1', 'b1', 'W2', 'root2', 'b2')}
    del _L2_gnn_all

    def _L3_gnn_setup():
        import jax, jax.numpy as jnp
        import numpy as np
        N_NODES = 3125
        key = jax.random.key(seed)
        k1, k2, k3 = jax.random.split(key, 3)
        features = jax.random.normal(k1, (N_NODES, 16), dtype=jnp.float32)
        src = jax.random.randint(k2, (156250,), 0, N_NODES, dtype=jnp.int64)
        dst = jax.random.randint(k3, (156250,), 0, N_NODES, dtype=jnp.int64)
        return {'features': features, 'src': src, 'dst': dst}
    _L3_gnn_all = _L3_gnn_setup()
    _L3_gnn_in = {k: v for k, v in _L3_gnn_all.items() if k in ()}
    del _L3_gnn_all
    return {'x': x, 'src': src, 'dst': dst, 'edge_attr_16': edge_attr_16, 'edge_attr_8': edge_attr_8, 'edge_type_8': edge_type_8, 'node_vec1': node_vec1, 'L0_gnn_W1': _L0_gnn_in['W1'], 'L0_gnn_b1': _L0_gnn_in['b1'], 'L0_gnn_W2': _L0_gnn_in['W2'], 'L0_gnn_b2': _L0_gnn_in['b2'], 'L0_gnn_root': _L0_gnn_in['root'], 'L0_gnn_bias': _L0_gnn_in['bias'], 'L0_gnn_gamma': _L0_gnn_in['gamma'], 'L0_gnn_beta': _L0_gnn_in['beta'], 'L1_gnn_W_msg_tp': _L1_gnn_in['W_msg_tp'], 'L1_gnn_W_msg_lin': _L1_gnn_in['W_msg_lin'], 'L1_gnn_W_upd_tp': _L1_gnn_in['W_upd_tp'], 'L1_gnn_W_upd_lin': _L1_gnn_in['W_upd_lin'], 'L2_gnn_W1': _L2_gnn_in['W1'], 'L2_gnn_root1': _L2_gnn_in['root1'], 'L2_gnn_b1': _L2_gnn_in['b1'], 'L2_gnn_W2': _L2_gnn_in['W2'], 'L2_gnn_root2': _L2_gnn_in['root2'], 'L2_gnn_b2': _L2_gnn_in['b2']}

def reference(x, src, dst, edge_attr_16, edge_attr_8, edge_type_8, node_vec1, L0_gnn_W1, L0_gnn_b1, L0_gnn_W2, L0_gnn_b2, L0_gnn_root, L0_gnn_bias, L0_gnn_gamma, L0_gnn_beta, L1_gnn_W_msg_tp, L1_gnn_W_msg_lin, L1_gnn_W_upd_tp, L1_gnn_W_upd_lin, L2_gnn_W1, L2_gnn_root1, L2_gnn_b1, L2_gnn_W2, L2_gnn_root2, L2_gnn_b2):
    import jax
    import jax.numpy as jnp

    def _L0_gnn_ref(x, edge_index, edge_attr, W1, b1, W2, b2, root, bias, gamma, beta):
        import jax, jax.numpy as jnp
        import numpy as np
        N_NODES = 3125
        N_EDGES = 15625
        IND = 16
        OUT = 16
        EDGE_DIM = 16
        HID = IND * OUT
        BN_EPS = 1e-05
        n_nodes, ind = x.shape
        out_dim = root.shape[1]
        src, dst = (edge_index[0], edge_index[1])
        h = jax.nn.relu(edge_attr @ W1 + b1)
        w_edge = (h @ W2 + b2).reshape(-1, ind, out_dim)
        msgs = jnp.einsum('ei,eio->eo', x[src], w_edge)
        aggr = jax.ops.segment_sum(msgs, dst, num_segments=n_nodes)
        out = aggr + x @ root + bias
        mean = out.mean(axis=0)
        var = out.var(axis=0)
        out = (out - mean) / jnp.sqrt(var + BN_EPS) * gamma + beta
        return jax.nn.relu(out)

    def _L1_gnn_ref(node_features, edge_attr_e3nn, node_attr_scalar_raw, W_msg_tp, W_msg_lin, W_upd_tp, W_upd_lin, edge_index):
        import jax, jax.numpy as jnp
        import numpy as np
        N_NODES = 3125
        N_EDGES = 100000
        D_NODE = 16
        D_EDGE = 8
        D_HIDDEN = 16
        n_nodes = node_features.shape[0]
        row = edge_index[0]
        col = edge_index[1]
        norm_msg_tp = 1.0 / np.float32(np.sqrt(D_NODE * D_EDGE))
        norm_upd_tp = 1.0 / np.float32(np.sqrt(D_NODE * D_HIDDEN))
        norm_lin = 1.0 / np.float32(np.sqrt(D_HIDDEN))
        x_j = node_features[col]
        m = jnp.einsum('ei,ej,ijh->eh', x_j, edge_attr_e3nn, W_msg_tp) * norm_msg_tp
        m = jax.nn.silu(m)
        m = m @ W_msg_lin * norm_lin
        agg = jax.ops.segment_sum(m, row, num_segments=n_nodes)
        u = jnp.einsum('ni,nh,ihk->nk', node_features, agg, W_upd_tp) * norm_upd_tp
        u = jax.nn.silu(u)
        u = u @ W_upd_lin * norm_lin
        return node_features + u

    def _L2_gnn_ref(embed, W1, root1, b1, W2, root2, b2, edge_index, edge_type):
        import jax, jax.numpy as jnp
        import numpy as np
        NUM_ENTITIES = 3125
        NUM_RELATIONS = 8
        NUM_CLASSES = 16
        HIDDEN = 16
        NUM_EDGES = 100000

        def rgcn_conv(x, src, dst, edge_type, W, root, bias):
            num_nodes = x.shape[0]
            x_src = x[src]
            msg = jnp.zeros((src.shape[0], W.shape[2]), x.dtype)
            for r in range(NUM_RELATIONS):
                msg = msg + jnp.where((edge_type == r)[:, None], x_src @ W[r], jnp.zeros((), x.dtype))
            cnt = jnp.zeros((num_nodes, NUM_RELATIONS), x.dtype).at[dst, edge_type].add(1.0)
            norm = 1.0 / jnp.maximum(cnt[dst, edge_type], 1.0)
            agg = jax.ops.segment_sum(msg * norm[:, None], dst, num_segments=num_nodes)
            return agg + x @ root + bias
        src, dst = (edge_index[0], edge_index[1])
        h = rgcn_conv(embed, src, dst, edge_type, W1, root1, b1)
        h = jax.nn.relu(h)
        h = rgcn_conv(h, src, dst, edge_type, W2, root2, b2)
        return jax.nn.log_softmax(h, axis=1)

    def _L3_gnn_ref(features, src, dst):
        import jax, jax.numpy as jnp
        import numpy as np
        N_NODES = 3125
        n = features.shape[0]
        ones = jnp.ones(src.shape[0], dtype=features.dtype)
        out_deg = jnp.zeros(n, dtype=features.dtype).at[src].add(ones)
        out_deg = jnp.clip(out_deg, 1.0, None)
        in_deg = jnp.zeros(n, dtype=features.dtype).at[dst].add(ones)
        in_deg = jnp.clip(in_deg, 1.0, None)
        x = features * (out_deg ** (-0.5))[:, None]
        agg = jnp.zeros_like(features).at[dst].add(x[src])
        return agg * (in_deg ** (-0.5))[:, None]
    edge_index = jnp.stack([src, dst])
    h = jnp.maximum(_layernorm(x, axis=-1), 0.0)
    x = x + _L0_gnn_ref(h, edge_index, edge_attr_16, L0_gnn_W1, L0_gnn_b1, L0_gnn_W2, L0_gnn_b2, L0_gnn_root, L0_gnn_bias, L0_gnn_gamma, L0_gnn_beta)
    h = jnp.maximum(_layernorm(x, axis=-1), 0.0)
    x = x + _L1_gnn_ref(h, edge_attr_8, node_vec1, L1_gnn_W_msg_tp, L1_gnn_W_msg_lin, L1_gnn_W_upd_tp, L1_gnn_W_upd_lin, edge_index)
    h = jnp.maximum(_layernorm(x, axis=-1), 0.0)
    x = x + _L2_gnn_ref(h, L2_gnn_W1, L2_gnn_root1, L2_gnn_b1, L2_gnn_W2, L2_gnn_root2, L2_gnn_b2, edge_index, edge_type_8)
    h = jnp.maximum(_layernorm(x, axis=-1), 0.0)
    x = x + _L3_gnn_ref(h, src, dst)
    return x

_drawn_inputs = setup_inputs


def setup_inputs(seed=0):
    import zlib

    import numpy as np

    out = dict(_drawn_inputs(seed))
    spreads = {'L0_gnn_b1': (0.0, 0.1),
     'L0_gnn_b2': (0.0, 0.1),
     'L0_gnn_bias': (0.0, 0.8),
     'L0_gnn_gamma': (1.0, 0.2),
     'L0_gnn_beta': (0.0, 0.1),
     'L2_gnn_b1': (0.0, 0.293),
     'L2_gnn_b2': (0.0, 0.419)}
    factors = {'L0_gnn_root': 3.681}
    for name, (base, spread) in spreads.items():
        noise = np.random.default_rng([zlib.crc32(name.encode()), seed]).standard_normal(out[name].shape)
        drawn = base * np.exp(spread * noise) if base else spread * noise
        out[name] = jnp.asarray(drawn.astype(out[name].dtype))
    for name, factor in factors.items():
        out[name] = (out[name] * factor).astype(out[name].dtype)
    return out
```

```python
import numpy as np
import concourse.bass as bass
from concourse import mybir
from contextlib import ExitStack

ALU = mybir.AluOpType
ACT = mybir.ActivationFunctionType
AX = mybir.AxisListType
F32 = mybir.dt.float32
BF16 = mybir.dt.bfloat16
F16 = mybir.dt.float16
I32 = mybir.dt.int32

N_NODES, F, RELATIONS = 3125, 16, 8
EP, T = 125, 8
E = 100000
TILES = E // EP
CHUNKS = TILES // T
PAIRS = CHUNKS // 2
LO = 8
LOCAL = 32
NP = -(-N_NODES // LOCAL)
GROUPS = LOCAL // LO
SLOTS = NP * LOCAL
HI = SLOTS // LO
FULL = N_NODES // LOCAL
REST = N_NODES - FULL * LOCAL
HID = F * F
PART = 3 * F
W = LO * F
SRC, DST, SRC_KEY, SRC_HI, SRC_LO, DST_HI, DST_LO, DST_KEY, TYPE, FIELDS = range(10)
EPS = 1e-5


def build(nc, A, out):
    with ExitStack() as ctx:
        def sb(name, shape, dt=F32):
            return ctx.enter_context(nc.sbuf_tensor(name, shape, dt))

        def sem(name):
            return ctx.enter_context(nc.semaphore(name))

        events = {}

        def ev(name):
            if name not in events:
                events[name] = sem(name)
            return events[name]

        meta_d = nc.dram_tensor("edge_fields", [EP, CHUNKS, FIELDS * T], I32).ap()
        table0 = nc.dram_tensor("table_l0", [SLOTS, 2 * F], F32).ap()
        table1 = nc.dram_tensor("table_l1", [SLOTS, RELATIONS * F + RELATIONS], F32).ap()
        table2 = {"a": nc.dram_tensor("table_l2a", [SLOTS * RELATIONS, F], F32).ap(),
                  "b": nc.dram_tensor("table_l2b", [SLOTS * RELATIONS, F], F32).ap()}
        table3 = nc.dram_tensor("table_l3", [SLOTS, PART], BF16).ap()

        ident = sb("ident", [128, 128])
        ident16 = sb("ident16", [128, 128], BF16)
        count_hi = sb("count_hi", [EP, HI], F16)
        count_key = sb("count_key", [EP, LO * RELATIONS])
        valid = sb("valid", [NP, LOCAL])
        part_of_row = sb("part_of_row", [128, 3])
        ones = sb("ones", [NP, NP])

        w1 = sb("w1", [128, HID])
        w1_stack = sb("w1_stack", [128, HID], BF16)
        w1_hi = sb("w1_hi", [128, HID], BF16)
        w1_mid = sb("w1_mid", [128, HID], BF16)
        w1_rest = sb("w1_rest", [128, HID])
        w1_lo = sb("w1_lo", [128, HID])
        w2 = sb("w2", [128, 2, HID])
        b1 = sb("b1", [128, 2])
        SQUARE = ("b2", "root", "lin", "upd_lin", "root1", "root2")
        bd = {k: sb(f"bd_{k}", [128, W]) for k in SQUARE}
        bd["msg"] = sb("bd_msg", [128, LO, RELATIONS * F])
        bd["upd"] = sb("bd_upd", [128, LO, HID])
        bd["rel1"] = sb("bd_rel1", [128, LO, RELATIONS, F])
        bd["rel2"] = sb("bd_rel2", [128, LO, RELATIONS, F])
        rows16 = sb("rows16", [NP, 5, F])
        BIAS, GAMMA, BETA, B1, B2 = range(5)

        x = sb("x_nodes", [NP, LOCAL, F])
        h = sb("h", [NP, LOCAL, F])
        t0 = sb("t0", [NP, LOCAL, F])
        t1 = sb("t1", [NP, LOCAL, F])
        rooted = sb("rooted", [NP, LOCAL, F])
        stat = sb("stat", [NP, LOCAL])
        stat2 = sb("stat2", [NP, LOCAL])
        chan = sb("chan", [NP, F])
        chan2 = sb("chan2", [NP, F])
        hT = sb("hT", [W, GROUPS, NP])
        aggT = sb("aggT", [W, NP, GROUPS])
        sT = sb("sT", [W, NP, GROUPS])
        cntT = sb("cntT", [LO * RELATIONS, NP, GROUPS])
        cnt = sb("cnt", [NP, GROUPS * LO * RELATIONS])
        degT = sb("degT", [LO, NP, GROUPS])
        in_scale = sb("in_scale", [NP, LOCAL])
        out_scale = sb("out_scale", [NP, LOCAL])
        stage0 = sb("stage0", [NP, LOCAL, 2 * F])
        stage1 = sb("stage1", [NP, LOCAL, RELATIONS * F + RELATIONS])
        stage2 = stage1[:].rearrange("p l f -> p (l f)")[:, 0:LOCAL * RELATIONS * F]
        stage3 = sb("stage3", [NP, LOCAL, PART], BF16)
        gated = sb("gated", [NP, 2, 2, F, F])

        src = sb("src_rows", [EP, TILES], I32)
        dst = sb("dst_rows", [EP, TILES], I32)
        typ = sb("types", [EP, TILES], I32)
        work = sb("work", [EP, TILES], I32)
        work2 = sb("work2", [EP, TILES], I32)
        fields_all = sb("fields_all", [EP, CHUNKS, FIELDS, T], I32)
        fields = sb("fields", [EP, 2, FIELDS, T], I32)
        edge_norm = sb("edge_norm", [EP, TILES])
        ea = sb("ea", [EP, 2, T, F])
        ea_rest = sb("ea_rest", [EP, T, F])
        ea_rest2 = sb("ea_rest2", [EP, T, F])
        ea8 = sb("ea8", [EP, 2, T, RELATIONS])
        stack = sb("stack", [EP, 2, T, 8, F], BF16)
        eaT = sb("eaT", [128, T * EP], BF16)
        h1T = sb("h1T", [128, 2, T * EP])
        gathered0 = sb("gathered0", [EP, 2, T, 2 * F])
        gathered1 = sb("gathered1", [EP, 2, T, RELATIONS * F + RELATIONS])
        gathered2 = sb("gathered2", [EP, 2, T, F])
        gathered3 = sb("gathered3", [EP, 2, T, PART], BF16)
        product = sb("product", [EP, 2, 2, F, F])
        product1 = sb("product1", [EP, T, RELATIONS * F])
        msg = sb("msg", [EP, 2, T, F])
        raw = sb("raw", [EP, 2, T, F])
        rest = sb("rest", [EP, T, F])
        parts = sb("parts", [EP, 2, T, PART], BF16)
        is_lo = sb("is_lo", [EP, 2, T, LO])
        is_type = sb("is_type", [EP, T, RELATIONS])
        lo_bf = sb("lo_bf", [EP, 2, T, LO], BF16)
        mask = sb("mask", [EP, 2, T, LO, F], BF16)
        key_mask = sb("key_mask", [EP, 2, T, LO * RELATIONS], BF16)
        one_hot = sb("one_hot", [EP, 2, T, HI], BF16)
        stationary = sb("stationary", [EP, 2, 3, T, LO, F], BF16)
        zeros = sb("zeros", [EP, HI + W], BF16)
        zero_moving, zero_stationary = zeros[:, 0:HI], zeros[:, HI:]
        spare = sb("spare", [EP, 2])

        acc = ctx.enter_context(nc.psum_tensor("acc", [128, HI], F32))
        counts = ctx.enter_context(nc.psum_tensor("counts", [128, HI], F32))
        eaT_ps = ctx.enter_context(nc.psum_tensor("eaT_ps", [128, T, EP + 1], BF16))
        bank = [ctx.enter_context(nc.psum_tensor(f"bank{i}", [128, 512], F32)) for i in range(5)]

        PHASES = ("l0", "l1", "l2a", "l2b", "l3")
        S = {}
        for ph in PHASES:
            S[ph] = {
                "rows_in": [sem(f"{ph}_rows_in{s}") for s in range(2)],
                "step": sem(f"{ph}_vector_step"),
            }
        fields_in = [sem(f"fields_in{s}") for s in range(2)]
        masked = sem("mask_ready")
        operands = sem("operands_ready")
        added = sem("chunk_added")

        def before(ph):
            return CHUNKS * PHASES.index(ph)

        def fields_in_by(ph, pair):
            return 16 * (before(ph) // 2 + pair + 1)

        ea_in = [sem(f"ea_in{s}") for s in range(2)]
        ea8_in = [sem(f"ea8_in{s}") for s in range(2)]
        ea_copied = sem("ea_parts_copied")
        ea_split = sem("ea_rest_ready")
        ea_turned = sem("ea_transposed")
        eaT_ready = sem("eaT_ready")
        h1_made = sem("h1_made")
        h1_ready = sem("h1_relu_done")
        w_made = sem("edge_weights_made")
        w_used = sem("edge_weights_used")
        products_summed = sem("products_summed")
        silu_ready = sem("silu_ready")

        gathered = {"l0": gathered0, "l1": gathered1, "l2a": gathered2, "l2b": gathered2, "l3": gathered3}
        table = {"l0": table0, "l1": table1, "l2a": table2["a"], "l2b": table2["b"], "l3": table3}
        row_field = {"l0": SRC, "l1": DST, "l2a": SRC_KEY, "l2b": SRC_KEY, "l3": SRC}
        hi_field = {"l0": DST_HI, "l1": SRC_HI, "l2a": DST_HI, "l2b": DST_HI, "l3": DST_HI}
        lo_field = {"l0": DST_LO, "l1": SRC_LO, "l2a": DST_LO, "l2b": DST_LO, "l3": DST_LO}
        ORDER = {
            "l0": ("is_lo", "msg", "hi", "rest", "mid", "low", "fields_read"),
            "l1": ("is_lo", "raw", "typed", "weighed", "rows_read", "hi", "rest", "mid", "low"),
            "l2a": ("is_lo", "msg", "hi", "rest", "mid", "low"),
            "l3": ("is_lo", "rows_read"),
        }
        ORDER["l2b"] = ORDER["l2a"]
        FIELDS_READ = {"l0": "fields_read", "l1": "hi", "l2a": "low", "l2b": "low", "l3": "rows_read"}
        ROWS_READ = {"l0": "msg", "l1": "rows_read", "l2a": "msg", "l2b": "msg", "l3": None}

        def done(ph, name, chunk):
            return chunk * len(ORDER[ph]) + ORDER[ph].index(name) + 1

        def later(chunk, n):
            return not isinstance(chunk, int) or chunk >= n

        def all_chunks(eng, body, after_first=None):
            for s in range(2):
                body(s, 0, s)
            if after_first:
                after_first()
            with eng.Fori(1, PAIRS) as pair:
                for s in range(2):
                    body(2 * pair + s, pair, s)

        def pairs_of_ends(eng, body):
            for s in range(2):
                body(s, 0, s, False)
            with eng.Fori(1, PAIRS - 1) as pair:
                for s in range(2):
                    body(2 * pair + s, pair, s, False)
            for s in range(2):
                body(CHUNKS - 2 + s, PAIRS - 1, s, s == 1)

        as_nodes = [(slice(0, FULL), slice(0, LOCAL), slice(0, FULL * LOCAL)),
                    (slice(FULL, NP), slice(0, REST), slice(FULL * LOCAL, N_NODES))]

        block = ctx.enter_context(nc.Block())

        @block.sync
        def _(sp):
            sp.dma_start(src[:], A["src"].rearrange("(p t) -> p t", p=EP)).then_inc(ev("src_in"), 16)
            sp.dma_start(dst[:], A["dst"].rearrange("(p t) -> p t", p=EP)).then_inc(ev("dst_in"), 16)
            sp.dma_start(typ[:], A["edge_type_8"].rearrange("(p t) -> p t", p=EP)).then_inc(ev("type_in"), 16)
            sp.dma_start(valid[:], A["c_valid"]).then_inc(ev("consts_in"), 16)
            sp.dma_start(ident[:], A["c_ident"]).then_inc(ev("consts_in"), 16)
            sp.dma_start(count_hi[:], A["c_hi"]).then_inc(ev("consts_in"), 16)
            sp.dma_start(count_key[:], A["c_key"]).then_inc(ev("consts_in"), 16)
            sp.dma_start(part_of_row[:], A["c_part"]).then_inc(ev("consts_in"), 16)
            sp.wait_ge(ev("x_cleared"), 1)
            for p, l, n in as_nodes:
                sp.dma_start(x[p, l, :], A["x"][n].rearrange("(p l) f -> p l f", l=l.stop)).then_inc(ev("x_in"), 16)
            for k in range(8):
                sp.dma_start(w1[k * F:(k + 1) * F, :], A["L0_gnn_W1"]).then_inc(ev("w1_in"), 16)
            for a in range(2):
                sp.dma_start(b1[:, a:a + 1], A["L0_gnn_b1"][a * 128:(a + 1) * 128][:, None]).then_inc(ev("w1_in"), 16)
            sp.dma_start(w2[:], A["L0_gnn_W2"].rearrange("(a p) n -> p a n", a=2)).then_inc(ev("w2_in"), 16)
            for i, k in enumerate(("L0_gnn_bias", "L0_gnn_gamma", "L0_gnn_beta", "L2_gnn_b1", "L2_gnn_b2")):
                sp.dma_start(rows16[:, i, :], A[k][None, :].to_broadcast([NP, F])).then_inc(ev("rows16_in"), 16)
            sp.wait_ge(ev("diagonals_cleared"), len(bd))
            blocks = {"b2": A["L0_gnn_b2"].rearrange("(i o) -> i o", o=F), "root": A["L0_gnn_root"],
                      "lin": A["L1_gnn_W_msg_lin"], "upd_lin": A["L1_gnn_W_upd_lin"],
                      "root1": A["L2_gnn_root1"], "root2": A["L2_gnn_root2"]}
            for lo in range(LO):
                rows = slice(lo * F, (lo + 1) * F)
                for k in ("b2", "root"):
                    sp.dma_start(bd[k][rows, rows], blocks[k]).then_inc(ev("l0_diagonals_in"), 16)

            def later_weights():
                for lo in range(LO):
                    rows = slice(lo * F, (lo + 1) * F)
                    for k in ("lin", "upd_lin", "root1", "root2"):
                        sp.dma_start(bd[k][rows, rows], blocks[k]).then_inc(ev("diagonals_in"), 16)
                    sp.dma_start(bd["msg"][rows, lo, :],
                                 A["L1_gnn_W_msg_tp"].rearrange("i j h -> i (j h)")).then_inc(ev("diagonals_in"), 16)
                    sp.dma_start(bd["upd"][rows, lo, :].rearrange("h (i k) -> h i k", k=F),
                                 A["L1_gnn_W_upd_tp"].rearrange("i h k -> h i k")).then_inc(ev("diagonals_in"), 16)
                    for k, w in (("rel1", "L2_gnn_W1"), ("rel2", "L2_gnn_W2")):
                        sp.dma_start(bd[k][rows, lo, :, :], A[w].rearrange("r i o -> i r o")).then_inc(ev("diagonals_in"), 16)

            sp.wait_ge(ev("fields_made"), 1)
            sp.dma_start(meta_d.rearrange("p c (k t) -> p c k t", k=FIELDS), fields_all[:]).then_inc(ev("fields_stored"), 16)
            sp.wait_ge(ev("fields_stored"), 16)

            ea_d = A["edge_attr_16"].rearrange("(p c t) f -> p c (t f)", p=EP, t=T)
            ea8_d = A["edge_attr_8"].rearrange("(p c t) f -> p c (t f)", p=EP, t=T)

            def stream(ph):
                def body(chunk, pair, s):
                    if ph == "l0":
                        if later(chunk, 2):
                            sp.wait_ge(ea_split, 2 * (chunk - 2) + 1)
                        sp.dma_start(ea[:, s].rearrange("p t f -> p (t f)"),
                                     ea_d[:, bass.ds(chunk, 1), :].rearrange("p c n -> p (c n)")).then_inc(ea_in[s], 16)
                    if later(chunk, 2):
                        sp.wait_ge(S[ph]["step"], done(ph, FIELDS_READ[ph], chunk - 2))
                    sp.dma_start(fields[:, s].rearrange("p k t -> p (k t)"),
                                 meta_d[:, bass.ds(chunk, 1), :].rearrange("p c n -> p (c n)")).then_inc(fields_in[s], 16)
                    if ph == "l1":
                        sp.dma_start(ea8[:, s].rearrange("p t f -> p (t f)"),
                                     ea8_d[:, bass.ds(chunk, 1), :].rearrange("p c n -> p (c n)")).then_inc(ea8_in[s], 16)
                all_chunks(sp, body, later_weights if ph == "l0" else None)

            def store_table(ph, stage, where):
                sp.wait_ge(ev(f"{ph}_stage_ready"), 1)
                sp.dma_start(where, stage).then_inc(ev(f"{ph}_table_in"), 16)

            store_table("l0", stage0[:].rearrange("p l f -> p (l f)"), table0.rearrange("(p l) f -> p (l f)", p=NP))
            stream("l0")
            store_table("l1", stage1[:].rearrange("p l f -> p (l f)"), table1.rearrange("(p l) f -> p (l f)", p=NP))
            stream("l1")
            for k in ("a", "b"):
                store_table("l2" + k, stage2, table2[k].rearrange("(p l) f -> p (l f)", p=NP))
                stream("l2" + k)
            store_table("l3", stage3[:].rearrange("p l f -> p (l f)"), table3.rearrange("(p l) f -> p (l f)", p=NP))
            stream("l3")
            sp.wait_ge(ev("result_ready"), 1)
            for p, l, n in as_nodes:
                sp.dma_start(out[n].rearrange("(p l) f -> p l f", l=l.stop), t1[p, l, :]).then_inc(ev("stored"), 16)
            sp.wait_ge(ev("stored"), 16 * len(as_nodes))

        @block.gpsimd
        def _(pool):
            pool.memset(x[:], 0.0).then_inc(ev("x_cleared"), 1)
            for k in bd:
                pool.memset(bd[k][:], 0.0).then_inc(ev("diagonals_cleared"), 1)
            pool.memset(ones[:], 1.0).then_inc(ev("ones_set"), 1)

            def gathers(ph):
                pool.wait_ge(ev(f"{ph}_table_in"), 16)

                def body(chunk, pair, s):
                    pool.wait_ge(fields_in[s], fields_in_by(ph, pair))
                    if later(chunk, 2):
                        if ROWS_READ[ph]:
                            pool.wait_ge(S[ph]["step"], done(ph, ROWS_READ[ph], chunk - 2))
                        else:
                            pool.wait_ge(operands, before(ph) + chunk - 1)
                    pool.sem_inc(ev("chunks_begun"), 1)
                    for t in range(T):
                        pool.indirect_dma_start(
                            out=gathered[ph][:, s, t, :], in_=table[ph], out_offset=None,
                            in_offset=bass.IndirectOffsetOnAxis(ap=fields[:, s, row_field[ph], t:t + 1], axis=0),
                        ).then_inc(S[ph]["rows_in"][s], 16)
                all_chunks(pool, body)

            for ph in PHASES:
                gathers(ph)

        @block.tensor
        def _(pe):
            def add_chunk(ph, chunk, s, tiles=range(T), first=False, last=False):
                for t in tiles:
                    for k in range(3):
                        mm = pe.matmul(acc[:, :], stationary[:, s, k, t, :, :].rearrange("p a b -> p (a b)"),
                                       one_hot[:, s, t, :], start=first and t == 0 and k == 0,
                                       stop=last and t == T - 1 and k == 2)
                    if ph == "l0":
                        mm = pe.matmul(counts[0:LO * RELATIONS, :], key_mask[:, s, t, :], one_hot[:, s, t, :],
                                       start=first and t == 0, stop=last and t == T - 1)
                    if ph == "l1":
                        mm = pe.matmul(counts[0:LO, :], lo_bf[:, s, t, :], one_hot[:, s, t, :],
                                       start=first and t == 0, stop=last and t == T - 1)
                if T - 1 in tiles:
                    mm.then_inc(added, 1)

            def turn_h(name):
                pe.wait_ge(ev(f"{name}_h"), 1)
                for c in range(GROUPS):
                    mm = pe.transpose(bank[0][:, c * NP:(c + 1) * NP], h[:, c * LO:(c + 1) * LO, :].rearrange("p l f -> p (l f)"),
                                      ident[0:NP, 0:NP])
                mm.then_inc(ev(f"{name}_turned"), 1)
                pe.wait_ge(ev(f"{name}_hT"), 1)

            def times(name, into, w):
                for c in range(GROUPS):
                    mm = pe.matmul(into[0:NP, c * W:(c + 1) * W], hT[:, c, :], bd[w][:, :], start=True, stop=True)
                mm.then_inc(ev(name), 1)

            def wide(name, w):
                flat = bd[w][:].rearrange("p a b c -> p (a b c)") if len(bd[w].shape) == 4 else bd[w][:].rearrange("p a b -> p (a b)")
                for i in range(2 * GROUPS):
                    if i >= 2:
                        pe.wait_ge(ev(f"{name}_wide_read"), i - 1)
                    pe.matmul(bank[2 + i % 2][0:NP, :], hT[:, i // 2, :], flat[:, (i % 2) * 512:(i % 2 + 1) * 512],
                              start=True, stop=True).then_inc(ev(f"{name}_wide"), 1)

            def turn_back(ph, source=None, ready=None):
                pe.wait_ge(ev(ready or f"{ph}_aggT"), 1)
                for c in range(GROUPS):
                    mm = pe.transpose(bank[1][0:NP, c * W:(c + 1) * W], (source or aggT)[:, :, c], ident[:, :])
                mm.then_inc(ev(f"{ph}_agg"), 1)

            pe.wait_ge(ev("consts_in"), 80)
            turn_h("l0")
            pe.wait_ge(ev("l0_diagonals_in"), 16 * 2 * LO)
            times("l0_b2_made", bank[1], "b2")
            times("l0_root_made", bank[2], "root")

            pe.wait_ge(ev("w1_stacked"), 1)
            pe.wait_ge(ev("w2_in"), 16)
            pe.wait_ge(ev("ident16_made"), 1)
            pe.wait_ge(ev("l0_rooted"), 1)
            pe.wait_ge(ev("zeros_set"), 1)
            pe.matmul(acc[:, :], zero_stationary, zero_moving, start=True, stop=False)
            pe.matmul(counts[0:LO * RELATIONS, :], zero_stationary[:, 0:LO * RELATIONS], zero_moving, start=True, stop=False)

            def turn_ea(chunk, s):
                pe.wait_ge(ea_copied, 3 * (chunk + 1))
                if later(chunk, 1):
                    pe.wait_ge(eaT_ready, chunk)
                for t in range(T):
                    mm = pe.transpose(eaT_ps[:, t, 0:EP],
                                      stack[:, s, t, :, :].rearrange("p a b -> p (a b)"), ident16[0:EP, 0:EP])
                mm.then_inc(ea_turned, 1)

            def hidden(chunk, g):
                if g >= 2 or later(chunk, 1):
                    pe.wait_ge(h1_ready, 4 * chunk + g - 1)
                if g == 0:
                    pe.wait_ge(eaT_ready, chunk + 1)
                half, side = g % 2, g // 2
                pe.matmul(bank[g % 2][:, 0:4 * EP], w1_stack[:, half * 128:(half + 1) * 128],
                          eaT[:, side * 4 * EP:(side + 1) * 4 * EP], start=True, stop=True).then_inc(h1_made, 1)

            def edge_weights(chunk):
                pe.wait_ge(h1_ready, 4 * chunk + 4)
                for q in range(T // 2):
                    if q >= 2 or later(chunk, 1):
                        pe.wait_ge(w_used, 4 * chunk + q - 1)
                    for j in range(2):
                        t = 2 * q + j
                        for half in range(2):
                            mm = pe.matmul(bank[2 + q % 2][0:EP, j * HID:(j + 1) * HID],
                                           h1T[:, half, t * EP:(t + 1) * EP], w2[:, half, :],
                                           start=half == 0, stop=half == 1)
                    mm.then_inc(w_made, 1)

            def l0(chunk, pair, s, last):
                def quarter(q):
                    if later(chunk, 2):
                        add_chunk("l0", chunk - 2, s, range(2 * q, 2 * q + 2))

                if later(chunk, 2):
                    pe.wait_ge(operands, before("l0") + chunk - 1)
                quarter(0)
                turn_ea(chunk, s)
                quarter(1)
                hidden(chunk, 0)
                hidden(chunk, 1)
                quarter(2)
                hidden(chunk, 2)
                hidden(chunk, 3)
                quarter(3)
                edge_weights(chunk)
                if last:
                    for n in (CHUNKS - 2, CHUNKS - 1):
                        pe.wait_ge(operands, before("l0") + n + 1)
                        add_chunk("l0", n, n % 2, last=n == CHUNKS - 1)

            pairs_of_ends(pe, l0)
            turn_back("l0")
            pe.wait_ge(ev("ones_set"), 1)
            for k in ("mean", "var"):
                pe.wait_ge(ev(f"bn_{k}_in"), 1)
                pe.matmul(bank[0][0:NP, :], ones[:, :], t0[:].rearrange("p l f -> p (l f)"),
                          start=True, stop=True).then_inc(ev(f"bn_{k}_sum"), 1)
            pe.wait_ge(ev("cntT_ready"), 1)
            KW = LO * RELATIONS
            for c in range(GROUPS):
                mm = pe.transpose(bank[4][0:NP, c * KW:(c + 1) * KW], cntT[:, :, c], ident[0:KW, 0:KW])
            mm.then_inc(ev("cnt_turned"), 1)
            turn_h("l1")
            pe.wait_ge(ev("diagonals_in"), 16 * 8 * LO)
            wide("l1", "msg")

            def sum_only(ph):
                def body(chunk, pair, s):
                    pe.wait_ge(operands, before(ph) + chunk + 1)
                    add_chunk(ph, chunk, s, first=isinstance(chunk, int) and chunk == 0)
                all_chunks(pe, body)
                pe.wait_ge(ev("zeros_set"), 1)
                mm = pe.matmul(acc[:, :], zero_stationary, zero_moving, start=False, stop=True)
                if ph == "l1":
                    mm = pe.matmul(counts[0:LO, :], zero_stationary[:, 0:LO], zero_moving, start=False, stop=True)
                mm.then_inc(ev(f"{ph}_summed"), 1)

            sum_only("l1")
            pe.wait_ge(ev("l1_sT"), 1)
            pe.matmul(bank[0][:, 0:HI], bd["lin"][:, :], sT[:].rearrange("p a b -> p (a b)"),
                      start=True, stop=True).then_inc(ev("l1_lin"), 1)
            pe.wait_ge(ev("degT_ready"), 1)
            for c in range(GROUPS):
                mm = pe.transpose(bank[4][0:NP, c * LO:(c + 1) * LO], degT[:, :, c], ident[0:LO, 0:LO])
            mm.then_inc(ev("deg_turned"), 1)
            pe.wait_ge(ev("l1_aggT"), 1)
            for i in range(4 * GROUPS):
                if i >= 2:
                    pe.wait_ge(ev("upd_read"), i - 1)
                c, q = divmod(i, 4)
                pe.matmul(bank[2 + i % 2][0:NP, :], aggT[:, :, c],
                          bd["upd"][:, 2 * q:2 * q + 2, :].rearrange("p a b -> p (a b)"),
                          start=True, stop=True).then_inc(ev("upd_made"), 1)
            turn_h("u")
            times("u_lin", bank[1], "upd_lin")
            for k in ("1", "2"):
                ph = "l2" + "ab"[int(k) - 1]
                turn_h(ph)
                times(f"{ph}_root_made", bank[1], "root" + k)
                wide(ph, "rel" + k)
                sum_only(ph)
                turn_back(ph)
            sum_only("l3")
            turn_back("l3")

        @block.scalar
        def _(act):
            def masks(ph, chunk, s):
                act.wait_ge(S[ph]["step"], done(ph, "is_lo", chunk))
                if later(chunk, 2):
                    act.wait_ge(operands, before(ph) + chunk - 1)
                if ph == "l1":
                    if later(chunk, 2):
                        act.wait_ge(added, before(ph) + chunk - 1)
                    act.copy(lo_bf[:, s], is_lo[:, s])
                act.copy(mask[:, s].rearrange("p t a f -> p (t a) f"),
                         is_lo[:, s].rearrange("p t a -> p (t a)")[:, :, None].to_broadcast([EP, T * LO, F])
                         ).then_inc(masked, 1)

            def turned(name):
                act.wait_ge(ev(f"{name}_turned"), 1)
                act.copy(hT[:].rearrange("p a b -> p (a b)"), bank[0][:, 0:HI]).then_inc(ev(f"{name}_hT"), 1)

            def root(name):
                act.wait_ge(ev(name), 1)

            def standard(name):
                act.wait_ge(ev(f"{name}_var"), 1)
                act.activation(stat2[:], stat[:], ACT.Sqrt).then_inc(ev(f"{name}_std"), 1)

            def relation_rows(name, stage):
                for i in range(2 * GROUPS):
                    act.wait_ge(ev(f"{name}_wide"), i + 1)
                    source = bank[2 + i % 2][0:NP, :]
                    if name == "l1":
                        ins = act.copy(stage[:, 4 * i:4 * i + 4, 0:RELATIONS * F],
                                       source.rearrange("p (a b) -> p a b", a=4))
                    else:
                        ins = act.copy(stage[:, 512 * i:512 * (i + 1)], source)
                    ins.then_inc(ev(f"{name}_wide_read"), 1)

            standard("ln0")
            turned("l0")
            act.wait_ge(ev("w1_in"), 160)

            def spread(chunk, pair, s, k):
                if k == 0:
                    act.wait_ge(ea_in[s], 16 * (pair + 1))
                    if later(chunk, 2):
                        act.wait_ge(ea_turned, chunk - 1)
                else:
                    act.wait_ge(ea_split, 2 * chunk + k)
                source = (ea[:, s], ea_rest[:], ea_rest2[:])[k]
                n = 3 if k < 2 else 2
                act.copy(stack[:, s, :, 3 * k:3 * k + n, :],
                         source[:, :, None, :].to_broadcast([EP, T, n, F])).then_inc(ea_copied, 1)

            for k in range(3):
                spread(0, 0, 0, k)

            def l0(chunk, pair, s, last):
                act.wait_ge(ea_turned, chunk + 1)
                act.copy(eaT[:].rearrange("p (t e) -> p t e", t=T), eaT_ps[:, :, 0:EP]).then_inc(eaT_ready, 1)
                for g in range(4):
                    act.wait_ge(h1_made, 4 * chunk + g + 1)
                    half, side = g % 2, g // 2
                    act.activation(h1T[:, half, side * 4 * EP:(side + 1) * 4 * EP], bank[g % 2][:, 0:4 * EP], ACT.Relu,
                                   bias=b1[:, half:half + 1]).then_inc(h1_ready, 1)
                if not last:
                    spread(chunk + 1, pair + s, 1 - s, 0)
                masks("l0", chunk, s)
                if not last:
                    spread(chunk + 1, pair + s, 1 - s, 1)
                    spread(chunk + 1, pair + s, 1 - s, 2)

            pairs_of_ends(act, l0)
            act.wait_ge(ev("bn_var"), 1)
            act.activation(chan2[:], chan[:], ACT.Sqrt).then_inc(ev("bn_std"), 1)
            standard("ln1")
            standard("in_degree")
            turned("l1")
            relation_rows("l1", stage1)

            def l1(chunk, pair, s):
                masks("l1", chunk, s)
                act.wait_ge(S["l1"]["step"], done("l1", "raw", chunk))
                act.activation(msg[:, s], raw[:, s], ACT.Silu,
                               scale=float(1.0 / np.float32(np.sqrt(F * RELATIONS)))).then_inc(silu_ready, 1)

            act.wait_ge(ev("spare_set"), 1)
            act.activation(spare[:, 1:2], spare[:, 0:1], ACT.Silu).then_inc(ev("silu_loaded"), 1)
            all_chunks(act, l1)
            act.wait_ge(ev("l1_lin"), 1)
            act.mul(aggT[:].rearrange("p a b -> p (a b)"), bank[0][:, 0:HI],
                    float(1.0 / np.float32(np.sqrt(F)))).then_inc(ev("l1_aggT"), 1)
            act.wait_ge(ev("u_raw"), 1)
            act.activation(h[:], t0[:], ACT.Silu, scale=float(1.0 / np.float32(np.sqrt(F * F)))).then_inc(ev("u_h"), 1)
            turned("u")
            standard("ln2")
            standard("out_degree")

            for ph in ("l2a", "l2b"):
                turned(ph)
                relation_rows(ph, stage2)
                all_chunks(act, lambda chunk, pair, s: masks(ph, chunk, s))
            act.wait_ge(ev("shifted"), 1)
            act.activation(t1[:], t0[:], ACT.Exp).then_inc(ev("exp_done"), 1)
            act.wait_ge(ev("exp_sum"), 1)
            act.activation(stat2[:], stat[:], ACT.Ln).then_inc(ev("log_done"), 1)
            standard("ln3")
            all_chunks(act, lambda chunk, pair, s: masks("l3", chunk, s))

        @block.vector
        def _(dve):
            chained = sem("vector_chain")
            count = [0]

            def link(ins, event=None):
                if event:
                    ins.then_inc(ev(event), 1)
                    dve.wait_ge(ev(event), 1)
                    return
                count[0] += 1
                ins.then_inc(chained, 1)
                dve.wait_ge(chained, count[0])

            def over(v, n=F):
                return v[:, :, None].to_broadcast([NP, LOCAL, n])

            def row(i):
                return rows16[:, i, :][:, None, :].to_broadcast([NP, LOCAL, F])

            def layernorm(name, scale=None, signal=None):
                link(dve.tensor_reduce(stat[:], x[:], AX.X, ALU.add))
                link(dve.tensor_scalar(stat[:], stat[:], 1.0 / F, None, ALU.mult))
                link(dve.tensor_tensor(t0[:], x[:], over(stat), ALU.subtract))
                link(dve.tensor_tensor(t1[:], t0[:], t0[:], ALU.mult))
                link(dve.tensor_reduce(stat2[:], t1[:], AX.X, ALU.add))
                link(dve.tensor_scalar(stat[:], stat2[:], 1.0 / F, EPS, ALU.mult, ALU.add), f"{name}_var")
                dve.wait_ge(ev(f"{name}_std"), 1)
                link(dve.reciprocal(stat[:], stat2[:]))
                link(dve.tensor_tensor(t1[:], t0[:], over(stat), ALU.mult))
                link(dve.tensor_scalar(h[:], t1[:], 0.0, None, ALU.max), signal)

            def inverse_root(name, into):
                link(dve.tensor_scalar(stat[:], stat[:], 1.0, None, ALU.max), f"{name}_var")
                dve.wait_ge(ev(f"{name}_std"), 1)
                link(dve.reciprocal(into[:], stat2[:]))

            def flat(t):
                return t[:].rearrange("p l f -> p (l f)")

            dve.wait_ge(ev("src_in"), 16)
            dve.wait_ge(ev("dst_in"), 16)
            dve.wait_ge(ev("type_in"), 16)

            def field(k):
                return fields_all[:, :, k, :]

            def by_chunk(v):
                return v[:].rearrange("p (c t) -> p c t", t=T)

            dve.tensor_copy(field(SRC), by_chunk(src))
            dve.tensor_copy(field(DST), by_chunk(dst))
            dve.tensor_copy(field(TYPE).bitcast(F32), by_chunk(typ))
            for v, hi, lo in ((src, SRC_HI, SRC_LO), (dst, DST_HI, DST_LO)):
                link(dve.tensor_scalar(work[:], v[:], 3, None, ALU.logical_shift_right))
                dve.tensor_copy(field(hi).bitcast(F32), by_chunk(work))
                link(dve.tensor_scalar(work2[:], v[:], LO - 1, None, ALU.bitwise_and))
                dve.tensor_copy(field(lo).bitcast(F32), by_chunk(work2))
            link(dve.tensor_scalar(work[:], work2[:], 3, None, ALU.logical_shift_left))
            link(dve.tensor_tensor(work2[:], work[:], typ[:], ALU.bitwise_or))
            dve.tensor_copy(field(DST_KEY).bitcast(F32), by_chunk(work2))
            link(dve.tensor_scalar(work[:], src[:], 3, None, ALU.logical_shift_left))
            link(dve.tensor_tensor(field(SRC_KEY), by_chunk(work), by_chunk(typ), ALU.bitwise_or), "fields_made")

            dve.memset(zeros[:], 0.0).then_inc(ev("zeros_set"), 1)
            dve.memset(spare[:], 0.0).then_inc(ev("spare_set"), 1)
            dve.wait_ge(ev("consts_in"), 80)
            link(dve.tensor_copy(ident16[:], ident[:]), "ident16_made")
            dve.wait_ge(ev("x_in"), 32)
            layernorm("ln0", signal="l0_h")
            dve.wait_ge(ev("w1_in"), 160)
            link(dve.tensor_copy(w1_hi[:], w1[:]))
            link(dve.tensor_tensor(w1_rest[:], w1[:], w1_hi[:], ALU.subtract))
            link(dve.tensor_copy(w1_mid[:], w1_rest[:]))
            link(dve.tensor_tensor(w1_lo[:], w1_rest[:], w1_mid[:], ALU.subtract))
            link(dve.tensor_scalar(w1_rest[:], w1_hi[:], part_of_row[:, 0:1], None, ALU.mult))
            link(dve.scalar_tensor_tensor(w1[:], w1_mid[:], part_of_row[:, 1:2], w1_rest[:], ALU.mult, ALU.add))
            link(dve.scalar_tensor_tensor(w1_stack[:], w1_lo[:], part_of_row[:, 2:3], w1[:], ALU.mult, ALU.add), "w1_stacked")
            dve.tensor_copy(stage0[:, :, 0:F], h[:])
            dve.wait_ge(ev("l0_b2_made"), 1)
            link(dve.tensor_copy(stage0[:, :, F:2 * F], bank[1][0:NP, :].rearrange("p (l f) -> p l f", f=F)), "l0_stage_ready")
            dve.wait_ge(ev("l0_root_made"), 1)
            link(dve.tensor_copy(flat(rooted), bank[2][0:NP, :]), "l0_rooted")

            def scalar_field(s, k, t):
                return fields[:, s, k, t:t + 1].bitcast(F32)

            def matches(into, counted, s, k, n):
                return dve.tensor_tensor(into, counted[:, None, 0:n].to_broadcast([EP, T, n]),
                                         fields[:, s, k, :].bitcast(F32)[:, :, None].to_broadcast([EP, T, n]), ALU.is_equal)

            count_lo = count_key[:, 0:LO]

            class Steps:

                def __init__(self, ph, chunk, s):
                    self.ph, self.chunk, self.s = ph, chunk, s

                def mark(self, ins):
                    ins.then_inc(S[self.ph]["step"], 1)

                def wait(self, name):
                    dve.wait_ge(S[self.ph]["step"], done(self.ph, name, self.chunk))

            def one_hots(ph, s, tiles):
                for t in tiles:
                    dve.tensor_scalar(one_hot[:, s, t, :], count_hi[:, :], scalar_field(s, hi_field[ph], t), None, ALU.is_equal)

            def slot_free(ph, chunk):
                if later(chunk, 2):
                    dve.wait_ge(added, before(ph) + chunk - 1)

            def split(st, source, between):
                s = st.s
                st.mark(dve.tensor_copy(parts[:, s, :, 0:F], source))
                between(0)
                st.wait("hi")
                st.mark(dve.tensor_tensor(rest[:], source, parts[:, s, :, 0:F], ALU.subtract))
                between(1)
                st.wait("rest")
                st.mark(dve.tensor_copy(parts[:, s, :, F:2 * F], rest[:]))
                between(2)
                st.wait("mid")
                st.mark(dve.tensor_tensor(parts[:, s, :, 2 * F:3 * F], rest[:], parts[:, s, :, F:2 * F], ALU.subtract))
                between(3)

            def to_stationary(ph, chunk, s, source, ready=None):
                dve.wait_ge(masked, before(ph) + chunk + 1)
                for k in range(3):
                    if k == 2 and ready:
                        ready()
                    ins = dve.tensor_tensor(stationary[:, s, k], mask[:, s],
                                            source[:, s, :, k * F:(k + 1) * F][:, :, None, :].to_broadcast([EP, T, LO, F]), ALU.mult)
                ins.then_inc(operands, 1)

            def split_ea(chunk, s, k):
                source, into = ((ea[:, s], ea_rest), (ea_rest[:], ea_rest2))[k]
                dve.wait_ge(ea_copied, 3 * chunk + k + 1)
                dve.tensor_tensor(into[:], source, stack[:, s, :, 3 * k, :], ALU.subtract).then_inc(ea_split, 1)

            split_ea(0, 0, 0)
            split_ea(0, 0, 1)

            def l0(chunk, pair, s, last):
                st = Steps("l0", chunk, s)
                dve.wait_ge(fields_in[s], fields_in_by("l0", pair))
                st.mark(matches(is_lo[:, s], count_lo, s, DST_LO, LO))
                dve.wait_ge(S["l0"]["rows_in"][s], 16 * T * (pair + 1))

                def multiply(q):
                    dve.wait_ge(w_made, 4 * chunk + q + 1)
                    if q >= 2 or later(chunk, 1):
                        dve.wait_ge(products_summed, 4 * chunk + q - 1)
                    dve.tensor_tensor(product[:, q % 2], bank[2 + q % 2][0:EP, :].rearrange("p (t i o) -> p t i o", t=2, i=F),
                                      gathered0[:, s, 2 * q:2 * q + 2, 0:F][:, :, :, None].to_broadcast([EP, 2, F, F]),
                                      ALU.mult).then_inc(w_used, 1)

                def add_up(q):
                    dve.wait_ge(w_used, 4 * chunk + q + 1)
                    dve.tensor_reduce(raw[:, s, 2 * q:2 * q + 2, :], product[:, q % 2].rearrange("p t i o -> p t o i"),
                                      AX.X, ALU.add).then_inc(products_summed, 1)

                multiply(0)
                for q in range(1, T // 2):
                    multiply(q)
                    add_up(q - 1)
                    if q < 3 and not last:
                        split_ea(chunk + 1, 1 - s, q - 1)
                slot_free("l0", chunk)
                add_up(T // 2 - 1)
                one_hots("l0", s, (0,))
                dve.wait_ge(products_summed, 4 * chunk + 4)
                st.mark(dve.tensor_tensor(msg[:, s], raw[:, s], gathered0[:, s, :, F:2 * F], ALU.add))
                one_hots("l0", s, (1,))
                st.wait("msg")
                split(st, msg[:, s], lambda k: one_hots("l0", s, ((2, 3), (4, 5), (6,), (7,))[k]))
                st.mark(matches(key_mask[:, s], count_key, s, DST_KEY, LO * RELATIONS))
                to_stationary("l0", chunk, s, parts, lambda: st.wait("low"))

            pairs_of_ends(dve, l0)
            dve.wait_ge(added, before("l0") + CHUNKS)
            link(dve.tensor_copy(aggT[:].rearrange("p a b -> p (a b)"), acc[:, :]), "l0_aggT")
            link(dve.tensor_copy(cntT[:].rearrange("p a b -> p (a b)"), counts[0:LO * RELATIONS, :]), "cntT_ready")
            dve.wait_ge(ev("rows16_in"), 80)
            dve.wait_ge(ev("l0_agg"), 1)
            link(dve.tensor_tensor(flat(t1), bank[1][0:NP, :], flat(rooted), ALU.add))
            link(dve.tensor_tensor(rooted[:], t1[:], row(BIAS), ALU.add))
            link(dve.tensor_tensor(t0[:], rooted[:], over(valid), ALU.mult), "bn_mean_in")
            dve.wait_ge(ev("bn_mean_sum"), 1)
            by_channel = bank[0][0:NP, :].rearrange("p (l f) -> p f l", f=F)

            def channels(v):
                return v[:, None, :].to_broadcast([NP, LOCAL, F])

            link(dve.tensor_reduce(chan[:], by_channel, AX.X, ALU.add))
            link(dve.tensor_scalar(chan[:], chan[:], 1.0 / N_NODES, None, ALU.mult))
            link(dve.tensor_tensor(t1[:], rooted[:], channels(chan), ALU.subtract))
            link(dve.tensor_tensor(rooted[:], t1[:], over(valid), ALU.mult))
            link(dve.tensor_tensor(t0[:], rooted[:], rooted[:], ALU.mult), "bn_var_in")
            dve.wait_ge(ev("bn_var_sum"), 1)
            link(dve.tensor_reduce(chan2[:], by_channel, AX.X, ALU.add))
            link(dve.tensor_scalar(chan[:], chan2[:], 1.0 / N_NODES, EPS, ALU.mult, ALU.add), "bn_var")
            dve.wait_ge(ev("bn_std"), 1)
            link(dve.reciprocal(chan[:], chan2[:]))
            link(dve.tensor_tensor(t0[:], t1[:], channels(chan), ALU.mult))
            link(dve.tensor_tensor(t1[:], t0[:], row(GAMMA), ALU.mult))
            link(dve.tensor_tensor(t0[:], t1[:], row(BETA), ALU.add))
            link(dve.tensor_scalar(t1[:], t0[:], 0.0, None, ALU.max))
            link(dve.tensor_tensor(x[:], x[:], t1[:], ALU.add))
            layernorm("ln1", signal="l1_h")
            dve.wait_ge(ev("cnt_turned"), 1)
            link(dve.tensor_copy(cnt[:], bank[4][0:NP, 0:GROUPS * LO * RELATIONS]))
            by_relation = cnt[:].rearrange("p (l r) -> p l r", r=RELATIONS)
            link(dve.tensor_reduce(stat[:], by_relation, AX.X, ALU.add))
            inverse_root("in_degree", in_scale)
            link(dve.tensor_scalar(cnt[:], cnt[:], 1.0, None, ALU.max))
            link(dve.reciprocal(stage1[:, :, RELATIONS * F:], by_relation))
            dve.wait_ge(ev("l1_wide_read"), 2 * GROUPS)
            link(dve.tensor_copy(stat[:, 0:1], stage1[:, 0, 0:1]), "l1_stage_ready")

            def l1(chunk, pair, s):
                st = Steps("l1", chunk, s)
                dve.wait_ge(fields_in[s], fields_in_by("l1", pair))
                slot_free("l1", chunk)
                st.mark(matches(is_lo[:, s], count_lo, s, SRC_LO, LO))
                dve.wait_ge(S["l1"]["rows_in"][s], 16 * T * (pair + 1))
                dve.wait_ge(ea8_in[s], 16 * (pair + 1))
                dve.tensor_tensor(product1[:].rearrange("p t (j h) -> p t j h", h=F),
                                  gathered1[:, s, :, 0:RELATIONS * F].rearrange("p t (j h) -> p t j h", h=F),
                                  ea8[:, s][:, :, :, None].to_broadcast([EP, T, RELATIONS, F]), ALU.mult
                                  ).then_inc(ev("l1_products"), 1)
                one_hots("l1", s, (0, 1))
                dve.wait_ge(ev("l1_products"), chunk + 1)
                st.mark(dve.tensor_reduce(raw[:, s], product1[:].rearrange("p t (j h) -> p t h j", h=F), AX.X, ALU.add))
                st.mark(matches(is_type[:], count_lo, s, TYPE, RELATIONS))
                one_hots("l1", s, (2,))
                st.wait("typed")
                st.mark(dve.tensor_tensor(is_type[:], is_type[:], gathered1[:, s, :, RELATIONS * F:], ALU.mult))
                one_hots("l1", s, (3,))
                st.wait("weighed")
                st.mark(dve.tensor_reduce(edge_norm[:, bass.ds(chunk * T, T)], is_type[:], AX.X, ALU.add))
                one_hots("l1", s, (4, 5, 6, 7))
                dve.wait_ge(silu_ready, chunk + 1)
                split(st, msg[:, s], lambda k: None)
                to_stationary("l1", chunk, s, parts, lambda: st.wait("low"))

            all_chunks(dve, l1)
            dve.wait_ge(ev("l1_summed"), 1)
            link(dve.tensor_copy(sT[:].rearrange("p a b -> p (a b)"), acc[:, :]), "l1_sT")
            link(dve.tensor_copy(degT[:].rearrange("p a b -> p (a b)"), counts[0:LO, :]), "degT_ready")
            for i in range(4 * GROUPS):
                dve.wait_ge(ev("upd_made"), i + 1)
                dve.tensor_tensor(gated[:, i % 2], bank[2 + i % 2][0:NP, :].rearrange("p (l i k) -> p l i k", l=2, i=F),
                                  h[:, 2 * i:2 * i + 2, :][:, :, :, None].to_broadcast([NP, 2, F, F]), ALU.mult
                                  ).then_inc(ev("upd_read"), 1)
                dve.wait_ge(ev("upd_read"), i + 1)
                ins = dve.tensor_reduce(t0[:, 2 * i:2 * i + 2, :], gated[:, i % 2].rearrange("p l i k -> p l k i"), AX.X, ALU.add)
                if i == 4 * GROUPS - 1:
                    link(ins)
                    link(dve.tensor_tensor(rooted[:], x[:], h[:], ALU.add), "u_raw")
            dve.wait_ge(ev("u_lin"), 1)
            link(dve.tensor_scalar(flat(t1), bank[1][0:NP, :], float(1.0 / np.float32(np.sqrt(F))), None, ALU.mult))
            link(dve.tensor_tensor(x[:], rooted[:], t1[:], ALU.add))
            layernorm("ln2", signal="l2a_h")
            dve.wait_ge(ev("deg_turned"), 1)
            link(dve.tensor_copy(stat[:], bank[4][0:NP, 0:LOCAL]))
            inverse_root("out_degree", out_scale)

            for k, bias in (("a", B1), ("b", B2)):
                ph = "l2" + k
                dve.wait_ge(ev(f"{ph}_root_made"), 1)
                link(dve.tensor_tensor(rooted[:], bank[1][0:NP, :].rearrange("p (l f) -> p l f", f=F), row(bias), ALU.add))
                dve.wait_ge(ev(f"{ph}_wide_read"), 2 * GROUPS)
                link(dve.tensor_copy(stat[:, 0:1], stage2[:, 0:1]), f"{ph}_stage_ready")

                def l2(chunk, pair, s):
                    st = Steps(ph, chunk, s)
                    dve.wait_ge(fields_in[s], fields_in_by(ph, pair))
                    slot_free(ph, chunk)
                    st.mark(matches(is_lo[:, s], count_lo, s, DST_LO, LO))
                    one_hots(ph, s, (0,))
                    dve.wait_ge(S[ph]["rows_in"][s], 16 * T * (pair + 1))
                    st.mark(dve.tensor_tensor(msg[:, s], gathered2[:, s],
                                              edge_norm[:, bass.ds(chunk * T, T)][:, :, None].to_broadcast([EP, T, F]), ALU.mult))
                    one_hots(ph, s, (1,))
                    st.wait("msg")
                    split(st, msg[:, s], lambda k: one_hots(ph, s, ((2, 3), (4, 5), (6, 7), ())[k]))
                    to_stationary(ph, chunk, s, parts, lambda: st.wait("low"))

                all_chunks(dve, l2)
                dve.wait_ge(ev(f"{ph}_summed"), 1)
                link(dve.tensor_copy(aggT[:].rearrange("p a b -> p (a b)"), acc[:, :]), f"{ph}_aggT")
                dve.wait_ge(ev(f"{ph}_agg"), 1)
                link(dve.tensor_tensor(flat(t0), bank[1][0:NP, :], flat(rooted), ALU.add))
                if k == "a":
                    link(dve.tensor_scalar(h[:], t0[:], 0.0, None, ALU.max), "l2b_h")
            link(dve.tensor_reduce(stat[:], t0[:], AX.X, ALU.max))
            link(dve.tensor_tensor(t0[:], t0[:], over(stat), ALU.subtract), "shifted")
            dve.wait_ge(ev("exp_done"), 1)
            link(dve.tensor_reduce(stat[:], t1[:], AX.X, ALU.add), "exp_sum")
            dve.wait_ge(ev("log_done"), 1)
            link(dve.tensor_tensor(t1[:], t0[:], over(stat2), ALU.subtract))
            link(dve.tensor_tensor(x[:], x[:], t1[:], ALU.add))
            layernorm("ln3")
            link(dve.tensor_tensor(t0[:], h[:], over(out_scale), ALU.mult))
            link(dve.tensor_copy(stage3[:, :, 0:F], t0[:]))
            link(dve.tensor_tensor(t1[:], t0[:], stage3[:, :, 0:F], ALU.subtract))
            link(dve.tensor_copy(stage3[:, :, F:2 * F], t1[:]))
            link(dve.tensor_tensor(stage3[:, :, 2 * F:], t1[:], stage3[:, :, F:2 * F], ALU.subtract), "l3_stage_ready")

            def l3(chunk, pair, s):
                st = Steps("l3", chunk, s)
                dve.wait_ge(fields_in[s], fields_in_by("l3", pair))
                slot_free("l3", chunk)
                st.mark(matches(is_lo[:, s], count_lo, s, DST_LO, LO))
                one_hots("l3", s, range(T - 1))
                dve.wait_ge(S["l3"]["rows_in"][s], 16 * T * (pair + 1))
                st.mark(dve.tensor_scalar(one_hot[:, s, T - 1, :], count_hi[:, :], scalar_field(s, DST_HI, T - 1), None, ALU.is_equal))
                to_stationary("l3", chunk, s, gathered3)

            all_chunks(dve, l3)
            dve.wait_ge(ev("l3_summed"), 1)
            link(dve.tensor_copy(aggT[:].rearrange("p a b -> p (a b)"), acc[:, :]), "l3_aggT")
            dve.wait_ge(ev("l3_agg"), 1)
            link(dve.tensor_tensor(t0[:], bank[1][0:NP, :].rearrange("p (l f) -> p l f", f=F), over(in_scale), ALU.mult))
            link(dve.tensor_tensor(t1[:], t0[:], x[:], ALU.add), "result_ready")


_INS = ["x", "src", "dst", "edge_attr_16", "edge_attr_8", "edge_type_8",
        "L0_gnn_W1", "L0_gnn_b1", "L0_gnn_W2", "L0_gnn_b2", "L0_gnn_root", "L0_gnn_bias", "L0_gnn_gamma", "L0_gnn_beta",
        "L1_gnn_W_msg_tp", "L1_gnn_W_msg_lin", "L1_gnn_W_upd_tp", "L1_gnn_W_upd_lin",
        "L2_gnn_W1", "L2_gnn_root1", "L2_gnn_b1", "L2_gnn_W2", "L2_gnn_root2", "L2_gnn_b2"]


def constants():
    part = np.arange(128)[:, None] // F % 3 == np.arange(3)[None, :]
    return {
        "c_valid": (np.arange(SLOTS) < N_NODES).reshape(NP, LOCAL).astype(np.float32),
        "c_ident": np.eye(128, dtype=np.float32),
        "c_hi": np.tile(np.arange(HI, dtype=np.float16), (EP, 1)),
        "c_key": np.tile(np.arange(LO * RELATIONS, dtype=np.float32), (EP, 1)),
        "c_part": part.astype(np.float32),
    }


def kernel(**inputs):
    import concourse.bacc as _bacc
    from concourse.bass_utils import run_bass_kernel_spmd as _run

    nc = _bacc.Bacc("TRN2", target_bir_lowering=False, num_devices=1)
    arrays, aps = {}, {}
    given = {k: np.ascontiguousarray(inputs[k]) for k in _INS}
    for name, a in {**given, **constants()}.items():
        arrays[f"in_{name}"] = a
        aps[name] = nc.dram_tensor(f"in_{name}", a.shape, mybir.dt.from_np(a.dtype), kind="ExternalInput").ap()
    out = nc.dram_tensor("out_0", (N_NODES, F), F32, kind="ExternalOutput").ap()
    build(nc, aps, out)
    r = _run(nc, [arrays], core_ids=[0])
    return r.results[0]["out_0"]
```

```python
import numpy as np
import concourse.bass as bass
from concourse import mybir
from contextlib import ExitStack

ALU = mybir.AluOpType
ACT = mybir.ActivationFunctionType
AX = mybir.AxisListType
F32 = mybir.dt.float32
BF16 = mybir.dt.bfloat16
F16 = mybir.dt.float16
I32 = mybir.dt.int32

N_NODES, F, RELATIONS = 3125, 16, 8
EP, T = 125, 8
E = 100000
TILES = E // EP
CHUNKS = TILES // T
PAIRS = CHUNKS // 2
NEAR = 2
FAR = T - NEAR
NEARS = 2 * NEAR
LO = 8
LOCAL = 32
NP = -(-N_NODES // LOCAL)
GROUPS = LOCAL // LO
SLOTS = NP * LOCAL
HI = SLOTS // LO
FULL = N_NODES // LOCAL
REST = N_NODES - FULL * LOCAL
HID = F * F
PART = 3 * F
W = LO * F
SRC, DST, SRC_KEY, SRC_HI, SRC_LO, DST_HI, DST_LO, DST_KEY, TYPE, FIELDS = range(10)
EPS = 1e-5


def build(nc, A, out):
    with ExitStack() as ctx:
        def sb(name, shape, dt=F32):
            return ctx.enter_context(nc.sbuf_tensor(name, shape, dt))

        def sem(name):
            return ctx.enter_context(nc.semaphore(name))

        events = {}

        def ev(name):
            if name not in events:
                events[name] = sem(name)
            return events[name]

        meta_d = nc.dram_tensor("edge_fields", [EP, CHUNKS, FIELDS * T], I32).ap()
        table0 = nc.dram_tensor("table_l0", [SLOTS, 2 * F], F32).ap()
        table1 = nc.dram_tensor("table_l1", [SLOTS, RELATIONS * F + RELATIONS], F32).ap()
        table2 = {"a": nc.dram_tensor("table_l2a", [SLOTS * RELATIONS, F], F32).ap(),
                  "b": nc.dram_tensor("table_l2b", [SLOTS * RELATIONS, F], F32).ap()}
        table3 = nc.dram_tensor("table_l3", [SLOTS, F], F32).ap()
        near_hi_d = nc.dram_tensor("near_src_hi", [CHUNKS, NEAR * EP], F16).ap()

        ident = sb("ident", [128, 128])
        ident16 = sb("ident16", [128, 128], BF16)
        count_hi = sb("count_hi", [EP, HI], F16)
        count_key = sb("count_key", [EP, LO * RELATIONS])
        valid = sb("valid", [NP, LOCAL])
        part_of_row = sb("part_of_row", [128, 3])
        ones = sb("ones", [NP, NP])

        w1 = sb("w1", [128, HID])
        w1_stack = sb("w1_stack", [128, HID], BF16)
        w1_hi = sb("w1_hi", [128, HID], BF16)
        w1_mid = sb("w1_mid", [128, HID], BF16)
        w1_rest = sb("w1_rest", [128, HID])
        w1_lo = sb("w1_lo", [128, HID])
        w2 = sb("w2", [128, 2, HID])
        b1 = sb("b1", [128, 2])
        SQUARE = ("b2", "root", "lin", "upd_lin", "root1", "root2")
        bd = {k: sb(f"bd_{k}", [128, W]) for k in SQUARE}
        bd["msg"] = sb("bd_msg", [128, LO, RELATIONS * F])
        bd["upd"] = sb("bd_upd", [128, LO, HID])
        bd["rel1"] = sb("bd_rel1", [128, LO, RELATIONS, F])
        bd["rel2"] = sb("bd_rel2", [128, LO, RELATIONS, F])
        rows16 = sb("rows16", [NP, 5, F])
        BIAS, GAMMA, BETA, B1, B2 = range(5)

        x = sb("x_nodes", [NP, LOCAL, F])
        h = sb("h", [NP, LOCAL, F])
        t0 = sb("t0", [NP, LOCAL, F])
        t1 = sb("t1", [NP, LOCAL, F])
        rooted = sb("rooted", [NP, LOCAL, F])
        stat = sb("stat", [NP, LOCAL])
        stat2 = sb("stat2", [NP, LOCAL])
        chan = sb("chan", [NP, F])
        chan2 = sb("chan2", [NP, F])
        hT = sb("hT", [W, GROUPS, NP])
        aggT = sb("aggT", [W, NP, GROUPS])
        sT = sb("sT", [W, NP, GROUPS])
        cntT = sb("cntT", [LO * RELATIONS, NP, GROUPS])
        cnt = sb("cnt", [NP, GROUPS * LO * RELATIONS])
        degT = sb("degT", [LO, NP, GROUPS])
        in_scale = sb("in_scale", [NP, LOCAL])
        out_scale = sb("out_scale", [NP, LOCAL])
        stage0 = sb("stage0", [NP, LOCAL, 2 * F])
        stage1 = sb("stage1", [NP, LOCAL, RELATIONS * F + RELATIONS])
        stage2 = stage1[:].rearrange("p l f -> p (l f)")[:, 0:LOCAL * RELATIONS * F]
        node_parts = sb("node_parts", [NP, 3, GROUPS, W], BF16)
        gated = sb("gated", [NP, 2, 2, F, F])

        src = sb("src_rows", [EP, TILES], I32)
        dst = sb("dst_rows", [EP, TILES], I32)
        typ = sb("types", [EP, TILES], I32)
        work = sb("work", [EP, TILES], I32)
        work2 = sb("work2", [EP, TILES], I32)
        fields_all = sb("fields_all", [EP, CHUNKS, FIELDS, T], I32)
        reused = fields_all[:].rearrange("p c k t -> p (c k t)").bitcast(F32)
        used = [0]

        def reuse(*shape):
            size = int(np.prod(shape))
            at, used[0] = used[0], used[0] + size
            assert used[0] <= TILES * FIELDS
            names = " ".join("abcd"[:len(shape)])
            return reused[:, at:at + size].rearrange(f"p ({names}) -> p {names}", **dict(zip("abcd", shape)))

        row_numbers = sb("row_numbers", [EP, 2, T], I32)
        fields = sb("fields", [EP, 2, FIELDS, T], I32)
        edge_norm = sb("edge_norm", [EP, TILES])
        ea = sb("ea", [EP, 2, T, F])
        ea_rest = sb("ea_rest", [EP, T, F])
        ea_rest2 = sb("ea_rest2", [EP, T, F])
        ea8 = sb("ea8", [EP, 2, T, RELATIONS])
        stack = sb("stack", [EP, 2, T, 8, F], BF16)
        eaT = sb("eaT", [128, T * EP], BF16)
        h1T = sb("h1T", [128, 2, T * EP])
        gathered0 = sb("gathered0", [EP, 2, T, 2 * F])
        gathered1 = reuse(2, T, RELATIONS * F + RELATIONS)
        gathered2 = sb("gathered2", [EP, 2, T, F])
        near_hi_rows = sb("near_hi_rows", [CHUNKS, NEAR * EP], F16)
        near_hi = sb("near_hi", [NP, NEARS * EP], F16)
        near_lo = sb("near_lo", [EP, CHUNKS, NEAR])
        near_type = sb("near_type", [EP, CHUNKS, NEAR])
        near_one_hot = sb("near_one_hot", [NP, GROUPS, NEARS * EP], BF16)
        near_is_lo = sb("near_is_lo", [EP, NEARS, LO])
        near_is_type = sb("near_is_type", [EP, NEARS, RELATIONS])
        near_mask = sb("near_mask", [EP, NEARS, LO, F], BF16)
        near_picked = reused[:, TILES * FIELDS - NEARS * W:].rearrange("p (t a f) -> p t a f", t=NEARS, a=LO)
        near_row = sb("near_row", [EP, NEARS, F])
        near_outer = reused[:, TILES * FIELDS - 2 * NEARS * W:TILES * FIELDS - NEARS * W].rearrange(
            "p (t r f) -> p t r f", t=NEARS, r=RELATIONS)
        near_outerT = sb("near_outerT", [128, NEARS * EP])
        relations = sb("relation_weights", [RELATIONS * F, 2, F])
        node_hi = sb("node_hi", [NP, GROUPS])
        product = sb("product", [EP, 2, 2, F, F])
        product1 = reuse(T, RELATIONS * F)
        msg = sb("msg", [EP, 2, T, F])
        raw = sb("raw", [EP, 2, T, F])
        rest = sb("rest", [EP, T, F])
        parts = sb("parts", [EP, 2, T, PART], BF16)
        is_lo = sb("is_lo", [EP, 2, T, LO])
        is_type = sb("is_type", [EP, T, RELATIONS])
        lo_bf = sb("lo_bf", [EP, 2, T, LO], BF16)
        mask = sb("mask", [EP, 2, T, LO, F], BF16)
        key_mask = sb("key_mask", [EP, 2, T, LO * RELATIONS], BF16)
        one_hot = sb("one_hot", [EP, 2, T, HI], BF16)
        stationary = sb("stationary", [EP, 2, 3, T, LO, F], BF16)
        zeros = sb("zeros", [EP, HI + W], BF16)
        zero_moving, zero_stationary = zeros[:, 0:HI], zeros[:, HI:]
        spare = sb("spare", [EP, 2])

        acc = ctx.enter_context(nc.psum_tensor("acc", [128, HI], F32))
        counts = ctx.enter_context(nc.psum_tensor("counts", [128, HI], F32))
        eaT_ps = ctx.enter_context(nc.psum_tensor("eaT_ps", [128, T, EP + 1], BF16))
        bank = [ctx.enter_context(nc.psum_tensor(f"bank{i}", [128, 512], F32)) for i in range(5)]

        PHASES = ("l0", "l1", "l2a", "l2b", "l3")
        S = {}
        for ph in PHASES:
            S[ph] = {
                "rows_in": [sem(f"{ph}_rows_in{s}") for s in range(2)],
                "step": sem(f"{ph}_vector_step"),
            }
        fields_in = [sem(f"fields_in{s}") for s in range(2)]
        numbers_in = [sem(f"row_numbers_in{s}") for s in range(2)]
        masked = sem("mask_ready")
        operands = sem("operands_ready")
        added = sem("chunk_added")

        def before(ph):
            return CHUNKS * PHASES.index(ph)

        def fields_in_by(ph, pair):
            return 16 * (before(ph) // 2 + pair + 1)

        near_hi_in = sem("near_hi_in")
        near_hot = sem("near_one_hots_ready")
        near_los = sem("near_lo_ready")
        near_masked = sem("near_mask_ready")
        near_gathered = sem("near_rows_in_psum")
        near_multiplied = sem("near_rows_masked")
        near_summed = sem("near_rows_ready")
        near_outers = sem("near_outer_ready")
        near_turned = sem("near_outer_transposed")
        near_copied = sem("near_outerT_ready")
        near_done = sem("near_messages_ready")

        def tiles_in(ph):
            return T if ph in ("l0", "l1") else FAR

        def pairs_before(ph):
            return PAIRS * ("l2a", "l2b", "l3").index(ph)

        ea_in = [sem(f"ea_in{s}") for s in range(2)]
        ea8_in = [sem(f"ea8_in{s}") for s in range(2)]
        ea_copied = sem("ea_parts_copied")
        ea_split = sem("ea_rest_ready")
        ea_turned = sem("ea_transposed")
        eaT_ready = sem("eaT_ready")
        h1_made = sem("h1_made")
        h1_ready = sem("h1_relu_done")
        w_made = sem("edge_weights_made")
        w_used = sem("edge_weights_used")
        products_summed = sem("products_summed")
        silu_ready = sem("silu_ready")

        gathered = {"l0": gathered0, "l1": gathered1, "l2a": gathered2, "l2b": gathered2, "l3": gathered2}
        table = {"l0": table0, "l1": table1, "l2a": table2["a"], "l2b": table2["b"], "l3": table3}
        row_field = {"l0": SRC, "l1": DST, "l2a": SRC_KEY, "l2b": SRC_KEY, "l3": SRC}
        hi_field = {"l0": DST_HI, "l1": SRC_HI, "l2a": DST_HI, "l2b": DST_HI, "l3": DST_HI}
        lo_field = {"l0": DST_LO, "l1": SRC_LO, "l2a": DST_LO, "l2b": DST_LO, "l3": DST_LO}
        ORDER = {
            "l0": ("is_lo", "msg", "hi", "rest", "mid", "low", "fields_read"),
            "l1": ("is_lo", "raw", "typed", "weighed", "rows_read", "hi", "rest", "mid", "low"),
            "l2a": ("is_lo", "msg", "hi", "rest", "mid", "low"),
            "l3": ("is_lo", "hi", "rest", "mid", "low"),
        }
        ORDER["l2b"] = ORDER["l2a"]
        FIELDS_READ = {"l0": "fields_read", "l1": "hi", "l2a": "low", "l2b": "low", "l3": "low"}
        ROWS_READ = {"l0": "msg", "l1": "rows_read", "l2a": "msg", "l2b": "msg", "l3": "low"}

        def done(ph, name, chunk):
            return chunk * len(ORDER[ph]) + ORDER[ph].index(name) + 1

        def later(chunk, n):
            return not isinstance(chunk, int) or chunk >= n

        def all_chunks(eng, body, after_first=None):
            for s in range(2):
                body(s, 0, s)
            if after_first:
                after_first()
            with eng.Fori(1, PAIRS) as pair:
                for s in range(2):
                    body(2 * pair + s, pair, s)

        def pairs_of_ends(eng, body):
            for s in range(2):
                body(s, 0, s, False)
            with eng.Fori(1, PAIRS - 1) as pair:
                for s in range(2):
                    body(2 * pair + s, pair, s, False)
            for s in range(2):
                body(CHUNKS - 2 + s, PAIRS - 1, s, s == 1)

        def near_pairs(eng, body):
            body(0, True, True)
            with eng.Fori(1, PAIRS - 2) as pair:
                body(pair, True, True)
            body(PAIRS - 2, True, False)
            body(PAIRS - 1, False, False)

        as_nodes = [(slice(0, FULL), slice(0, LOCAL), slice(0, FULL * LOCAL)),
                    (slice(FULL, NP), slice(0, REST), slice(FULL * LOCAL, N_NODES))]

        block = ctx.enter_context(nc.Block())

        @block.sync
        def _(sp):
            sp.dma_start(src[:], A["src"].rearrange("(p t) -> p t", p=EP)).then_inc(ev("src_in"), 16)
            sp.dma_start(dst[:], A["dst"].rearrange("(p t) -> p t", p=EP)).then_inc(ev("dst_in"), 16)
            sp.dma_start(typ[:], A["edge_type_8"].rearrange("(p t) -> p t", p=EP)).then_inc(ev("type_in"), 16)
            sp.dma_start(valid[:], A["c_valid"]).then_inc(ev("consts_in"), 16)
            sp.dma_start(ident[:], A["c_ident"]).then_inc(ev("consts_in"), 16)
            sp.dma_start(count_hi[:], A["c_hi"]).then_inc(ev("consts_in"), 16)
            sp.dma_start(count_key[:], A["c_key"]).then_inc(ev("consts_in"), 16)
            sp.dma_start(part_of_row[:], A["c_part"]).then_inc(ev("consts_in"), 16)
            sp.dma_start(node_hi[:], A["c_node_hi"]).then_inc(ev("consts_in"), 16)
            sp.wait_ge(ev("x_cleared"), 1)
            for p, l, n in as_nodes:
                sp.dma_start(x[p, l, :], A["x"][n].rearrange("(p l) f -> p l f", l=l.stop)).then_inc(ev("x_in"), 16)
            for k in range(8):
                sp.dma_start(w1[k * F:(k + 1) * F, :], A["L0_gnn_W1"]).then_inc(ev("w1_in"), 16)
            for a in range(2):
                sp.dma_start(b1[:, a:a + 1], A["L0_gnn_b1"][a * 128:(a + 1) * 128][:, None]).then_inc(ev("w1_in"), 16)
            sp.dma_start(w2[:], A["L0_gnn_W2"].rearrange("(a p) n -> p a n", a=2)).then_inc(ev("w2_in"), 16)
            for i, k in enumerate(("L0_gnn_bias", "L0_gnn_gamma", "L0_gnn_beta", "L2_gnn_b1", "L2_gnn_b2")):
                sp.dma_start(rows16[:, i, :], A[k][None, :].to_broadcast([NP, F])).then_inc(ev("rows16_in"), 16)
            sp.wait_ge(ev("diagonals_cleared"), len(bd))
            blocks = {"b2": A["L0_gnn_b2"].rearrange("(i o) -> i o", o=F), "root": A["L0_gnn_root"],
                      "lin": A["L1_gnn_W_msg_lin"], "upd_lin": A["L1_gnn_W_upd_lin"],
                      "root1": A["L2_gnn_root1"], "root2": A["L2_gnn_root2"]}
            for lo in range(LO):
                rows = slice(lo * F, (lo + 1) * F)
                for k in ("b2", "root"):
                    sp.dma_start(bd[k][rows, rows], blocks[k]).then_inc(ev("l0_diagonals_in"), 16)

            def later_weights():
                for i in range(2):
                    sp.dma_start(relations[:, i, :], A[f"L2_gnn_W{i + 1}"].rearrange("r i o -> (r i) o")).then_inc(ev("diagonals_in"), 16)
                sp.wait_ge(ev("near_hi_turned"), 1)
                sp.dma_start(near_hi_d, near_hi_rows[:]).then_inc(ev("near_hi_stored"), 16)
                for lo in range(LO):
                    rows = slice(lo * F, (lo + 1) * F)
                    for k in ("lin", "upd_lin", "root1", "root2"):
                        sp.dma_start(bd[k][rows, rows], blocks[k]).then_inc(ev("diagonals_in"), 16)
                    sp.dma_start(bd["msg"][rows, lo, :],
                                 A["L1_gnn_W_msg_tp"].rearrange("i j h -> i (j h)")).then_inc(ev("diagonals_in"), 16)
                    sp.dma_start(bd["upd"][rows, lo, :].rearrange("h (i k) -> h i k", k=F),
                                 A["L1_gnn_W_upd_tp"].rearrange("i h k -> h i k")).then_inc(ev("diagonals_in"), 16)
                    for k, w in (("rel1", "L2_gnn_W1"), ("rel2", "L2_gnn_W2")):
                        sp.dma_start(bd[k][rows, lo, :, :], A[w].rearrange("r i o -> i r o")).then_inc(ev("diagonals_in"), 16)

            sp.wait_ge(ev("fields_made"), 1)
            sp.dma_start(meta_d.rearrange("p c (k t) -> p c k t", k=FIELDS), fields_all[:]).then_inc(ev("fields_stored"), 16)
            sp.wait_ge(ev("fields_stored"), 16)

            ea_d = A["edge_attr_16"].rearrange("(p c t) f -> p c (t f)", p=EP, t=T)
            ea8_d = A["edge_attr_8"].rearrange("(p c t) f -> p c (t f)", p=EP, t=T)

            def load_numbers(ph, chunk, pair, s):
                if later(chunk, 2):
                    sp.wait_ge(S[ph]["rows_in"][s], 16 * tiles_in(ph) * pair)
                k = row_field[ph]
                sp.dma_start(row_numbers[:, s, :],
                             meta_d[:, bass.ds(chunk, 1), k * T:(k + 1) * T].rearrange("p c n -> p (c n)")).then_inc(numbers_in[s], 16)

            def load_near_hi(ph, pair):
                if later(pair, 1) or ph != "l2a":
                    sp.wait_ge(near_hot, pairs_before(ph) + pair)
                sp.dma_start(near_hi[:],
                             near_hi_d.rearrange("(a b) n -> a (b n)", b=2)[bass.ds(pair, 1), :].to_broadcast([NP, NEARS * EP])
                             ).then_inc(near_hi_in, 16)

            def stream_near(ph):
                if ph == "l2a":
                    sp.wait_ge(ev("near_hi_stored"), 16)
                load_near_hi(ph, 0)

                def body(pair, ahead1, ahead2):
                    for s in range(2):
                        chunk = 2 * pair + s
                        load_numbers(ph, chunk, pair, s)
                        if later(chunk, 2):
                            sp.wait_ge(S[ph]["step"], done(ph, FIELDS_READ[ph], chunk - 2))
                            sp.sem_inc(ev("chunks_begun"), 1)
                        sp.dma_start(fields[:, s].rearrange("p k t -> p (k t)"),
                                     meta_d[:, bass.ds(chunk, 1), :].rearrange("p c n -> p (c n)")).then_inc(fields_in[s], 16)
                        if s == 0 and isinstance(pair, int) and pair == 0:
                            load_near_hi(ph, 1)
                        if s == 1 and ahead2:
                            load_near_hi(ph, pair + 2)
                near_pairs(sp, body)

            def stream(ph):
                def body(chunk, pair, s):
                    load_numbers(ph, chunk, pair, s)
                    if ph == "l0":
                        if later(chunk, 2):
                            sp.wait_ge(ea_split, 2 * (chunk - 2) + 1)
                        sp.dma_start(ea[:, s].rearrange("p t f -> p (t f)"),
                                     ea_d[:, bass.ds(chunk, 1), :].rearrange("p c n -> p (c n)")).then_inc(ea_in[s], 16)
                    if later(chunk, 2):
                        sp.wait_ge(S[ph]["step"], done(ph, FIELDS_READ[ph], chunk - 2))
                        sp.sem_inc(ev("chunks_begun"), 1)
                    sp.dma_start(fields[:, s].rearrange("p k t -> p (k t)"),
                                 meta_d[:, bass.ds(chunk, 1), :].rearrange("p c n -> p (c n)")).then_inc(fields_in[s], 16)
                    if ph == "l1":
                        sp.dma_start(ea8[:, s].rearrange("p t f -> p (t f)"),
                                     ea8_d[:, bass.ds(chunk, 1), :].rearrange("p c n -> p (c n)")).then_inc(ea8_in[s], 16)
                all_chunks(sp, body, later_weights if ph == "l0" else None)

            def store_table(ph, stage, where):
                sp.wait_ge(ev(f"{ph}_stage_ready"), 1)
                sp.dma_start(where, stage).then_inc(ev(f"{ph}_table_in"), 16)

            store_table("l0", stage0[:].rearrange("p l f -> p (l f)"), table0.rearrange("(p l) f -> p (l f)", p=NP))
            stream("l0")
            store_table("l1", stage1[:].rearrange("p l f -> p (l f)"), table1.rearrange("(p l) f -> p (l f)", p=NP))
            stream("l1")
            for k in ("a", "b"):
                store_table("l2" + k, stage2, table2[k].rearrange("(p l) f -> p (l f)", p=NP))
                stream_near("l2" + k)
            store_table("l3", t0[:].rearrange("p l f -> p (l f)"), table3.rearrange("(p l) f -> p (l f)", p=NP))
            stream_near("l3")
            sp.wait_ge(ev("result_ready"), 1)
            for p, l, n in as_nodes:
                sp.dma_start(out[n].rearrange("(p l) f -> p l f", l=l.stop), t1[p, l, :]).then_inc(ev("stored"), 16)
            sp.wait_ge(ev("stored"), 16 * len(as_nodes))

        @block.gpsimd
        def _(pool):
            pool.memset(x[:], 0.0).then_inc(ev("x_cleared"), 1)
            for k in bd:
                pool.memset(bd[k][:], 0.0).then_inc(ev("diagonals_cleared"), 1)
            pool.memset(ones[:], 1.0).then_inc(ev("ones_set"), 1)

            def gathers(ph):
                pool.wait_ge(ev(f"{ph}_table_in"), 16)

                def body(chunk, pair, s):
                    pool.wait_ge(numbers_in[s], fields_in_by(ph, pair))
                    if later(chunk, 2):
                        pool.wait_ge(S[ph]["step"], done(ph, ROWS_READ[ph], chunk - 2))
                    pool.sem_inc(ev("chunks_begun"), 1)
                    for t in range(tiles_in(ph)):
                        pool.indirect_dma_start(
                            out=gathered[ph][:, s, t, :], in_=table[ph], out_offset=None,
                            in_offset=bass.IndirectOffsetOnAxis(ap=row_numbers[:, s, t:t + 1], axis=0),
                        ).then_inc(S[ph]["rows_in"][s], 16)
                all_chunks(pool, body)

            for ph in PHASES:
                gathers(ph)

        @block.tensor
        def _(pe):
            def add_chunk(ph, chunk, s, tiles=range(T), first=False, last=False):
                for t in tiles:
                    for k in range(3):
                        mm = pe.matmul(acc[:, :], stationary[:, s, k, t, :, :].rearrange("p a b -> p (a b)"),
                                       one_hot[:, s, t, :], start=first and t == 0 and k == 0,
                                       stop=last and t == T - 1 and k == 2)
                    if ph == "l0":
                        mm = pe.matmul(counts[0:LO * RELATIONS, :], key_mask[:, s, t, :], one_hot[:, s, t, :],
                                       start=first and t == 0, stop=last and t == T - 1)
                    if ph == "l1":
                        mm = pe.matmul(counts[0:LO, :], lo_bf[:, s, t, :], one_hot[:, s, t, :],
                                       start=first and t == 0, stop=last and t == T - 1)
                if T - 1 in tiles:
                    mm.then_inc(added, 1)

            def turn_h(name):
                pe.wait_ge(ev(f"{name}_h"), 1)
                for c in range(GROUPS):
                    mm = pe.transpose(bank[0][:, c * NP:(c + 1) * NP], h[:, c * LO:(c + 1) * LO, :].rearrange("p l f -> p (l f)"),
                                      ident[0:NP, 0:NP])
                mm.then_inc(ev(f"{name}_turned"), 1)
                pe.wait_ge(ev(f"{name}_hT"), 1)

            def times(name, into, w):
                for c in range(GROUPS):
                    mm = pe.matmul(into[0:NP, c * W:(c + 1) * W], hT[:, c, :], bd[w][:, :], start=True, stop=True)
                mm.then_inc(ev(name), 1)

            def wide(name, w):
                flat = bd[w][:].rearrange("p a b c -> p (a b c)") if len(bd[w].shape) == 4 else bd[w][:].rearrange("p a b -> p (a b)")
                for i in range(2 * GROUPS):
                    if i >= 2:
                        pe.wait_ge(ev(f"{name}_wide_read"), i - 1)
                    pe.matmul(bank[2 + i % 2][0:NP, :], hT[:, i // 2, :], flat[:, (i % 2) * 512:(i % 2 + 1) * 512],
                              start=True, stop=True).then_inc(ev(f"{name}_wide"), 1)

            def turn_back(ph, source=None, ready=None):
                pe.wait_ge(ev(ready or f"{ph}_aggT"), 1)
                for c in range(GROUPS):
                    mm = pe.transpose(bank[1][0:NP, c * W:(c + 1) * W], (source or aggT)[:, :, c], ident[:, :])
                mm.then_inc(ev(f"{ph}_agg"), 1)

            pe.wait_ge(ev("consts_in"), 96)
            pe.wait_ge(ev("fields_made"), 1)
            for j in range(NEAR):
                mm = pe.transpose(bank[4][0:CHUNKS, j * EP:(j + 1) * EP],
                                  fields_all[:, :, SRC_HI, FAR + j].bitcast(F32), ident[0:EP, 0:EP])
            mm.then_inc(ev("near_hi_in_psum"), 1)
            turn_h("l0")
            pe.wait_ge(ev("l0_diagonals_in"), 16 * 2 * LO)
            times("l0_b2_made", bank[1], "b2")
            times("l0_root_made", bank[2], "root")

            pe.wait_ge(ev("w1_stacked"), 1)
            pe.wait_ge(ev("w2_in"), 16)
            pe.wait_ge(ev("ident16_made"), 1)
            pe.wait_ge(ev("l0_rooted"), 1)
            pe.wait_ge(ev("zeros_set"), 1)
            pe.matmul(acc[:, :], zero_stationary, zero_moving, start=True, stop=False)
            pe.matmul(counts[0:LO * RELATIONS, :], zero_stationary[:, 0:LO * RELATIONS], zero_moving, start=True, stop=False)

            def turn_ea(chunk, s):
                pe.wait_ge(ea_copied, 3 * (chunk + 1))
                if later(chunk, 1):
                    pe.wait_ge(eaT_ready, chunk)
                for t in range(T):
                    mm = pe.transpose(eaT_ps[:, t, 0:EP],
                                      stack[:, s, t, :, :].rearrange("p a b -> p (a b)"), ident16[0:EP, 0:EP])
                mm.then_inc(ea_turned, 1)

            def hidden(chunk, g):
                if g >= 2 or later(chunk, 1):
                    pe.wait_ge(h1_ready, 4 * chunk + g - 1)
                if g == 0:
                    pe.wait_ge(eaT_ready, chunk + 1)
                half, side = g % 2, g // 2
                pe.matmul(bank[g % 2][:, 0:4 * EP], w1_stack[:, half * 128:(half + 1) * 128],
                          eaT[:, side * 4 * EP:(side + 1) * 4 * EP], start=True, stop=True).then_inc(h1_made, 1)

            def edge_weights(chunk):
                pe.wait_ge(h1_ready, 4 * chunk + 4)
                for q in range(T // 2):
                    if q >= 2 or later(chunk, 1):
                        pe.wait_ge(w_used, 4 * chunk + q - 1)
                    for j in range(2):
                        t = 2 * q + j
                        for half in range(2):
                            mm = pe.matmul(bank[2 + q % 2][0:EP, j * HID:(j + 1) * HID],
                                           h1T[:, half, t * EP:(t + 1) * EP], w2[:, half, :],
                                           start=half == 0, stop=half == 1)
                    mm.then_inc(w_made, 1)

            def l0(chunk, pair, s, last):
                def quarter(q):
                    if later(chunk, 2):
                        add_chunk("l0", chunk - 2, s, range(2 * q, 2 * q + 2))

                if later(chunk, 2):
                    pe.wait_ge(operands, before("l0") + chunk - 1)
                quarter(0)
                turn_ea(chunk, s)
                quarter(1)
                hidden(chunk, 0)
                hidden(chunk, 1)
                quarter(2)
                hidden(chunk, 2)
                hidden(chunk, 3)
                quarter(3)
                edge_weights(chunk)
                if last:
                    for n in (CHUNKS - 2, CHUNKS - 1):
                        pe.wait_ge(operands, before("l0") + n + 1)
                        add_chunk("l0", n, n % 2, last=n == CHUNKS - 1)

            pairs_of_ends(pe, l0)
            turn_back("l0")
            pe.wait_ge(ev("ones_set"), 1)
            for k in ("mean", "var"):
                pe.wait_ge(ev(f"bn_{k}_in"), 1)
                pe.matmul(bank[0][0:NP, :], ones[:, :], t0[:].rearrange("p l f -> p (l f)"),
                          start=True, stop=True).then_inc(ev(f"bn_{k}_sum"), 1)
            pe.wait_ge(ev("cntT_ready"), 1)
            KW = LO * RELATIONS
            for c in range(GROUPS):
                mm = pe.transpose(bank[4][0:NP, c * KW:(c + 1) * KW], cntT[:, :, c], ident[0:KW, 0:KW])
            mm.then_inc(ev("cnt_turned"), 1)
            turn_h("l1")
            pe.wait_ge(ev("diagonals_in"), 16 * (8 * LO + 2))
            wide("l1", "msg")

            def sum_only(ph):
                def body(chunk, pair, s):
                    pe.wait_ge(operands, before(ph) + chunk + 1)
                    add_chunk(ph, chunk, s, first=isinstance(chunk, int) and chunk == 0)
                all_chunks(pe, body)
                pe.wait_ge(ev("zeros_set"), 1)
                mm = pe.matmul(acc[:, :], zero_stationary, zero_moving, start=False, stop=True)
                if ph == "l1":
                    mm = pe.matmul(counts[0:LO, :], zero_stationary[:, 0:LO], zero_moving, start=False, stop=True)
                mm.then_inc(ev(f"{ph}_summed"), 1)

            def near_rows(ph, pair):
                pe.wait_ge(near_hot, pairs_before(ph) + pair + 1)
                for t in range(NEARS):
                    for c in range(GROUPS):
                        for k in range(3):
                            mm = pe.matmul(bank[0][0:EP, t * W:(t + 1) * W], near_one_hot[:, c, t * EP:(t + 1) * EP],
                                           node_parts[:, k, c, :], start=c == 0 and k == 0, stop=c == GROUPS - 1 and k == 2)
                mm.then_inc(near_gathered, 1)

            def near_turn(ph, pair):
                pe.wait_ge(near_outers, pairs_before(ph) + pair + 1)
                for t in range(NEARS):
                    mm = pe.transpose(bank[1][:, t * EP:(t + 1) * EP], near_outer[:, t, :, :].rearrange("p r f -> p (r f)"),
                                      ident[0:EP, 0:EP])
                mm.then_inc(near_turned, 1)

            def near_messages(ph, pair):
                pe.wait_ge(near_copied, pairs_before(ph) + pair + 1)
                for t in range(NEARS):
                    mm = pe.matmul(bank[4][0:EP, t * F:(t + 1) * F], near_outerT[:, t * EP:(t + 1) * EP],
                                   relations[:, "ab".index(ph[2]), :], start=True, stop=True)
                mm.then_inc(near_done, 1)

            def sum_near(ph):
                pe.wait_ge(ev(f"{ph}_parts_ready"), 1)
                near_rows(ph, 0)
                if ph != "l3":
                    near_turn(ph, 0)
                    near_messages(ph, 0)
                near_rows(ph, 1)

                def body(pair, ahead1, ahead2):
                    pe.wait_ge(operands, before(ph) + 2 * pair + 1)
                    add_chunk(ph, 2 * pair, 0, first=isinstance(pair, int) and pair == 0)
                    if ahead1 and ph != "l3":
                        near_turn(ph, pair + 1)
                    if ahead2:
                        near_rows(ph, pair + 2)
                    if ahead1 and ph != "l3":
                        near_messages(ph, pair + 1)
                    pe.wait_ge(operands, before(ph) + 2 * pair + 2)
                    add_chunk(ph, 2 * pair + 1, 1, last=not ahead1)
                near_pairs(pe, body)

            sum_only("l1")
            pe.wait_ge(ev("l1_sT"), 1)
            pe.matmul(bank[0][:, 0:HI], bd["lin"][:, :], sT[:].rearrange("p a b -> p (a b)"),
                      start=True, stop=True).then_inc(ev("l1_lin"), 1)
            pe.wait_ge(ev("degT_ready"), 1)
            for c in range(GROUPS):
                mm = pe.transpose(bank[4][0:NP, c * LO:(c + 1) * LO], degT[:, :, c], ident[0:LO, 0:LO])
            mm.then_inc(ev("deg_turned"), 1)
            pe.wait_ge(ev("l1_aggT"), 1)
            for i in range(4 * GROUPS):
                if i >= 2:
                    pe.wait_ge(ev("upd_read"), i - 1)
                c, q = divmod(i, 4)
                pe.matmul(bank[2 + i % 2][0:NP, :], aggT[:, :, c],
                          bd["upd"][:, 2 * q:2 * q + 2, :].rearrange("p a b -> p (a b)"),
                          start=True, stop=True).then_inc(ev("upd_made"), 1)
            turn_h("u")
            times("u_lin", bank[1], "upd_lin")
            for k in ("1", "2"):
                ph = "l2" + "ab"[int(k) - 1]
                turn_h(ph)
                times(f"{ph}_root_made", bank[1], "root" + k)
                wide(ph, "rel" + k)
                sum_near(ph)
                turn_back(ph)
            sum_near("l3")
            turn_back("l3")

        @block.scalar
        def _(act):
            def masks(ph, chunk, s):
                act.wait_ge(S[ph]["step"], done(ph, "is_lo", chunk))
                if later(chunk, 2):
                    act.wait_ge(operands, before(ph) + chunk - 1)
                if ph == "l1":
                    if later(chunk, 2):
                        act.wait_ge(added, before(ph) + chunk - 1)
                    act.copy(lo_bf[:, s], is_lo[:, s])
                act.copy(mask[:, s].rearrange("p t a f -> p (t a) f"),
                         is_lo[:, s].rearrange("p t a -> p (t a)")[:, :, None].to_broadcast([EP, T * LO, F])
                         ).then_inc(masked, 1)

            def turned(name):
                act.wait_ge(ev(f"{name}_turned"), 1)
                act.copy(hT[:].rearrange("p a b -> p (a b)"), bank[0][:, 0:HI]).then_inc(ev(f"{name}_hT"), 1)

            def root(name):
                act.wait_ge(ev(name), 1)

            def standard(name):
                act.wait_ge(ev(f"{name}_var"), 1)
                act.activation(stat2[:], stat[:], ACT.Sqrt).then_inc(ev(f"{name}_std"), 1)

            def relation_rows(name, stage):
                for i in range(2 * GROUPS):
                    act.wait_ge(ev(f"{name}_wide"), i + 1)
                    source = bank[2 + i % 2][0:NP, :]
                    if name == "l1":
                        ins = act.copy(stage[:, 4 * i:4 * i + 4, 0:RELATIONS * F],
                                       source.rearrange("p (a b) -> p a b", a=4))
                    else:
                        ins = act.copy(stage[:, 512 * i:512 * (i + 1)], source)
                    ins.then_inc(ev(f"{name}_wide_read"), 1)

            standard("ln0")
            act.wait_ge(ev("near_hi_in_psum"), 1)
            act.copy(near_hi_rows[:], bank[4][0:CHUNKS, 0:NEAR * EP]).then_inc(ev("near_hi_turned"), 1)
            turned("l0")
            act.wait_ge(ev("w1_in"), 160)

            def spread(chunk, pair, s, k):
                if k == 0:
                    act.wait_ge(ea_in[s], 16 * (pair + 1))
                    if later(chunk, 2):
                        act.wait_ge(ea_turned, chunk - 1)
                else:
                    act.wait_ge(ea_split, 2 * chunk + k)
                source = (ea[:, s], ea_rest[:], ea_rest2[:])[k]
                n = 3 if k < 2 else 2
                act.copy(stack[:, s, :, 3 * k:3 * k + n, :],
                         source[:, :, None, :].to_broadcast([EP, T, n, F])).then_inc(ea_copied, 1)

            for k in range(3):
                spread(0, 0, 0, k)

            def l0(chunk, pair, s, last):
                act.wait_ge(ea_turned, chunk + 1)
                act.copy(eaT[:].rearrange("p (t e) -> p t e", t=T), eaT_ps[:, :, 0:EP]).then_inc(eaT_ready, 1)
                for g in range(4):
                    act.wait_ge(h1_made, 4 * chunk + g + 1)
                    half, side = g % 2, g // 2
                    act.activation(h1T[:, half, side * 4 * EP:(side + 1) * 4 * EP], bank[g % 2][:, 0:4 * EP], ACT.Relu,
                                   bias=b1[:, half:half + 1]).then_inc(h1_ready, 1)
                if not last:
                    spread(chunk + 1, pair + s, 1 - s, 0)
                masks("l0", chunk, s)
                if not last:
                    spread(chunk + 1, pair + s, 1 - s, 1)
                    spread(chunk + 1, pair + s, 1 - s, 2)

            pairs_of_ends(act, l0)
            act.wait_ge(ev("bn_var"), 1)
            act.activation(chan2[:], chan[:], ACT.Sqrt).then_inc(ev("bn_std"), 1)
            standard("ln1")
            standard("in_degree")
            turned("l1")
            relation_rows("l1", stage1)

            def l1(chunk, pair, s):
                masks("l1", chunk, s)
                act.wait_ge(S["l1"]["step"], done("l1", "raw", chunk))
                act.activation(msg[:, s], raw[:, s], ACT.Silu,
                               scale=float(1.0 / np.float32(np.sqrt(F * RELATIONS)))).then_inc(silu_ready, 1)

            act.wait_ge(ev("spare_set"), 1)
            act.activation(spare[:, 1:2], spare[:, 0:1], ACT.Silu).then_inc(ev("silu_loaded"), 1)
            all_chunks(act, l1)
            act.wait_ge(ev("l1_lin"), 1)
            act.mul(aggT[:].rearrange("p a b -> p (a b)"), bank[0][:, 0:HI],
                    float(1.0 / np.float32(np.sqrt(F)))).then_inc(ev("l1_aggT"), 1)
            act.wait_ge(ev("u_raw"), 1)
            act.activation(h[:], t0[:], ACT.Silu, scale=float(1.0 / np.float32(np.sqrt(F * F)))).then_inc(ev("u_h"), 1)
            turned("u")
            standard("ln2")
            standard("out_degree")

            def near_masks(ph, pair):
                act.wait_ge(near_los, pairs_before(ph) + pair + 1)
                act.copy(near_mask[:].rearrange("p t a f -> p (t a) f"),
                         near_is_lo[:].rearrange("p t a -> p (t a)")[:, :, None].to_broadcast([EP, NEARS * LO, F])
                         ).then_inc(near_masked, 1)

            def near_copy(ph, pair):
                act.wait_ge(near_turned, pairs_before(ph) + pair + 1)
                act.copy(near_outerT[:], bank[1][:, 0:NEARS * EP]).then_inc(near_copied, 1)

            def masks_and_near(ph):
                near_masks(ph, 0)
                if ph != "l3":
                    near_copy(ph, 0)
                near_masks(ph, 1)

                def body(pair, ahead1, ahead2):
                    masks(ph, 2 * pair, 0)
                    if ahead2:
                        near_masks(ph, pair + 2)
                    masks(ph, 2 * pair + 1, 1)
                    if ahead1 and ph != "l3":
                        near_copy(ph, pair + 1)
                near_pairs(act, body)

            for ph in ("l2a", "l2b"):
                turned(ph)
                relation_rows(ph, stage2)
                masks_and_near(ph)
            act.wait_ge(ev("shifted"), 1)
            act.activation(t1[:], t0[:], ACT.Exp).then_inc(ev("exp_done"), 1)
            act.wait_ge(ev("exp_sum"), 1)
            act.activation(stat2[:], stat[:], ACT.Ln).then_inc(ev("log_done"), 1)
            standard("ln3")
            masks_and_near("l3")

        @block.vector
        def _(dve):
            chained = sem("vector_chain")
            count = [0]

            def link(ins, event=None):
                if event:
                    ins.then_inc(ev(event), 1)
                    dve.wait_ge(ev(event), 1)
                    return
                count[0] += 1
                ins.then_inc(chained, 1)
                dve.wait_ge(chained, count[0])

            def over(v, n=F):
                return v[:, :, None].to_broadcast([NP, LOCAL, n])

            def row(i):
                return rows16[:, i, :][:, None, :].to_broadcast([NP, LOCAL, F])

            def layernorm(name, scale=None, signal=None):
                link(dve.tensor_reduce(stat[:], x[:], AX.X, ALU.add))
                link(dve.tensor_scalar(stat[:], stat[:], 1.0 / F, None, ALU.mult))
                link(dve.tensor_tensor(t0[:], x[:], over(stat), ALU.subtract))
                link(dve.tensor_tensor(t1[:], t0[:], t0[:], ALU.mult))
                link(dve.tensor_reduce(stat2[:], t1[:], AX.X, ALU.add))
                link(dve.tensor_scalar(stat[:], stat2[:], 1.0 / F, EPS, ALU.mult, ALU.add), f"{name}_var")
                dve.wait_ge(ev(f"{name}_std"), 1)
                link(dve.reciprocal(stat[:], stat2[:]))
                link(dve.tensor_tensor(t1[:], t0[:], over(stat), ALU.mult))
                link(dve.tensor_scalar(h[:], t1[:], 0.0, None, ALU.max), signal)

            def inverse_root(name, into):
                link(dve.tensor_scalar(stat[:], stat[:], 1.0, None, ALU.max), f"{name}_var")
                dve.wait_ge(ev(f"{name}_std"), 1)
                link(dve.reciprocal(into[:], stat2[:]))

            def flat(t):
                return t[:].rearrange("p l f -> p (l f)")

            dve.wait_ge(ev("src_in"), 16)
            dve.wait_ge(ev("dst_in"), 16)
            dve.wait_ge(ev("type_in"), 16)

            def field(k):
                return fields_all[:, :, k, :]

            def by_chunk(v):
                return v[:].rearrange("p (c t) -> p c t", t=T)

            dve.tensor_copy(field(SRC), by_chunk(src))
            dve.tensor_copy(field(DST), by_chunk(dst))
            dve.tensor_copy(field(TYPE).bitcast(F32), by_chunk(typ))
            for v, hi, lo in ((src, SRC_HI, SRC_LO), (dst, DST_HI, DST_LO)):
                link(dve.tensor_scalar(work[:], v[:], 3, None, ALU.logical_shift_right))
                dve.tensor_copy(field(hi).bitcast(F32), by_chunk(work))
                link(dve.tensor_scalar(work2[:], v[:], LO - 1, None, ALU.bitwise_and))
                dve.tensor_copy(field(lo).bitcast(F32), by_chunk(work2))
            link(dve.tensor_scalar(work[:], work2[:], 3, None, ALU.logical_shift_left))
            link(dve.tensor_tensor(work2[:], work[:], typ[:], ALU.bitwise_or))
            dve.tensor_copy(field(DST_KEY).bitcast(F32), by_chunk(work2))
            link(dve.tensor_scalar(work[:], src[:], 3, None, ALU.logical_shift_left))
            link(dve.tensor_tensor(field(SRC_KEY), by_chunk(work), by_chunk(typ), ALU.bitwise_or), "fields_made")

            dve.tensor_copy(near_lo[:], fields_all[:, :, SRC_LO, FAR:T].bitcast(F32))
            dve.tensor_copy(near_type[:], fields_all[:, :, TYPE, FAR:T].bitcast(F32))
            dve.memset(zeros[:], 0.0).then_inc(ev("zeros_set"), 1)
            dve.memset(spare[:], 0.0).then_inc(ev("spare_set"), 1)
            dve.wait_ge(ev("consts_in"), 96)
            link(dve.tensor_copy(ident16[:], ident[:]), "ident16_made")
            dve.wait_ge(ev("x_in"), 32)
            layernorm("ln0", signal="l0_h")
            dve.wait_ge(ev("w1_in"), 160)
            link(dve.tensor_copy(w1_hi[:], w1[:]))
            link(dve.tensor_tensor(w1_rest[:], w1[:], w1_hi[:], ALU.subtract))
            link(dve.tensor_copy(w1_mid[:], w1_rest[:]))
            link(dve.tensor_tensor(w1_lo[:], w1_rest[:], w1_mid[:], ALU.subtract))
            link(dve.tensor_scalar(w1_rest[:], w1_hi[:], part_of_row[:, 0:1], None, ALU.mult))
            link(dve.scalar_tensor_tensor(w1[:], w1_mid[:], part_of_row[:, 1:2], w1_rest[:], ALU.mult, ALU.add))
            link(dve.scalar_tensor_tensor(w1_stack[:], w1_lo[:], part_of_row[:, 2:3], w1[:], ALU.mult, ALU.add), "w1_stacked")
            dve.tensor_copy(stage0[:, :, 0:F], h[:])
            dve.wait_ge(ev("l0_b2_made"), 1)
            link(dve.tensor_copy(stage0[:, :, F:2 * F], bank[1][0:NP, :].rearrange("p (l f) -> p l f", f=F)), "l0_stage_ready")
            dve.wait_ge(ev("l0_root_made"), 1)
            link(dve.tensor_copy(flat(rooted), bank[2][0:NP, :]), "l0_rooted")

            def scalar_field(s, k, t):
                return fields[:, s, k, t:t + 1].bitcast(F32)

            def matches(into, counted, s, k, n):
                return dve.tensor_tensor(into, counted[:, None, 0:n].to_broadcast([EP, T, n]),
                                         fields[:, s, k, :].bitcast(F32)[:, :, None].to_broadcast([EP, T, n]), ALU.is_equal)

            count_lo = count_key[:, 0:LO]

            class Steps:

                def __init__(self, ph, chunk, s):
                    self.ph, self.chunk, self.s = ph, chunk, s

                def mark(self, ins):
                    ins.then_inc(S[self.ph]["step"], 1)

                def wait(self, name):
                    dve.wait_ge(S[self.ph]["step"], done(self.ph, name, self.chunk))

            def one_hots(ph, s, tiles):
                for t in tiles:
                    dve.tensor_scalar(one_hot[:, s, t, :], count_hi[:, :], scalar_field(s, hi_field[ph], t), None, ALU.is_equal)

            def slot_free(ph, chunk):
                if later(chunk, 2):
                    dve.wait_ge(added, before(ph) + chunk - 1)

            def split(st, source, between):
                s = st.s
                st.mark(dve.tensor_copy(parts[:, s, :, 0:F], source))
                between(0)
                st.wait("hi")
                st.mark(dve.tensor_tensor(rest[:], source, parts[:, s, :, 0:F], ALU.subtract))
                between(1)
                st.wait("rest")
                st.mark(dve.tensor_copy(parts[:, s, :, F:2 * F], rest[:]))
                between(2)
                st.wait("mid")
                st.mark(dve.tensor_tensor(parts[:, s, :, 2 * F:3 * F], rest[:], parts[:, s, :, F:2 * F], ALU.subtract))
                between(3)

            def to_stationary(ph, chunk, s, source, ready=None):
                dve.wait_ge(masked, before(ph) + chunk + 1)
                for k in range(3):
                    if k == 2 and ready:
                        ready()
                    ins = dve.tensor_tensor(stationary[:, s, k], mask[:, s],
                                            source[:, s, :, k * F:(k + 1) * F][:, :, None, :].to_broadcast([EP, T, LO, F]), ALU.mult)
                ins.then_inc(operands, 1)

            def split_ea(chunk, s, k):
                source, into = ((ea[:, s], ea_rest), (ea_rest[:], ea_rest2))[k]
                dve.wait_ge(ea_copied, 3 * chunk + k + 1)
                dve.tensor_tensor(into[:], source, stack[:, s, :, 3 * k, :], ALU.subtract).then_inc(ea_split, 1)

            split_ea(0, 0, 0)
            split_ea(0, 0, 1)

            def l0(chunk, pair, s, last):
                st = Steps("l0", chunk, s)
                dve.wait_ge(fields_in[s], fields_in_by("l0", pair))
                st.mark(matches(is_lo[:, s], count_lo, s, DST_LO, LO))
                dve.wait_ge(S["l0"]["rows_in"][s], 16 * T * (pair + 1))

                def multiply(q):
                    dve.wait_ge(w_made, 4 * chunk + q + 1)
                    if q >= 2 or later(chunk, 1):
                        dve.wait_ge(products_summed, 4 * chunk + q - 1)
                    dve.tensor_tensor(product[:, q % 2], bank[2 + q % 2][0:EP, :].rearrange("p (t i o) -> p t i o", t=2, i=F),
                                      gathered0[:, s, 2 * q:2 * q + 2, 0:F][:, :, :, None].to_broadcast([EP, 2, F, F]),
                                      ALU.mult).then_inc(w_used, 1)

                def add_up(q):
                    dve.wait_ge(w_used, 4 * chunk + q + 1)
                    dve.tensor_reduce(raw[:, s, 2 * q:2 * q + 2, :], product[:, q % 2].rearrange("p t i o -> p t o i"),
                                      AX.X, ALU.add).then_inc(products_summed, 1)

                multiply(0)
                for q in range(1, T // 2):
                    multiply(q)
                    add_up(q - 1)
                    if q < 3 and not last:
                        split_ea(chunk + 1, 1 - s, q - 1)
                slot_free("l0", chunk)
                add_up(T // 2 - 1)
                one_hots("l0", s, (0,))
                dve.wait_ge(products_summed, 4 * chunk + 4)
                st.mark(dve.tensor_tensor(msg[:, s], raw[:, s], gathered0[:, s, :, F:2 * F], ALU.add))
                one_hots("l0", s, (1,))
                st.wait("msg")
                split(st, msg[:, s], lambda k: one_hots("l0", s, ((2, 3), (4, 5), (6,), (7,))[k]))
                st.mark(matches(key_mask[:, s], count_key, s, DST_KEY, LO * RELATIONS))
                to_stationary("l0", chunk, s, parts, lambda: st.wait("low"))

            pairs_of_ends(dve, l0)
            dve.wait_ge(added, before("l0") + CHUNKS)
            link(dve.tensor_copy(aggT[:].rearrange("p a b -> p (a b)"), acc[:, :]), "l0_aggT")
            link(dve.tensor_copy(cntT[:].rearrange("p a b -> p (a b)"), counts[0:LO * RELATIONS, :]), "cntT_ready")
            dve.wait_ge(ev("rows16_in"), 80)
            dve.wait_ge(ev("l0_agg"), 1)
            link(dve.tensor_tensor(flat(t1), bank[1][0:NP, :], flat(rooted), ALU.add))
            link(dve.tensor_tensor(rooted[:], t1[:], row(BIAS), ALU.add))
            link(dve.tensor_tensor(t0[:], rooted[:], over(valid), ALU.mult), "bn_mean_in")
            dve.wait_ge(ev("bn_mean_sum"), 1)
            by_channel = bank[0][0:NP, :].rearrange("p (l f) -> p f l", f=F)

            def channels(v):
                return v[:, None, :].to_broadcast([NP, LOCAL, F])

            link(dve.tensor_reduce(chan[:], by_channel, AX.X, ALU.add))
            link(dve.tensor_scalar(chan[:], chan[:], 1.0 / N_NODES, None, ALU.mult))
            link(dve.tensor_tensor(t1[:], rooted[:], channels(chan), ALU.subtract))
            link(dve.tensor_tensor(rooted[:], t1[:], over(valid), ALU.mult))
            link(dve.tensor_tensor(t0[:], rooted[:], rooted[:], ALU.mult), "bn_var_in")
            dve.wait_ge(ev("bn_var_sum"), 1)
            link(dve.tensor_reduce(chan2[:], by_channel, AX.X, ALU.add))
            link(dve.tensor_scalar(chan[:], chan2[:], 1.0 / N_NODES, EPS, ALU.mult, ALU.add), "bn_var")
            dve.wait_ge(ev("bn_std"), 1)
            link(dve.reciprocal(chan[:], chan2[:]))
            link(dve.tensor_tensor(t0[:], t1[:], channels(chan), ALU.mult))
            link(dve.tensor_tensor(t1[:], t0[:], row(GAMMA), ALU.mult))
            link(dve.tensor_tensor(t0[:], t1[:], row(BETA), ALU.add))
            link(dve.tensor_scalar(t1[:], t0[:], 0.0, None, ALU.max))
            link(dve.tensor_tensor(x[:], x[:], t1[:], ALU.add))
            layernorm("ln1", signal="l1_h")
            dve.wait_ge(ev("cnt_turned"), 1)
            link(dve.tensor_copy(cnt[:], bank[4][0:NP, 0:GROUPS * LO * RELATIONS]))
            by_relation = cnt[:].rearrange("p (l r) -> p l r", r=RELATIONS)
            link(dve.tensor_reduce(stat[:], by_relation, AX.X, ALU.add))
            inverse_root("in_degree", in_scale)
            link(dve.tensor_scalar(cnt[:], cnt[:], 1.0, None, ALU.max))
            link(dve.reciprocal(stage1[:, :, RELATIONS * F:], by_relation))
            dve.wait_ge(ev("l1_wide_read"), 2 * GROUPS)
            link(dve.tensor_copy(stat[:, 0:1], stage1[:, 0, 0:1]), "l1_stage_ready")

            def l1(chunk, pair, s):
                st = Steps("l1", chunk, s)
                dve.wait_ge(fields_in[s], fields_in_by("l1", pair))
                slot_free("l1", chunk)
                st.mark(matches(is_lo[:, s], count_lo, s, SRC_LO, LO))
                dve.wait_ge(S["l1"]["rows_in"][s], 16 * T * (pair + 1))
                dve.wait_ge(ea8_in[s], 16 * (pair + 1))
                dve.tensor_tensor(product1.rearrange("p t (j h) -> p t j h", h=F),
                                  gathered1[:, s, :, 0:RELATIONS * F].rearrange("p t (j h) -> p t j h", h=F),
                                  ea8[:, s][:, :, :, None].to_broadcast([EP, T, RELATIONS, F]), ALU.mult
                                  ).then_inc(ev("l1_products"), 1)
                one_hots("l1", s, (0, 1))
                dve.wait_ge(ev("l1_products"), chunk + 1)
                st.mark(dve.tensor_reduce(raw[:, s], product1.rearrange("p t (j h) -> p t h j", h=F), AX.X, ALU.add))
                st.mark(matches(is_type[:], count_lo, s, TYPE, RELATIONS))
                one_hots("l1", s, (2,))
                st.wait("typed")
                st.mark(dve.tensor_tensor(is_type[:], is_type[:], gathered1[:, s, :, RELATIONS * F:], ALU.mult))
                one_hots("l1", s, (3,))
                st.wait("weighed")
                st.mark(dve.tensor_reduce(edge_norm[:, bass.ds(chunk * T, T)], is_type[:], AX.X, ALU.add))
                one_hots("l1", s, (4, 5, 6, 7))
                dve.wait_ge(silu_ready, chunk + 1)
                split(st, msg[:, s], lambda k: None)
                to_stationary("l1", chunk, s, parts, lambda: st.wait("low"))

            all_chunks(dve, l1)
            dve.wait_ge(ev("l1_summed"), 1)
            link(dve.tensor_copy(sT[:].rearrange("p a b -> p (a b)"), acc[:, :]), "l1_sT")
            link(dve.tensor_copy(degT[:].rearrange("p a b -> p (a b)"), counts[0:LO, :]), "degT_ready")
            for i in range(4 * GROUPS):
                dve.wait_ge(ev("upd_made"), i + 1)
                dve.tensor_tensor(gated[:, i % 2], bank[2 + i % 2][0:NP, :].rearrange("p (l i k) -> p l i k", l=2, i=F),
                                  h[:, 2 * i:2 * i + 2, :][:, :, :, None].to_broadcast([NP, 2, F, F]), ALU.mult
                                  ).then_inc(ev("upd_read"), 1)
                dve.wait_ge(ev("upd_read"), i + 1)
                ins = dve.tensor_reduce(t0[:, 2 * i:2 * i + 2, :], gated[:, i % 2].rearrange("p l i k -> p l k i"), AX.X, ALU.add)
                if i == 4 * GROUPS - 1:
                    link(ins)
                    link(dve.tensor_tensor(rooted[:], x[:], h[:], ALU.add), "u_raw")
            dve.wait_ge(ev("u_lin"), 1)
            link(dve.tensor_scalar(flat(t1), bank[1][0:NP, :], float(1.0 / np.float32(np.sqrt(F))), None, ALU.mult))
            link(dve.tensor_tensor(x[:], rooted[:], t1[:], ALU.add))
            layernorm("ln2", signal="l2a_h")
            dve.wait_ge(ev("deg_turned"), 1)
            link(dve.tensor_copy(stat[:], bank[4][0:NP, 0:LOCAL]))
            inverse_root("out_degree", out_scale)

            def split_nodes(source, event):
                part = [node_parts[:, k].rearrange("p c w -> p (c w)") for k in range(3)]
                link(dve.tensor_copy(part[0], flat(source)))
                link(dve.tensor_tensor(flat(t1), flat(source), part[0], ALU.subtract))
                link(dve.tensor_copy(part[1], flat(t1)))
                link(dve.tensor_tensor(part[2], flat(t1), part[1], ALU.subtract), event)

            def near_matches(into, what, pair):
                number = what[:].rearrange("p c j -> p (c j)")[:, bass.ds(pair * NEARS, NEARS)]
                return dve.tensor_tensor(into, count_key[:, None, 0:LO].to_broadcast([EP, NEARS, LO]),
                                         number[:, :, None].to_broadcast([EP, NEARS, LO]), ALU.is_equal)

            def near_begin(ph, pair):
                near_matches(near_is_lo[:], near_lo, pair).then_inc(near_los, 1)
                dve.wait_ge(near_hi_in, 16 * (pairs_before(ph) + pair + 1))
                for c in range(GROUPS):
                    ins = dve.tensor_scalar(near_one_hot[:, c, :], near_hi[:, :], node_hi[:, c:c + 1], None, ALU.is_equal)
                ins.then_inc(near_hot, 1)

            def near_finish(ph, pair):
                n = pairs_before(ph) + pair + 1
                if ph != "l3":
                    near_matches(near_is_type[:], near_type, pair)
                dve.wait_ge(near_gathered, n)
                dve.wait_ge(near_masked, n)
                dve.tensor_tensor(near_picked.rearrange("p t a f -> p (t a f)"), bank[0][0:EP, 0:NEARS * W],
                                  near_mask[:].rearrange("p t a f -> p (t a f)"), ALU.mult).then_inc(near_multiplied, 1)
                dve.wait_ge(near_multiplied, n)
                dve.tensor_reduce(near_row[:], near_picked.rearrange("p t a f -> p t f a"), AX.X, ALU.add).then_inc(near_summed, 1)
                if ph != "l3":
                    dve.wait_ge(near_summed, n)
                    dve.tensor_tensor(near_outer, near_row[:, :, None, :].to_broadcast([EP, NEARS, RELATIONS, F]),
                                      near_is_type[:, :, :, None].to_broadcast([EP, NEARS, RELATIONS, F]),
                                      ALU.mult).then_inc(near_outers, 1)

            def with_near(ph, chunk_body):
                near_begin(ph, 0)
                near_finish(ph, 0)
                near_begin(ph, 1)

                def body(pair, ahead1, ahead2):
                    chunk_body(2 * pair, pair, 0)
                    if ahead1:
                        near_finish(ph, pair + 1)
                    if ahead2:
                        near_begin(ph, pair + 2)
                    chunk_body(2 * pair + 1, pair, 1)
                near_pairs(dve, body)

            for k, bias in (("a", B1), ("b", B2)):
                ph = "l2" + k
                split_nodes(h, f"{ph}_parts_ready")
                dve.wait_ge(ev(f"{ph}_root_made"), 1)
                link(dve.tensor_tensor(rooted[:], bank[1][0:NP, :].rearrange("p (l f) -> p l f", f=F), row(bias), ALU.add))
                dve.wait_ge(ev(f"{ph}_wide_read"), 2 * GROUPS)
                link(dve.tensor_copy(stat[:, 0:1], stage2[:, 0:1]), f"{ph}_stage_ready")

                def l2(chunk, pair, s):
                    st = Steps(ph, chunk, s)
                    dve.wait_ge(fields_in[s], fields_in_by(ph, pair))
                    slot_free(ph, chunk)
                    st.mark(matches(is_lo[:, s], count_lo, s, DST_LO, LO))
                    one_hots(ph, s, (0,))
                    if s == 0:
                        dve.wait_ge(near_done, pairs_before(ph) + pair + 1)
                        dve.tensor_tensor(msg[:, :, FAR:T, :],
                                          bank[4][0:EP, 0:NEARS * F].rearrange("p (s t f) -> p s t f", s=2, t=NEAR),
                                          edge_norm[:, bass.ds(chunk * T, 2 * T)].rearrange("p (s t) -> p s t", s=2)[
                                              :, :, FAR:T, None].to_broadcast([EP, 2, NEAR, F]), ALU.mult)
                    dve.wait_ge(S[ph]["rows_in"][s], 16 * FAR * (pair + 1))
                    st.mark(dve.tensor_tensor(msg[:, s, 0:FAR, :], gathered2[:, s, 0:FAR, :],
                                              edge_norm[:, bass.ds(chunk * T, FAR)][:, :, None].to_broadcast([EP, FAR, F]), ALU.mult))
                    one_hots(ph, s, (1,))
                    st.wait("msg")
                    split(st, msg[:, s], lambda k: one_hots(ph, s, ((2, 3), (4, 5), (6, 7), ())[k]))
                    to_stationary(ph, chunk, s, parts, lambda: st.wait("low"))

                with_near(ph, l2)
                dve.wait_ge(added, before(ph) + CHUNKS)
                link(dve.tensor_copy(aggT[:].rearrange("p a b -> p (a b)"), acc[:, :]), f"{ph}_aggT")
                dve.wait_ge(ev(f"{ph}_agg"), 1)
                link(dve.tensor_tensor(flat(t0), bank[1][0:NP, :], flat(rooted), ALU.add))
                if k == "a":
                    link(dve.tensor_scalar(h[:], t0[:], 0.0, None, ALU.max), "l2b_h")
            link(dve.tensor_reduce(stat[:], t0[:], AX.X, ALU.max))
            link(dve.tensor_tensor(t0[:], t0[:], over(stat), ALU.subtract), "shifted")
            dve.wait_ge(ev("exp_done"), 1)
            link(dve.tensor_reduce(stat[:], t1[:], AX.X, ALU.add), "exp_sum")
            dve.wait_ge(ev("log_done"), 1)
            link(dve.tensor_tensor(t1[:], t0[:], over(stat2), ALU.subtract))
            link(dve.tensor_tensor(x[:], x[:], t1[:], ALU.add))
            layernorm("ln3")
            link(dve.tensor_tensor(t0[:], h[:], over(out_scale), ALU.mult), "l3_stage_ready")
            split_nodes(t0, "l3_parts_ready")

            def l3(chunk, pair, s):
                st = Steps("l3", chunk, s)
                dve.wait_ge(fields_in[s], fields_in_by("l3", pair))
                slot_free("l3", chunk)
                st.mark(matches(is_lo[:, s], count_lo, s, DST_LO, LO))
                if s == 0:
                    dve.wait_ge(near_summed, pairs_before("l3") + pair + 1)
                    dve.tensor_copy(gathered2[:, :, FAR:T, :], near_row[:].rearrange("p (s t) f -> p s t f", s=2)
                                    ).then_inc(ev("l3_near_placed"), 1)
                one_hots("l3", s, (0, 1))
                dve.wait_ge(S["l3"]["rows_in"][s], 16 * FAR * (pair + 1))
                dve.wait_ge(ev("l3_near_placed"), pair + 1)
                split(st, gathered2[:, s], lambda k: one_hots("l3", s, ((2, 3), (4, 5), (6, 7), ())[k]))
                to_stationary("l3", chunk, s, parts, lambda: st.wait("low"))

            with_near("l3", l3)
            dve.wait_ge(added, before("l3") + CHUNKS)
            link(dve.tensor_copy(aggT[:].rearrange("p a b -> p (a b)"), acc[:, :]), "l3_aggT")
            dve.wait_ge(ev("l3_agg"), 1)
            link(dve.tensor_tensor(t0[:], bank[1][0:NP, :].rearrange("p (l f) -> p l f", f=F), over(in_scale), ALU.mult))
            link(dve.tensor_tensor(t1[:], t0[:], x[:], ALU.add), "result_ready")


_INS = ["x", "src", "dst", "edge_attr_16", "edge_attr_8", "edge_type_8",
        "L0_gnn_W1", "L0_gnn_b1", "L0_gnn_W2", "L0_gnn_b2", "L0_gnn_root", "L0_gnn_bias", "L0_gnn_gamma", "L0_gnn_beta",
        "L1_gnn_W_msg_tp", "L1_gnn_W_msg_lin", "L1_gnn_W_upd_tp", "L1_gnn_W_upd_lin",
        "L2_gnn_W1", "L2_gnn_root1", "L2_gnn_b1", "L2_gnn_W2", "L2_gnn_root2", "L2_gnn_b2"]


def constants():
    part = np.arange(128)[:, None] // F % 3 == np.arange(3)[None, :]
    return {
        "c_valid": (np.arange(SLOTS) < N_NODES).reshape(NP, LOCAL).astype(np.float32),
        "c_ident": np.eye(128, dtype=np.float32),
        "c_hi": np.tile(np.arange(HI, dtype=np.float16), (EP, 1)),
        "c_key": np.tile(np.arange(LO * RELATIONS, dtype=np.float32), (EP, 1)),
        "c_part": part.astype(np.float32),
        "c_node_hi": np.arange(HI, dtype=np.float32).reshape(NP, GROUPS),
    }


def kernel(**inputs):
    import concourse.bacc as _bacc
    from concourse.bass_utils import run_bass_kernel_spmd as _run

    nc = _bacc.Bacc("TRN2", target_bir_lowering=False, num_devices=1)
    arrays, aps = {}, {}
    given = {k: np.ascontiguousarray(inputs[k]) for k in _INS}
    for name, a in {**given, **constants()}.items():
        arrays[f"in_{name}"] = a
        aps[name] = nc.dram_tensor(f"in_{name}", a.shape, mybir.dt.from_np(a.dtype), kind="ExternalInput").ap()
    out = nc.dram_tensor("out_0", (N_NODES, F), F32, kind="ExternalOutput").ap()
    build(nc, aps, out)
    r = _run(nc, [arrays], core_ids=[0])
    return r.results[0]["out_0"]
```

```python
import numpy as np
import concourse.bass as bass
from concourse import mybir
from contextlib import ExitStack

ALU = mybir.AluOpType
ACT = mybir.ActivationFunctionType
AX = mybir.AxisListType
F32 = mybir.dt.float32
BF16 = mybir.dt.bfloat16
F16 = mybir.dt.float16
I32 = mybir.dt.int32

N_NODES, F, RELATIONS = 3125, 16, 8
EP, T = 125, 8
E = 100000
TILES = E // EP
CHUNKS = TILES // T
PAIRS = CHUNKS // 2
NEAR1 = 1
FAR1 = T - NEAR1
NEARS1 = 2 * NEAR1
NEAR = 2
FAR = T - NEAR
NEARS = 2 * NEAR
LO = 8
LOCAL = 32
NP = -(-N_NODES // LOCAL)
GROUPS = LOCAL // LO
SLOTS = NP * LOCAL
HI = SLOTS // LO
FULL = N_NODES // LOCAL
REST = N_NODES - FULL * LOCAL
HID = F * F
PART = 3 * F
W = LO * F
ROW1 = F + RELATIONS
WIDE_LO = 128 // RELATIONS
WIDE_GROUPS = LOCAL // WIDE_LO
WIDE_HI = SLOTS // WIDE_LO
SRC_KEY, SRC_HI, SRC_LO, DST_HI, DST_LO, DST_WIDE_HI, DST_KEY, TYPE, FIELDS = range(9)
EPS = 1e-5


def build(nc, A, out):
    with ExitStack() as ctx:
        def sb(name, shape, dt=F32):
            return ctx.enter_context(nc.sbuf_tensor(name, shape, dt))

        def sem(name):
            return ctx.enter_context(nc.semaphore(name))

        events = {}

        def ev(name):
            if name not in events:
                events[name] = sem(name)
            return events[name]

        meta_d = nc.dram_tensor("edge_fields", [EP, CHUNKS, FIELDS * T], I32).ap()
        table0 = nc.dram_tensor("table_l0", [SLOTS, 2 * F], F32).ap()
        table1 = nc.dram_tensor("table_l1", [SLOTS, RELATIONS * F + RELATIONS], F32).ap()
        table2 = {"a": nc.dram_tensor("table_l2a", [SLOTS * RELATIONS, F], F32).ap(),
                  "b": nc.dram_tensor("table_l2b", [SLOTS * RELATIONS, F], F32).ap()}
        table3 = nc.dram_tensor("table_l3", [SLOTS, F], F32).ap()
        near_hi_d = nc.dram_tensor("near_hi_by_chunk", [CHUNKS, (NEAR + NEAR1) * EP], F16).ap()

        SCALAR_TILES = {"l0": 0, "l1": 5, "l2a": 2, "l2b": 2, "l3": 2}

        ident = sb("ident", [128, 128])
        ident16 = sb("ident16", [128, 128], BF16)
        count_hi = sb("count_hi", [EP, HI], F16)
        count_key = sb("count_key", [EP, WIDE_LO * RELATIONS])
        valid = sb("valid", [NP, LOCAL])
        part_of_row = sb("part_of_row", [128, 3])
        ones = sb("ones", [128, NP])

        w1 = sb("w1", [128, HID])
        w1_stack = sb("w1_stack", [128, HID], BF16)
        w1_hi = sb("w1_hi", [128, HID], BF16)
        w1_mid = sb("w1_mid", [128, HID], BF16)
        w1_rest = sb("w1_rest", [128, HID])
        w1_lo = sb("w1_lo", [128, HID])
        w2 = sb("w2", [128, 2, HID])
        b1 = sb("b1", [128, 2])
        SQUARE = ("b2", "root", "lin", "upd_lin", "root1", "root2")
        bd = {k: sb(f"bd_{k}", [128, W]) for k in SQUARE}
        on_diagonal = sb("on_diagonal", [128, LO])
        repeated = {k: sb(f"repeated_{k}", [128, F]) for k in ("b2", "root")}
        bd["msg"] = sb("bd_msg", [128, LO, RELATIONS * F])
        bd["upd"] = sb("bd_upd", [128, LO, HID])
        bd["rel1"] = sb("bd_rel1", [128, LO, RELATIONS, F])
        bd["rel2"] = sb("bd_rel2", [128, LO, RELATIONS, F])
        rows16 = sb("rows16", [NP, 5, F])
        BIAS, GAMMA, BETA, B1, B2 = range(5)

        x = sb("x_nodes", [NP, LOCAL, F])
        h = sb("h", [NP, LOCAL, F])
        t0 = sb("t0", [NP, LOCAL, F])
        t1 = sb("t1", [NP, LOCAL, F])
        rooted = sb("rooted", [NP, LOCAL, F])
        stat = sb("stat", [NP, LOCAL])
        stat2 = sb("stat2", [NP, LOCAL])
        chan = sb("chan", [NP, F])
        chan2 = sb("chan2", [NP, F])
        hT = sb("hT", [W, GROUPS, NP])
        aggT = sb("aggT", [W, NP, GROUPS])
        sT = sb("sT", [W, NP, GROUPS])
        cntT = sb("cntT", [128, NP, WIDE_GROUPS])
        cnt = sb("cnt", [NP, LOCAL * RELATIONS])
        degT = sb("degT", [LO, NP, GROUPS])
        in_scale = sb("in_scale", [NP, LOCAL])
        out_scale = sb("out_scale", [NP, LOCAL])
        stage0 = sb("stage0", [NP, LOCAL, 2 * F])
        room = sb("stage1", [EP, LOCAL * (RELATIONS * F + RELATIONS)])
        stage1 = room[0:NP, :].rearrange("p (l f) -> p l f", l=LOCAL)
        stage2 = room[0:NP, 0:LOCAL * RELATIONS * F]
        node_parts = sb("node_parts", [NP, 3, GROUPS, W], BF16)
        gated = sb("gated", [NP, 2, 2, F, F])

        src, dst, typ, work, work2 = (room[:, i * TILES:(i + 1) * TILES].bitcast(I32) for i in range(5))
        fields_all = sb("fields_all", [EP, CHUNKS, FIELDS, T], I32)
        reused = fields_all[:].rearrange("p c k t -> p (c k t)").bitcast(F32)
        used = [0]

        def reuse(*shape):
            size = int(np.prod(shape))
            at, used[0] = used[0], used[0] + size
            assert used[0] <= TILES * FIELDS
            names = " ".join("abcd"[:len(shape)])
            return reused[:, at:at + size].rearrange(f"p ({names}) -> p {names}", **dict(zip("abcd", shape)))

        row_numbers = sb("row_numbers", [EP, 2, T], I32)
        fields = sb("fields", [EP, 2, FIELDS, T], I32)
        edge_norm = sb("edge_norm", [EP, TILES])
        ea = sb("ea", [EP, 2, T, F])
        ea_rest = sb("ea_rest", [EP, T, F])
        ea_rest2 = sb("ea_rest2", [EP, T, F])
        ea8 = sb("ea8", [EP, 2, T, RELATIONS])
        stack = sb("stack", [EP, 2, T, 8, F], BF16)
        eaT = sb("eaT", [128, T * EP], BF16)
        h1T = sb("h1T", [128, 2, T * EP])
        gathered0 = sb("gathered0", [EP, 2, T, 2 * F])
        gathered1 = reuse(2, T, RELATIONS * F + RELATIONS)
        gathered2 = sb("gathered2", [EP, 2, T, F])
        near_hi_rows = sb("near_hi_rows", [CHUNKS, (NEAR + NEAR1) * EP], F16)
        near_hi = sb("near_hi", [NP, NEARS * EP], F16)
        near_lo = sb("near_lo", [EP, CHUNKS, NEAR])
        near_type = sb("near_type", [EP, CHUNKS, NEAR])
        near_lo1 = sb("near_lo1", [EP, CHUNKS, NEAR1])
        near_type1 = sb("near_type1", [EP, CHUNKS, NEAR1])
        near_ea8 = sb("near_ea8", [EP, CHUNKS, RELATIONS])
        message_weights = sb("message_weights", [RELATIONS * F, F])
        near_count = sb("near_count", [EP, NEARS1])
        near_row1 = sb("near_row1", [EP, NEARS1, ROW1])
        node_rows1 = reuse(LOCAL, ROW1)
        node_parts1 = reuse(3 * LOCAL * ROW1 // 2).bitcast(BF16).rearrange("p (k c w) -> p k c w", k=3, c=GROUPS)
        near_one_hot = sb("near_one_hot", [NP, GROUPS, NEARS * EP], BF16)
        near_is_lo = sb("near_is_lo", [EP, NEARS, LO])
        near_is_type = sb("near_is_type", [EP, NEARS, RELATIONS])
        near_mask = sb("near_mask", [EP, NEARS, LO, F], BF16)
        near_picked = reused[:, TILES * FIELDS - NEARS * W:].rearrange("p (t a f) -> p t a f", t=NEARS, a=LO)
        near_row = sb("near_row", [EP, NEARS, F])
        near_outer = reused[:, TILES * FIELDS - 2 * NEARS * W:TILES * FIELDS - NEARS * W].rearrange(
            "p (t r f) -> p t r f", t=NEARS, r=RELATIONS)
        near_outerT = sb("near_outerT", [128, NEARS * EP])
        relations = sb("relation_weights", [RELATIONS * F, 2, F])
        node_hi = sb("node_hi", [NP, GROUPS])
        product = sb("product", [EP, 2, 2, F, F])
        product1 = reuse(T, RELATIONS * F)
        msg = sb("msg", [EP, 2, T, F])
        raw = sb("raw", [EP, 2, T, F])
        rest = sb("rest", [EP, T, F])
        parts = sb("parts", [EP, 2, T, PART], BF16)
        is_lo = sb("is_lo", [EP, 2, T, LO])
        is_type = sb("is_type", [EP, T, RELATIONS])
        lo_bf = sb("lo_bf", [EP, 2, T, LO], BF16)
        mask = sb("mask", [EP, 2, T, LO, F], BF16)
        key_mask = sb("key_mask", [EP, 2, T, WIDE_LO * RELATIONS], BF16)
        distances = sb("distances", [EP, max(T * WIDE_HI, max(SCALAR_TILES.values()) * HI)], BF16)
        wide_one_hot = sb("wide_one_hot", [EP, 2, T, WIDE_HI], BF16)
        one_hot = sb("one_hot", [EP, 2, T, HI], BF16)
        stationary = sb("stationary", [EP, 2, 3, T, LO, F], BF16)
        zeros = sb("zeros", [EP, HI + W], BF16)
        zero_moving, zero_stationary = zeros[:, 0:HI], zeros[:, HI:]
        spare = sb("spare", [EP, 5])

        acc = ctx.enter_context(nc.psum_tensor("acc", [128, HI], F32))
        counts = ctx.enter_context(nc.psum_tensor("counts", [128, HI], F32))
        eaT_ps = ctx.enter_context(nc.psum_tensor("eaT_ps", [128, T, EP + 1], BF16))
        bank = [ctx.enter_context(nc.psum_tensor(f"bank{i}", [128, 512], F32)) for i in range(5)]

        PHASES = ("l0", "l1", "l2a", "l2b", "l3")
        S = {}
        for ph in PHASES:
            S[ph] = {
                "rows_in": [sem(f"{ph}_rows_in{s}") for s in range(2)],
                "step": sem(f"{ph}_vector_step"),
            }
        fields_in = [sem(f"fields_in{s}") for s in range(2)]
        numbers_in = [sem(f"row_numbers_in{s}") for s in range(2)]
        masked = sem("mask_ready")
        operands = sem("operands_ready")
        added = sem("chunk_added")

        def before(ph):
            return CHUNKS * PHASES.index(ph)

        def fields_in_by(ph, pair):
            return 16 * (before(ph) // 2 + pair + 1)

        TURNS = ("l0", "l1", "u", "l2a", "l2b")
        h_ready = sem("h_ready")
        h_turned = sem("h_turned")
        hT_ready = sem("hT_ready")

        def turn(name):
            return TURNS.index(name) + 1

        TABLE_STORES = {"l0": 1, "l1": GROUPS, "l2a": GROUPS, "l2b": GROUPS, "l3": 1}
        table_in = sem("table_in")

        def table_in_by(ph):
            return 16 * sum(TABLE_STORES[k] for k in PHASES[:PHASES.index(ph) + 1])

        near_hi_in = sem("near_hi_in")
        near_hot = sem("near_one_hots_ready")
        near_los = sem("near_lo_ready")
        near_masked = sem("near_mask_ready")
        near_gathered = sem("near_rows_in_psum")
        near_multiplied = sem("near_rows_masked")
        near_summed = sem("near_rows_ready")
        near_outers = sem("near_outer_ready")
        near_turned = sem("near_outer_transposed")
        near_copied = sem("near_outerT_ready")
        near_done = sem("near_messages_ready")
        near_counted = sem("near_counts_step")

        def tiles_in(ph):
            return {"l0": T, "l1": FAR1}.get(ph, FAR)

        def nears(ph):
            return NEARS1 if ph == "l1" else NEARS

        def pairs_before(ph):
            return PAIRS * ("l1", "l2a", "l2b", "l3").index(ph)

        distances_ready = sem("distances_ready")
        scalar_hot = sem("scalar_one_hots_ready")
        ea_in = [sem(f"ea_in{s}") for s in range(2)]
        ea8_in = [sem(f"ea8_in{s}") for s in range(2)]
        ea_copied = sem("ea_parts_copied")
        ea_split = sem("ea_rest_ready")
        ea_turned = sem("ea_transposed")
        eaT_ready = sem("eaT_ready")
        h1_made = sem("h1_made")
        h1_ready = sem("h1_relu_done")
        w_made = sem("edge_weights_made")
        w_used = sem("edge_weights_used")
        products_summed = sem("products_summed")
        silu_ready = sem("silu_ready")

        gathered = {"l0": gathered0, "l1": gathered1, "l2a": gathered2, "l2b": gathered2, "l3": gathered2}
        table = {"l0": table0, "l1": table1, "l2a": table2["a"], "l2b": table2["b"], "l3": table3}
        hi_field = {"l0": DST_HI, "l1": SRC_HI, "l2a": DST_HI, "l2b": DST_HI, "l3": DST_HI}
        ORDER = {
            "l0": ("is_lo", "msg", "hi", "rest", "mid", "low", "fields_read"),
            "l1": ("is_lo", "raw", "typed", "hi", "weighed", "rest", "rows_read", "mid", "low"),
            "l2a": ("is_lo", "msg", "hi", "rest", "mid", "low"),
            "l3": ("is_lo", "hi", "rest", "mid", "low"),
        }
        ORDER["l2b"] = ORDER["l2a"]
        FIELDS_READ = {"l0": "fields_read", "l1": "low", "l2a": "low", "l2b": "low", "l3": "low"}
        ROWS_READ = {"l0": "msg", "l1": "rows_read", "l2a": "msg", "l2b": "msg", "l3": "low"}

        def done(ph, name, chunk):
            return chunk * len(ORDER[ph]) + ORDER[ph].index(name) + 1

        def later(chunk, n):
            return not isinstance(chunk, int) or chunk >= n

        def all_chunks(eng, body):
            for s in range(2):
                body(s, 0, s)
            with eng.Fori(1, PAIRS) as pair:
                for s in range(2):
                    body(2 * pair + s, pair, s)

        def pairs_of_ends(eng, body):
            for s in range(2):
                body(s, 0, s, False)
            with eng.Fori(1, PAIRS - 1) as pair:
                for s in range(2):
                    body(2 * pair + s, pair, s, False)
            for s in range(2):
                body(CHUNKS - 2 + s, PAIRS - 1, s, s == 1)

        def near_pairs(eng, body):
            body(0, True, True)
            with eng.Fori(1, PAIRS - 2) as pair:
                body(pair, True, True)
            body(PAIRS - 2, True, False)
            body(PAIRS - 1, False, False)

        as_nodes = [(slice(0, FULL), slice(0, LOCAL), slice(0, FULL * LOCAL)),
                    (slice(FULL, NP), slice(0, REST), slice(FULL * LOCAL, N_NODES))]

        WIDE_BANKS = (2, 3, 0)

        block = ctx.enter_context(nc.Block())

        @block.sync
        def _(sp):
            sp.wait_ge(ev("x_cleared"), 1)
            for p, l, n in as_nodes:
                sp.dma_start(x[p, l, :], A["x"][n].rearrange("(p l) f -> p l f", l=l.stop)).then_inc(ev("x_in"), 16)
            sp.dma_start(src[:], A["src"].rearrange("(p t) -> p t", p=EP)).then_inc(ev("edges_in"), 16)
            sp.dma_start(dst[:], A["dst"].rearrange("(p t) -> p t", p=EP)).then_inc(ev("edges_in"), 16)
            sp.dma_start(typ[:], A["edge_type_8"].rearrange("(p t) -> p t", p=EP)).then_inc(ev("edges_in"), 16)
            for k, w in (("b2", A["L0_gnn_b2"].rearrange("(i o) -> i o", o=F)), ("root", A["L0_gnn_root"])):
                sp.dma_start(repeated[k][:], w[None].to_broadcast([LO, F, F])).then_inc(ev("l0_blocks_in"), 16)
            sp.dma_start(on_diagonal[:], A["c_diagonal"]).then_inc(ev("l0_blocks_in"), 16)
            sp.dma_start(ident[:], A["c_ident"]).then_inc(ev("ident_in"), 16)
            sp.dma_start(w1[:], A["L0_gnn_W1"][None].to_broadcast([128 // F, F, HID])).then_inc(ev("w1_in"), 16)
            sp.dma_start(part_of_row[:], A["c_part"]).then_inc(ev("w1_in"), 16)
            for a in range(2):
                sp.dma_start(b1[:, a:a + 1], A["L0_gnn_b1"][a * 128:(a + 1) * 128][:, None]).then_inc(ev("w1_in"), 16)

            ea_d = A["edge_attr_16"].rearrange("(p c t) f -> p c (t f)", p=EP, t=T)
            ea8_d = A["edge_attr_8"].rearrange("(p c t) f -> p c (t f)", p=EP, t=T)
            rows_d = {ph: A[k].rearrange("(p c t) -> p c t", p=EP, t=T) for ph, k in (("l0", "src"), ("l1", "dst"), ("l3", "src"))}

            def load_ea(chunk, s):
                sp.dma_start(ea[:, s].rearrange("p t f -> p (t f)"),
                             ea_d[:, bass.ds(chunk, 1), :].rearrange("p c n -> p (c n)")).then_inc(ea_in[s], 16)

            for s in range(2):
                load_ea(s, s)
            sp.dma_start(w2[:], A["L0_gnn_W2"].rearrange("(a p) n -> p a n", a=2)).then_inc(ev("w2_in"), 16)
            sp.dma_start(count_hi[:], A["c_hi"]).then_inc(ev("consts_in"), 16)
            sp.dma_start(count_key[:], A["c_key"]).then_inc(ev("consts_in"), 16)
            sp.dma_start(valid[:], A["c_valid"]).then_inc(ev("consts_in"), 16)
            sp.dma_start(node_hi[:], A["c_node_hi"]).then_inc(ev("consts_in"), 16)
            for i, k in enumerate(("L0_gnn_bias", "L0_gnn_gamma", "L0_gnn_beta", "L2_gnn_b1", "L2_gnn_b2")):
                sp.dma_start(rows16[:, i, :], A[k][None, :].to_broadcast([NP, F])).then_inc(ev("rows16_in"), 16)

            def store_fields(chunks):
                sp.dma_start(meta_d[:, chunks].rearrange("p c (k t) -> p c k t", k=FIELDS),
                             fields_all[:, chunks]).then_inc(ev("fields_stored"), 16)

            blocks = {"lin": A["L1_gnn_W_msg_lin"], "upd_lin": A["L1_gnn_W_upd_lin"],
                      "root1": A["L2_gnn_root1"], "root2": A["L2_gnn_root2"]}

            def later_copies(lo):
                rows = slice(lo * F, (lo + 1) * F)
                for k in ("lin", "upd_lin", "root1", "root2"):
                    sp.dma_start(bd[k][rows, rows], blocks[k]).then_inc(ev("diagonals_in"), 16)
                sp.dma_start(bd["msg"][rows, lo, :],
                             A["L1_gnn_W_msg_tp"].rearrange("i j h -> i (j h)")).then_inc(ev("diagonals_in"), 16)
                sp.dma_start(bd["upd"][rows, lo, :].rearrange("h (i k) -> h i k", k=F),
                             A["L1_gnn_W_upd_tp"].rearrange("i h k -> h i k")).then_inc(ev("diagonals_in"), 16)
                for k, w in (("rel1", "L2_gnn_W1"), ("rel2", "L2_gnn_W2")):
                    sp.dma_start(bd[k][rows, lo, :, :], A[w].rearrange("r i o -> i r o")).then_inc(ev("diagonals_in"), 16)

            def load_numbers(ph, chunk, pair, s):
                if later(chunk, 2):
                    sp.wait_ge(S[ph]["rows_in"][s], 16 * tiles_in(ph) * pair)
                if ph in rows_d:
                    rows = rows_d[ph][:, bass.ds(chunk, 1), :]
                else:
                    rows = meta_d[:, bass.ds(chunk, 1), SRC_KEY * T:(SRC_KEY + 1) * T]
                sp.dma_start(row_numbers[:, s, :], rows.rearrange("p c n -> p (c n)")).then_inc(numbers_in[s], 16)

            def load_near_hi(ph, pair):
                if later(pair, 1) or ph != "l1":
                    sp.wait_ge(near_hot, pairs_before(ph) + pair)
                n = nears(ph) // 2 * EP
                first = NEAR * EP if ph == "l1" else 0
                sp.dma_start(near_hi[:, 0:2 * n].rearrange("p (b n) -> p b n", b=2),
                             near_hi_d.rearrange("(a b) n -> a b n", b=2)[bass.ds(pair, 1), :, first:first + n].to_broadcast([NP, 2, n])
                             ).then_inc(near_hi_in, 16)

            def stream_near(ph):
                def body(pair, ahead1, ahead2):
                    for s in range(2):
                        chunk = 2 * pair + s
                        load_numbers(ph, chunk, pair, s)
                        if later(chunk, 2):
                            sp.wait_ge(distances_ready, before(ph) + chunk - 1)
                            sp.wait_ge(S[ph]["step"], done(ph, FIELDS_READ[ph], chunk - 2))
                            sp.sem_inc(ev("chunks_begun"), 1)
                        sp.dma_start(fields[:, s].rearrange("p k t -> p (k t)"),
                                     meta_d[:, bass.ds(chunk, 1), :].rearrange("p c n -> p (c n)")).then_inc(fields_in[s], 16)
                        if ph == "l1":
                            sp.dma_start(ea8[:, s].rearrange("p t f -> p (t f)"),
                                         ea8_d[:, bass.ds(chunk, 1), :].rearrange("p c n -> p (c n)")).then_inc(ea8_in[s], 16)
                        if s == 0 and isinstance(pair, int) and pair == 0:
                            load_near_hi(ph, 1)
                        if s == 1 and ahead2:
                            load_near_hi(ph, pair + 2)
                near_pairs(sp, body)

            def stream_l0():
                ph = "l0"

                def body(chunk, pair, s):
                    if later(chunk, 2):
                        load_numbers(ph, chunk, pair, s)
                        sp.wait_ge(ea_split, 2 * (chunk - 2) + 1)
                        load_ea(chunk, s)
                    if later(chunk, 2):
                        sp.wait_ge(distances_ready, before(ph) + chunk - 1)
                        sp.wait_ge(S[ph]["step"], done(ph, FIELDS_READ[ph], chunk - 2))
                        sp.sem_inc(ev("chunks_begun"), 1)
                    sp.dma_start(fields[:, s].rearrange("p k t -> p (k t)"),
                                 meta_d[:, bass.ds(chunk, 1), :].rearrange("p c n -> p (c n)")).then_inc(fields_in[s], 16)
                for chunk in range(2 + LO):
                    if chunk == 4:
                        sp.wait_ge(ev("fields_stored"), 32)
                    body(chunk, chunk // 2, chunk % 2)
                    if chunk == 1:
                        store_fields(slice(4, CHUNKS))
                    if chunk >= 2:
                        if chunk == 2:
                            for i in range(2):
                                sp.dma_start(relations[:, i, :],
                                             A[f"L2_gnn_W{i + 1}"].rearrange("r i o -> (r i) o")).then_inc(ev("diagonals_in"), 16)
                            sp.dma_start(message_weights[:],
                                         A["L1_gnn_W_msg_tp"].rearrange("i j h -> j i h")).then_inc(ev("diagonals_in"), 16)
                            sp.dma_start(near_ea8[:], ea8_d[:, :, FAR1 * RELATIONS:]).then_inc(ev("diagonals_in"), 16)
                            sp.wait_ge(ev("near_hi_turned"), 1)
                            sp.dma_start(near_hi_d, near_hi_rows[:]).then_inc(ev("near_hi_stored"), 16)
                            sp.wait_ge(ev("diagonals_cleared"), len(bd) - 2)
                        later_copies(chunk - 2)
                with sp.Fori((2 + LO) // 2, PAIRS) as pair:
                    for s in range(2):
                        body(2 * pair + s, pair, s)

            def store_table(ph, stage, where):
                sp.wait_ge(ev(f"{ph}_stage_ready"), 1)
                sp.dma_start(where, stage).then_inc(table_in, 16)

            def store_quarters(ph, stage, where):
                n = stage.shape[1] // GROUPS
                for c in range(GROUPS):
                    sp.wait_ge(ev(f"{ph}_wide_read"), 2 * (c + 1))
                    sp.dma_start(where[:, c * n:(c + 1) * n], stage[:, c * n:(c + 1) * n]).then_inc(table_in, 16)

            for s in range(2):
                load_numbers("l0", s, 0, s)
            store_table("l0", stage0[:].rearrange("p l f -> p (l f)"), table0.rearrange("(p l) f -> p (l f)", p=NP))
            sp.wait_ge(ev("fields_converted"), FIELDS - 1)
            sp.wait_ge(ev("row_keys_made"), 1)
            store_fields(slice(0, 4))
            sp.wait_ge(ev("fields_stored"), 16)
            stream_l0()
            sp.wait_ge(ev("near_hi_stored"), 16)
            load_near_hi("l1", 0)
            sp.wait_ge(ev("inverse_counts"), 1)
            store_quarters("l1", room[0:NP, :], table1.rearrange("(p l) f -> p (l f)", p=NP))
            stream_near("l1")
            for k in ("a", "b"):
                load_near_hi("l2" + k, 0)
                store_quarters("l2" + k, stage2, table2[k].rearrange("(p l) f -> p (l f)", p=NP))
                stream_near("l2" + k)
            load_near_hi("l3", 0)
            store_table("l3", t0[:].rearrange("p l f -> p (l f)"), table3.rearrange("(p l) f -> p (l f)", p=NP))
            stream_near("l3")
            sp.wait_ge(ev("result_ready"), 1)
            for p, l, n in as_nodes:
                sp.dma_start(out[n].rearrange("(p l) f -> p l f", l=l.stop), t1[p, l, :]).then_inc(ev("stored"), 16)
            sp.wait_ge(ev("stored"), 16 * len(as_nodes))

        @block.gpsimd
        def _(pool):
            pool.memset(x[:], 0.0).then_inc(ev("x_cleared"), 1)
            for k in (k for k in bd if k not in ("b2", "root")):
                pool.memset(bd[k][:], 0.0).then_inc(ev("diagonals_cleared"), 1)
            pool.memset(ones[:], 1.0).then_inc(ev("ones_set"), 1)

            def gathers(ph):
                pool.wait_ge(table_in, table_in_by(ph))

                def body(chunk, pair, s):
                    pool.wait_ge(numbers_in[s], fields_in_by(ph, pair))
                    if later(chunk, 2):
                        pool.wait_ge(S[ph]["step"], done(ph, ROWS_READ[ph], chunk - 2))
                    pool.sem_inc(ev("chunks_begun"), 1)
                    for t in range(tiles_in(ph)):
                        pool.indirect_dma_start(
                            out=gathered[ph][:, s, t, :], in_=table[ph], out_offset=None,
                            in_offset=bass.IndirectOffsetOnAxis(ap=row_numbers[:, s, t:t + 1], axis=0),
                        ).then_inc(S[ph]["rows_in"][s], 16)
                all_chunks(pool, body)

            for ph in PHASES:
                gathers(ph)

        @block.tensor
        def _(pe):
            def add_chunk(ph, chunk, s, tiles=range(T), first=False, last=False):
                for t in tiles:
                    for k in range(3):
                        mm = pe.matmul(acc[:, :], stationary[:, s, k, t, :, :].rearrange("p a b -> p (a b)"),
                                       one_hot[:, s, t, :], start=first and t == 0 and k == 0,
                                       stop=last and t == T - 1 and k == 2)
                    if ph == "l0":
                        mm = pe.matmul(counts[:, 0:WIDE_HI], key_mask[:, s, t, :], wide_one_hot[:, s, t, :],
                                       start=first and t == 0, stop=last and t == T - 1)
                    if ph == "l1":
                        mm = pe.matmul(counts[0:LO, :], lo_bf[:, s, t, :], one_hot[:, s, t, :],
                                       start=first and t == 0, stop=last and t == T - 1)
                if T - 1 in tiles:
                    mm.then_inc(added, 1)

            def turn_h(name):
                pe.wait_ge(h_ready, turn(name))
                for c in range(GROUPS):
                    mm = pe.transpose(bank[0][:, c * NP:(c + 1) * NP], h[:, c * LO:(c + 1) * LO, :].rearrange("p l f -> p (l f)"),
                                      ident[0:NP, 0:NP])
                mm.then_inc(h_turned, 1)
                pe.wait_ge(hT_ready, turn(name))

            def times(name, into, w):
                for c in range(GROUPS):
                    mm = pe.matmul(into[0:NP, c * W:(c + 1) * W], hT[:, c, :], bd[w][:, :], start=True, stop=True)
                mm.then_inc(ev(name), 1)

            def wide(name, w):
                flat = bd[w][:].rearrange("p a b c -> p (a b c)") if len(bd[w].shape) == 4 else bd[w][:].rearrange("p a b -> p (a b)")
                for i in range(2 * GROUPS):
                    if i >= 3:
                        pe.wait_ge(ev(f"{name}_wide_read"), i - 2)
                    pe.matmul(bank[WIDE_BANKS[i % 3]][0:NP, :], hT[:, i // 2, :], flat[:, (i % 2) * 512:(i % 2 + 1) * 512],
                              start=True, stop=True).then_inc(ev(f"{name}_wide"), 1)

            def turn_back(ph, source=None, ready=None):
                pe.wait_ge(ev(ready or f"{ph}_aggT"), 1)
                for c in range(GROUPS):
                    mm = pe.transpose(bank[1][0:NP, c * W:(c + 1) * W], (source or aggT)[:, :, c], ident[:, :])
                mm.then_inc(ev(f"{ph}_agg"), 1)

            pe.wait_ge(ev("ident_in"), 16)
            turn_h("l0")
            pe.wait_ge(ev("l0_diagonals"), 2)
            times("l0_b2_made", bank[1], "b2")
            times("l0_root_made", bank[2], "root")
            pe.wait_ge(ev("fields_converted"), 4)
            for j in range(NEAR):
                mm = pe.transpose(bank[4][0:CHUNKS, j * EP:(j + 1) * EP],
                                  fields_all[:, :, SRC_HI, FAR + j].bitcast(F32), ident[0:EP, 0:EP])
            for j in range(NEAR1):
                mm = pe.transpose(bank[4][0:CHUNKS, (NEAR + j) * EP:(NEAR + j + 1) * EP],
                                  fields_all[:, :, DST_HI, FAR1 + j].bitcast(F32), ident[0:EP, 0:EP])
            mm.then_inc(ev("near_hi_in_psum"), 1)

            pe.wait_ge(ev("ident16_made"), 1)
            pe.wait_ge(ev("zeros_set"), 1)
            pe.matmul(acc[:, :], zero_stationary, zero_moving, start=True, stop=False)
            pe.matmul(counts[:, 0:WIDE_HI], zero_stationary, zero_moving[:, 0:WIDE_HI], start=True, stop=False)

            def turn_ea(chunk, s):
                pe.wait_ge(ea_copied, 3 * (chunk + 1))
                if later(chunk, 1):
                    pe.wait_ge(eaT_ready, chunk)
                for t in range(T):
                    mm = pe.transpose(eaT_ps[:, t, 0:EP],
                                      stack[:, s, t, :, :].rearrange("p a b -> p (a b)"), ident16[0:EP, 0:EP])
                mm.then_inc(ea_turned, 1)

            def hidden(chunk, g):
                if g >= 2 or later(chunk, 1):
                    pe.wait_ge(h1_ready, 4 * chunk + g - 1)
                if g == 0:
                    pe.wait_ge(eaT_ready, chunk + 1)
                half, side = g % 2, g // 2
                pe.matmul(bank[g % 2][:, 0:4 * EP], w1_stack[:, half * 128:(half + 1) * 128],
                          eaT[:, side * 4 * EP:(side + 1) * 4 * EP], start=True, stop=True).then_inc(h1_made, 1)

            def edge_weights(chunk):
                pe.wait_ge(h1_ready, 4 * chunk + 4)
                for q in range(T // 2):
                    if q >= 2 or later(chunk, 1):
                        pe.wait_ge(w_used, 4 * chunk + q - 1)
                    for j in range(2):
                        t = 2 * q + j
                        for half in range(2):
                            mm = pe.matmul(bank[2 + q % 2][0:EP, j * HID:(j + 1) * HID],
                                           h1T[:, half, t * EP:(t + 1) * EP], w2[:, half, :],
                                           start=half == 0, stop=half == 1)
                    mm.then_inc(w_made, 1)

            def l0(chunk, pair, s, last):
                def part_of_sums(first, end):
                    if later(chunk, 2):
                        add_chunk("l0", chunk - 2, s, range(first, end))

                if later(chunk, 2):
                    pe.wait_ge(operands, before("l0") + chunk - 1)
                    pe.wait_ge(scalar_hot, before("l0") + chunk - 1)
                part_of_sums(0, 1)
                turn_ea(chunk, s)
                part_of_sums(1, 3)
                if not later(chunk, 1):
                    pe.wait_ge(ev("w1_stacked"), 1)
                hidden(chunk, 0)
                hidden(chunk, 1)
                part_of_sums(3, 5)
                hidden(chunk, 2)
                hidden(chunk, 3)
                part_of_sums(5, T)
                if not later(chunk, 1):
                    pe.wait_ge(ev("w2_in"), 16)
                    pe.wait_ge(ev("l0_rooted"), 1)
                edge_weights(chunk)
                if last:
                    for n in (CHUNKS - 2, CHUNKS - 1):
                        pe.wait_ge(operands, before("l0") + n + 1)
                        pe.wait_ge(scalar_hot, before("l0") + n + 1)
                        add_chunk("l0", n, n % 2, last=n == CHUNKS - 1)

            pairs_of_ends(pe, l0)
            turn_back("l0")
            pe.wait_ge(ev("ones_set"), 1)
            for k in ("mean", "var"):
                pe.wait_ge(ev(f"bn_{k}_in"), 1)
                pe.matmul(bank[0][0:NP, 0:F], ones[0:NP, :], chan[:, :], start=True, stop=True).then_inc(ev(f"bn_{k}_sum"), 1)
            pe.wait_ge(ev("cntT_ready"), 1)
            for c in range(WIDE_GROUPS):
                mm = pe.transpose(bank[4][0:NP, c * 128:(c + 1) * 128], cntT[:, :, c], ident[:, :])
            mm.then_inc(ev("cnt_turned"), 1)
            turn_h("l1")
            pe.wait_ge(ev("diagonals_in"), 16 * (8 * LO + 4))
            wide("l1", "msg")

            def near_rows(ph, pair):
                pe.wait_ge(near_hot, pairs_before(ph) + pair + 1)
                parts_of, n = (node_parts1, LO * ROW1) if ph == "l1" else (node_parts, W)
                for t in range(nears(ph)):
                    for c in range(GROUPS):
                        for k in range(3):
                            mm = pe.matmul(bank[0][0:EP, t * n:(t + 1) * n], near_one_hot[:, c, t * EP:(t + 1) * EP],
                                           parts_of[0:NP, k, c, :], start=c == 0 and k == 0, stop=c == GROUPS - 1 and k == 2)
                mm.then_inc(near_gathered, 1)

            def near_turn(ph, pair):
                pe.wait_ge(near_outers, pairs_before(ph) + pair + 1)
                for t in range(nears(ph)):
                    mm = pe.transpose(bank[1][:, t * EP:(t + 1) * EP], near_outer[:, t, :, :].rearrange("p r f -> p (r f)"),
                                      ident[0:EP, 0:EP])
                mm.then_inc(near_turned, 1)

            def near_messages(ph, pair):
                pe.wait_ge(near_copied, pairs_before(ph) + pair + 1)
                weights = message_weights[:, :] if ph == "l1" else relations[:, "ab".index(ph[2]), :]
                for t in range(nears(ph)):
                    mm = pe.matmul(bank[4][0:EP, t * F:(t + 1) * F], near_outerT[:, t * EP:(t + 1) * EP],
                                   weights, start=True, stop=True)
                mm.then_inc(near_done, 1)

            def sum_near(ph):
                pe.wait_ge(ev(f"{ph}_parts_ready"), 1)
                near_rows(ph, 0)
                if ph != "l3":
                    near_turn(ph, 0)
                    near_messages(ph, 0)
                near_rows(ph, 1)

                def body(pair, ahead1, ahead2):
                    pe.wait_ge(operands, before(ph) + 2 * pair + 1)
                    pe.wait_ge(scalar_hot, before(ph) + 2 * pair + 1)
                    add_chunk(ph, 2 * pair, 0, first=isinstance(pair, int) and pair == 0)
                    if ahead1 and ph != "l3":
                        near_turn(ph, pair + 1)
                    if ahead2:
                        near_rows(ph, pair + 2)
                    if ahead1 and ph != "l3":
                        near_messages(ph, pair + 1)
                    pe.wait_ge(operands, before(ph) + 2 * pair + 2)
                    pe.wait_ge(scalar_hot, before(ph) + 2 * pair + 2)
                    add_chunk(ph, 2 * pair + 1, 1, last=not ahead1)
                near_pairs(pe, body)

            pe.wait_ge(ev("l1_wide_read"), 2 * GROUPS)
            sum_near("l1")
            pe.wait_ge(ev("l1_sT"), 1)
            pe.matmul(bank[0][:, 0:HI], bd["lin"][:, :], sT[:].rearrange("p a b -> p (a b)"),
                      start=True, stop=True).then_inc(ev("l1_lin"), 1)
            pe.wait_ge(ev("degT_ready"), 1)
            for c in range(GROUPS):
                mm = pe.transpose(bank[4][0:NP, c * LO:(c + 1) * LO], degT[:, :, c], ident[0:LO, 0:LO])
            mm.then_inc(ev("deg_turned"), 1)
            pe.wait_ge(ev("l1_aggT"), 1)
            for i in range(4 * GROUPS):
                if i >= 2:
                    pe.wait_ge(ev("upd_read"), i - 1)
                c, q = divmod(i, 4)
                pe.matmul(bank[2 + i % 2][0:NP, :], aggT[:, :, c],
                          bd["upd"][:, 2 * q:2 * q + 2, :].rearrange("p a b -> p (a b)"),
                          start=True, stop=True).then_inc(ev("upd_made"), 1)
            turn_h("u")
            times("u_lin", bank[1], "upd_lin")
            for k in ("1", "2"):
                ph = "l2" + "ab"[int(k) - 1]
                turn_h(ph)
                wide(ph, "rel" + k)
                times(f"{ph}_root_made", bank[1], "root" + k)
                pe.wait_ge(ev(f"{ph}_wide_read"), 2 * GROUPS)
                pe.wait_ge(ev(f"{ph}_rooted"), 1)
                sum_near(ph)
                turn_back(ph)
            sum_near("l3")
            turn_back("l3")

        @block.scalar
        def _(act):
            def masks(ph, chunk, s):
                act.wait_ge(S[ph]["step"], done(ph, "is_lo", chunk))
                if later(chunk, 2):
                    act.wait_ge(operands, before(ph) + chunk - 1)
                if ph == "l1":
                    if later(chunk, 2):
                        act.wait_ge(added, before(ph) + chunk - 1)
                    act.copy(lo_bf[:, s], is_lo[:, s])
                act.copy(mask[:, s].rearrange("p t a f -> p (t a) f"),
                         is_lo[:, s].rearrange("p t a -> p (t a)")[:, :, None].to_broadcast([EP, T * LO, F])
                         ).then_inc(masked, 1)

            def hi_distances(ph, chunk, pair, s, begin=True, end=True):
                k, n = (DST_WIDE_HI, WIDE_HI) if ph == "l0" else (hi_field[ph], HI)
                tiles = list(enumerate(range(T - (T if ph == "l0" else SCALAR_TILES[ph]), T)))
                half = len(tiles) // 2
                if begin:
                    act.wait_ge(fields_in[s], fields_in_by(ph, pair))
                    if ph != "l0" or later(chunk, 1):
                        act.wait_ge(scalar_hot, before(ph) + chunk)
                for i, t in tiles[0 if begin else half:len(tiles) if end else half]:
                    ins = act.activation(distances[:, i * n:(i + 1) * n], count_hi[:, 0:n], ACT.Abs, scale=-1.0,
                                         bias=fields[:, s, k, t:t + 1].bitcast(F32))
                if end:
                    ins.then_inc(distances_ready, 1)

            def hi_one_hots(ph, chunk, s, reused):
                act.wait_ge(distances_ready, before(ph) + chunk + 1)
                if reused:
                    act.wait_ge(added, before(ph) + chunk - 1)
                into = wide_one_hot[:, s] if ph == "l0" else one_hot[:, s, T - SCALAR_TILES[ph]:T, :]
                into = into.rearrange("p t n -> p (t n)")
                act.activation(into, distances[:, 0:into.shape[1]], ACT.Relu, scale=-1.0, bias=ones[0:EP, 0:1]).then_inc(scalar_hot, 1)

            def turned(name):
                act.wait_ge(h_turned, turn(name))
                act.copy(hT[:].rearrange("p a b -> p (a b)"), bank[0][:, 0:HI]).then_inc(hT_ready, 1)

            def standard(name):
                act.wait_ge(ev(f"{name}_var"), 1)
                act.activation(stat2[:], stat[:], ACT.Sqrt).then_inc(ev(f"{name}_std"), 1)

            def relation_rows(name, stage):
                for i in range(2 * GROUPS):
                    act.wait_ge(ev(f"{name}_wide"), i + 1)
                    source = bank[WIDE_BANKS[i % 3]][0:NP, :]
                    if name == "l1":
                        ins = act.copy(stage[:, 4 * i:4 * i + 4, 0:RELATIONS * F],
                                       source.rearrange("p (a b) -> p a b", a=4))
                    else:
                        ins = act.copy(stage[:, 512 * i:512 * (i + 1)], source)
                    ins.then_inc(ev(f"{name}_wide_read"), 1)

            standard("ln0")
            turned("l0")
            act.wait_ge(ev("edges_in"), 48)
            act.copy(fields_all[:, :, TYPE, :].bitcast(F32), typ[:].rearrange("p (c t) -> p c t", t=T)
                     ).then_inc(ev("fields_converted"), 1)
            for n, k in enumerate((SRC_HI, SRC_LO, DST_HI, DST_LO, DST_WIDE_HI, DST_KEY)):
                act.wait_ge(ev("field_made"), n + 1)
                act.copy(fields_all[:, :, k, :].bitcast(F32), fields_all[:, :, k, :]).then_inc(ev("fields_converted"), 1)
            act.wait_ge(ev("near_hi_in_psum"), 1)
            act.copy(near_hi_rows[:], bank[4][0:CHUNKS, 0:(NEAR + NEAR1) * EP]).then_inc(ev("near_hi_turned"), 1)
            act.wait_ge(ev("w1_in"), 64)
            act.wait_ge(ev("ones_set"), 1)
            act.wait_ge(ev("consts_in"), 64)

            def spread(chunk, pair, s, k):
                if k == 0:
                    act.wait_ge(ea_in[s], 16 * (pair + 1))
                    if later(chunk, 2):
                        act.wait_ge(ea_turned, chunk - 1)
                else:
                    act.wait_ge(ea_split, 2 * chunk + k)
                source = (ea[:, s], ea_rest[:], ea_rest2[:])[k]
                n = 3 if k < 2 else 2
                act.copy(stack[:, s, :, 3 * k:3 * k + n, :],
                         source[:, :, None, :].to_broadcast([EP, T, n, F])).then_inc(ea_copied, 1)

            for k in range(3):
                spread(0, 0, 0, k)

            def l0(chunk, pair, s, last):
                act.wait_ge(ea_turned, chunk + 1)
                act.copy(eaT[:].rearrange("p (t e) -> p t e", t=T), eaT_ps[:, :, 0:EP]).then_inc(eaT_ready, 1)
                for g in range(4):
                    act.wait_ge(h1_made, 4 * chunk + g + 1)
                    half, side = g % 2, g // 2
                    act.activation(h1T[:, half, side * 4 * EP:(side + 1) * 4 * EP], bank[g % 2][:, 0:4 * EP], ACT.Relu,
                                   bias=b1[:, half:half + 1]).then_inc(h1_ready, 1)
                if later(chunk, 1):
                    hi_one_hots("l0", chunk - 1, 1 - s, later(chunk, 3))
                if not last:
                    spread(chunk + 1, pair + s, 1 - s, 0)
                masks("l0", chunk, s)
                hi_distances("l0", chunk, pair, s)
                if not last:
                    spread(chunk + 1, pair + s, 1 - s, 1)
                    spread(chunk + 1, pair + s, 1 - s, 2)
                else:
                    hi_one_hots("l0", chunk, s, True)

            pairs_of_ends(act, l0)
            act.wait_ge(ev("bn_var"), 1)
            act.activation(chan[:], chan2[:], ACT.Sqrt).then_inc(ev("bn_std"), 1)
            standard("ln1")
            turned("l1")
            relation_rows("l1", stage1)
            standard("in_degree")

            def silus(chunk, pair, s):
                scale = float(1.0 / np.float32(np.sqrt(F * RELATIONS)))
                if s == 0:
                    act.wait_ge(near_done, pairs_before("l1") + pair + 1)
                    if later(pair, 1):
                        act.wait_ge(operands, before("l1") + chunk)
                    act.activation(msg[:, :, FAR1:T, :], bank[4][0:EP, 0:NEARS1 * F].rearrange("p (s t f) -> p s t f", s=2, t=NEAR1),
                                   ACT.Silu, scale=scale)
                act.wait_ge(S["l1"]["step"], done("l1", "raw", chunk))
                act.activation(msg[:, s, 0:FAR1], raw[:, s, 0:FAR1], ACT.Silu, scale=scale).then_inc(silu_ready, 1)

            def near_masks(ph, pair):
                act.wait_ge(near_los, pairs_before(ph) + pair + 1)
                n, width = nears(ph) * LO, ROW1 if ph == "l1" else F
                act.copy(near_mask[:].rearrange("p t a f -> p (t a f)")[:, 0:n * width].rearrange("p (a f) -> p a f", f=width),
                         near_is_lo[:].rearrange("p t a -> p (t a)")[:, 0:n][:, :, None].to_broadcast([EP, n, width])
                         ).then_inc(near_masked, 1)

            def near_copy(ph, pair):
                act.wait_ge(near_turned, pairs_before(ph) + pair + 1)
                act.copy(near_outerT[:, 0:nears(ph) * EP], bank[1][:, 0:nears(ph) * EP]).then_inc(near_copied, 1)

            def masks_and_near(ph):
                near_masks(ph, 0)
                if ph != "l3":
                    near_copy(ph, 0)
                near_masks(ph, 1)

                def body(pair, ahead1, ahead2):
                    masks(ph, 2 * pair, 0)
                    hi_distances(ph, 2 * pair, pair, 0, end=ph != "l1")
                    if ph == "l1":
                        silus(2 * pair, pair, 0)
                        hi_distances(ph, 2 * pair, pair, 0, begin=False)
                    hi_one_hots(ph, 2 * pair, 0, later(pair, 1))
                    if ahead2:
                        near_masks(ph, pair + 2)
                    masks(ph, 2 * pair + 1, 1)
                    hi_distances(ph, 2 * pair + 1, pair, 1, end=ph != "l1")
                    if ph == "l1":
                        silus(2 * pair + 1, pair, 1)
                        hi_distances(ph, 2 * pair + 1, pair, 1, begin=False)
                    hi_one_hots(ph, 2 * pair + 1, 1, later(pair, 1))
                    if ahead1 and ph != "l3":
                        near_copy(ph, pair + 1)
                near_pairs(act, body)

            def preload(column, function):
                act.activation(spare[:, column:column + 1], spare[:, 0:1], function)

            act.wait_ge(ev("spare_set"), 1)
            preload(1, ACT.Silu)
            masks_and_near("l1")
            act.wait_ge(ev("l1_lin"), 1)
            act.mul(aggT[:].rearrange("p a b -> p (a b)"), bank[0][:, 0:HI],
                    float(1.0 / np.float32(np.sqrt(F)))).then_inc(ev("l1_aggT"), 1)
            act.wait_ge(ev("upd_summed"), 4 * GROUPS)
            act.activation(h[:], t0[:], ACT.Silu, scale=float(1.0 / np.float32(np.sqrt(F * F)))).then_inc(h_ready, 1)
            turned("u")
            standard("ln2")

            for ph in ("l2a", "l2b"):
                turned(ph)
                relation_rows(ph, stage2)
                if ph == "l2a":
                    standard("out_degree")
                masks_and_near(ph)
            preload(2, ACT.Exp)
            act.wait_ge(ev("shifted"), 1)
            act.activation(t1[:], t0[:], ACT.Exp).then_inc(ev("exp_done"), 1)
            preload(3, ACT.Ln)
            act.wait_ge(ev("exp_sum"), 1)
            act.activation(stat2[:], stat[:], ACT.Ln).then_inc(ev("log_done"), 1)
            preload(4, ACT.Sqrt)
            standard("ln3")
            masks_and_near("l3")

        @block.vector
        def _(dve):
            chained = sem("vector_chain")
            count = [0]

            def link(ins, event=None, value=1):
                if event:
                    signal = ev(event) if isinstance(event, str) else event
                    ins.then_inc(signal, 1)
                    dve.wait_ge(signal, value)
                    return
                count[0] += 1
                ins.then_inc(chained, 1)
                dve.wait_ge(chained, count[0])

            def over(v, n=F):
                return v[:, :, None].to_broadcast([NP, LOCAL, n])

            def row(i):
                return rows16[:, i, :][:, None, :].to_broadcast([NP, LOCAL, F])

            def layernorm(name, turned_as=None):
                link(dve.tensor_reduce(stat[:], x[:], AX.X, ALU.add))
                link(dve.scalar_tensor_tensor(t0[:], over(stat), -1.0 / F, x[:], ALU.mult, ALU.add))
                link(dve.tensor_tensor(t1[:], t0[:], t0[:], ALU.mult))
                link(dve.tensor_reduce(stat2[:], t1[:], AX.X, ALU.add))
                link(dve.tensor_scalar(stat[:], stat2[:], 1.0 / F, EPS, ALU.mult, ALU.add), f"{name}_var")
                dve.wait_ge(ev(f"{name}_std"), 1)
                link(dve.reciprocal(stat[:], stat2[:]))
                last = dve.scalar_tensor_tensor(h[:], t0[:], 0.0, over(stat), ALU.max, ALU.mult)
                if turned_as:
                    link(last, h_ready, turn(turned_as))
                else:
                    link(last)

            def inverse_root(name, into):
                link(dve.tensor_scalar(stat[:], stat[:], 1.0, None, ALU.max), f"{name}_var")
                dve.wait_ge(ev(f"{name}_std"), 1)
                link(dve.reciprocal(into[:], stat2[:]))

            def flat(t):
                return t[:].rearrange("p l f -> p (l f)")

            dve.memset(zeros[:], 0.0).then_inc(ev("zeros_set"), 1)
            dve.memset(spare[:], 1.0).then_inc(ev("spare_set"), 1)
            dve.wait_ge(ev("x_in"), 32)
            layernorm("ln0", turned_as="l0")
            for k in ("b2", "root"):
                dve.wait_ge(ev("l0_blocks_in"), 48)
                dve.tensor_tensor(bd[k][:].rearrange("p (a b) -> p a b", a=LO), on_diagonal[:, :, None].to_broadcast([128, LO, F]),
                                  repeated[k][:, None, :].to_broadcast([128, LO, F]), ALU.mult).then_inc(ev("l0_diagonals"), 1)

            dve.wait_ge(ev("edges_in"), 48)

            def by_chunk(v):
                return v[:].rearrange("p (c t) -> p c t", t=T)

            for v, k, shift, low in ((src, SRC_HI, 3, 0), (src, SRC_LO, 0, LO - 1), (dst, DST_HI, 3, 0), (dst, DST_LO, 0, LO - 1)):
                dve.tensor_scalar(fields_all[:, :, k, :], by_chunk(v), low or shift, None,
                                  ALU.bitwise_and if low else ALU.logical_shift_right).then_inc(ev("field_made"), 1)
            dve.tensor_copy(stage0[:, :, 0:F], h[:])
            dve.wait_ge(ev("l0_b2_made"), 1)
            dve.tensor_copy(stage0[:, :, F:2 * F], bank[1][0:NP, :].rearrange("p (l f) -> p l f", f=F)).then_inc(ev("l0_stage_ready"), 1)
            dve.tensor_scalar(fields_all[:, :, DST_WIDE_HI, :], by_chunk(dst), 4, None,
                              ALU.logical_shift_right).then_inc(ev("field_made"), 1)
            link(dve.tensor_scalar(work2[:], dst[:], WIDE_LO - 1, None, ALU.bitwise_and))
            link(dve.tensor_scalar(work[:], work2[:], 3, None, ALU.logical_shift_left))
            dve.tensor_tensor(fields_all[:, :, DST_KEY, :], by_chunk(work), by_chunk(typ), ALU.bitwise_or).then_inc(ev("field_made"), 1)
            link(dve.tensor_scalar(work2[:], src[:], 3, None, ALU.logical_shift_left))
            dve.tensor_tensor(fields_all[:, :, SRC_KEY, :], by_chunk(work2), by_chunk(typ), ALU.bitwise_or
                              ).then_inc(ev("row_keys_made"), 1)
            dve.wait_ge(ev("ident_in"), 16)
            dve.tensor_copy(ident16[:], ident[:]).then_inc(ev("ident16_made"), 1)
            def split_ea(chunk, s, k):
                source, into = ((ea[:, s], ea_rest), (ea_rest[:], ea_rest2))[k]
                dve.wait_ge(ea_copied, 3 * chunk + k + 1)
                dve.tensor_tensor(into[:], source, stack[:, s, :, 3 * k, :], ALU.subtract).then_inc(ea_split, 1)

            split_ea(0, 0, 0)
            dve.wait_ge(ev("w1_in"), 64)
            dve.wait_ge(ev("consts_in"), 64)
            link(dve.tensor_copy(w1_hi[:], w1[:]))
            link(dve.tensor_tensor(w1_rest[:], w1[:], w1_hi[:], ALU.subtract))
            split_ea(0, 0, 1)
            link(dve.tensor_copy(w1_mid[:], w1_rest[:]))
            link(dve.tensor_tensor(w1_lo[:], w1_rest[:], w1_mid[:], ALU.subtract))
            link(dve.tensor_scalar(w1_rest[:], w1_hi[:], part_of_row[:, 0:1], None, ALU.mult))
            link(dve.scalar_tensor_tensor(w1[:], w1_mid[:], part_of_row[:, 1:2], w1_rest[:], ALU.mult, ALU.add))
            dve.scalar_tensor_tensor(w1_stack[:], w1_lo[:], part_of_row[:, 2:3], w1[:], ALU.mult, ALU.add).then_inc(ev("w1_stacked"), 1)
            dve.wait_ge(ev("rows16_in"), 80)
            link(dve.tensor_tensor(t1[:], row(BIAS), over(valid), ALU.mult))
            dve.wait_ge(ev("l0_root_made"), 1)
            dve.tensor_tensor(flat(rooted), bank[2][0:NP, :], flat(t1), ALU.add).then_inc(ev("l0_rooted"), 1)
            dve.wait_ge(ev("fields_converted"), FIELDS - 1)
            dve.tensor_copy(near_lo1[:], fields_all[:, :, DST_LO, FAR1:T].bitcast(F32))
            dve.tensor_copy(near_type1[:], fields_all[:, :, TYPE, FAR1:T].bitcast(F32))
            dve.tensor_copy(near_lo[:], fields_all[:, :, SRC_LO, FAR:T].bitcast(F32))
            dve.tensor_copy(near_type[:], fields_all[:, :, TYPE, FAR:T].bitcast(F32))

            def scalar_field(s, k, t):
                return fields[:, s, k, t:t + 1].bitcast(F32)

            def matches(into, counted, s, k, n):
                return dve.tensor_tensor(into, counted[:, None, 0:n].to_broadcast([EP, T, n]),
                                         fields[:, s, k, :].bitcast(F32)[:, :, None].to_broadcast([EP, T, n]), ALU.is_equal)

            count_lo = count_key[:, 0:LO]

            class Steps:

                def __init__(self, ph, chunk, s):
                    self.ph, self.chunk, self.s = ph, chunk, s

                def mark(self, ins):
                    ins.then_inc(S[self.ph]["step"], 1)

                def wait(self, name):
                    dve.wait_ge(S[self.ph]["step"], done(self.ph, name, self.chunk))

            def one_hots(ph, s, tiles):
                for t in (t for t in tiles if t < T - SCALAR_TILES[ph]):
                    dve.tensor_scalar(one_hot[:, s, t, :], count_hi[:, :], scalar_field(s, hi_field[ph], t), None, ALU.is_equal)

            def slot_free(ph, chunk):
                if later(chunk, 2):
                    dve.wait_ge(added, before(ph) + chunk - 1)

            def split(st, source, between):
                s = st.s
                st.mark(dve.tensor_copy(parts[:, s, :, 0:F], source))
                between(0)
                st.wait("hi")
                st.mark(dve.tensor_tensor(rest[:], source, parts[:, s, :, 0:F], ALU.subtract))
                between(1)
                st.wait("rest")
                st.mark(dve.tensor_copy(parts[:, s, :, F:2 * F], rest[:]))
                between(2)
                st.wait("mid")
                st.mark(dve.tensor_tensor(parts[:, s, :, 2 * F:3 * F], rest[:], parts[:, s, :, F:2 * F], ALU.subtract))
                between(3)

            def to_stationary(ph, chunk, s, source, ready=None):
                dve.wait_ge(masked, before(ph) + chunk + 1)
                for k in range(3):
                    if k == 2 and ready:
                        ready()
                    ins = dve.tensor_tensor(stationary[:, s, k], mask[:, s],
                                            source[:, s, :, k * F:(k + 1) * F][:, :, None, :].to_broadcast([EP, T, LO, F]), ALU.mult)
                ins.then_inc(operands, 1)

            def l0(chunk, pair, s, last):
                st = Steps("l0", chunk, s)
                dve.wait_ge(fields_in[s], fields_in_by("l0", pair))
                st.mark(matches(is_lo[:, s], count_lo, s, DST_LO, LO))
                dve.wait_ge(S["l0"]["rows_in"][s], 16 * T * (pair + 1))

                def multiply(q):
                    dve.wait_ge(w_made, 4 * chunk + q + 1)
                    if q >= 2 or later(chunk, 1):
                        dve.wait_ge(products_summed, 4 * chunk + q - 1)
                    dve.tensor_tensor(product[:, q % 2], bank[2 + q % 2][0:EP, :].rearrange("p (t i o) -> p t i o", t=2, i=F),
                                      gathered0[:, s, 2 * q:2 * q + 2, 0:F][:, :, :, None].to_broadcast([EP, 2, F, F]),
                                      ALU.mult).then_inc(w_used, 1)

                def add_up(q):
                    dve.wait_ge(w_used, 4 * chunk + q + 1)
                    dve.tensor_reduce(raw[:, s, 2 * q:2 * q + 2, :], product[:, q % 2].rearrange("p t i o -> p t o i"),
                                      AX.X, ALU.add).then_inc(products_summed, 1)

                multiply(0)
                for q in range(1, T // 2):
                    multiply(q)
                    add_up(q - 1)
                    if q < 3 and not last:
                        split_ea(chunk + 1, 1 - s, q - 1)
                slot_free("l0", chunk)
                add_up(T // 2 - 1)
                one_hots("l0", s, (0,))
                dve.wait_ge(products_summed, 4 * chunk + 4)
                st.mark(dve.tensor_tensor(msg[:, s], raw[:, s], gathered0[:, s, :, F:2 * F], ALU.add))
                one_hots("l0", s, (1,))
                st.wait("msg")
                split(st, msg[:, s], lambda k: one_hots("l0", s, ((2, 3), (4, 5), (6,), (7,))[k]))
                st.mark(matches(key_mask[:, s], count_key, s, DST_KEY, WIDE_LO * RELATIONS))
                to_stationary("l0", chunk, s, parts, lambda: st.wait("low"))

            pairs_of_ends(dve, l0)
            def split_nodes(source, into, left, event):
                part = [into[0:NP, k].rearrange("p c w -> p (c w)") for k in range(3)]
                link(dve.tensor_copy(part[0], source))
                link(dve.tensor_tensor(left, source, part[0], ALU.subtract))
                link(dve.tensor_copy(part[1], left))
                link(dve.tensor_tensor(part[2], left, part[1], ALU.subtract), event)

            def near_matches(ph, into, what, pair):
                n = nears(ph)
                number = what[:].rearrange("p c j -> p (c j)")[:, bass.ds(pair * n, n)]
                return dve.tensor_tensor(into[:, 0:n], count_key[:, None, 0:LO].to_broadcast([EP, n, LO]),
                                         number[:, :, None].to_broadcast([EP, n, LO]), ALU.is_equal)

            def near_begin(ph, pair, first=0, end=1 + GROUPS):
                n = nears(ph) * EP
                for step in range(first, end):
                    if step == 0:
                        near_matches(ph, near_is_lo, near_lo1 if ph == "l1" else near_lo, pair).then_inc(near_los, 1)
                        continue
                    if step == 1:
                        dve.wait_ge(near_hi_in, 16 * (pairs_before(ph) + pair + 1))
                    c = step - 1
                    ins = dve.tensor_scalar(near_one_hot[:, c, 0:n], near_hi[:, 0:n], node_hi[:, c:c + 1], None, ALU.is_equal)
                    if step == GROUPS:
                        ins.then_inc(near_hot, 1)

            def near_finish(ph, pair, following=None):
                def fill(first, end):
                    if following is not None:
                        near_begin(ph, following, first, end)

                n = pairs_before(ph) + pair + 1
                count, width, row = (NEARS1, ROW1, near_row1) if ph == "l1" else (NEARS, F, near_row)
                if ph != "l3":
                    near_matches(ph, near_is_type, near_type1 if ph == "l1" else near_type, pair)
                dve.wait_ge(near_gathered, n)
                dve.wait_ge(near_masked, n)
                size = count * LO * width
                picked = near_picked.rearrange("p t a f -> p (t a f)")[:, 0:size]
                dve.tensor_tensor(picked, bank[0][0:EP, 0:size], near_mask[:].rearrange("p t a f -> p (t a f)")[:, 0:size],
                                  ALU.mult).then_inc(near_multiplied, 1)
                fill(0, 2)
                dve.wait_ge(near_multiplied, n)
                dve.tensor_reduce(row[:], picked.rearrange("p (t a f) -> p t f a", t=count, a=LO), AX.X, ALU.add).then_inc(near_summed, 1)
                fill(2, 3)
                if ph == "l3":
                    fill(3, 1 + GROUPS)
                    return
                dve.wait_ge(near_summed, n)
                if ph == "l1":
                    dve.tensor_tensor(near_is_type[:, 0:count], near_is_type[:, 0:count], row[:, :, F:ROW1],
                                      ALU.mult).then_inc(near_counted, 1)
                    factor = near_ea8[:, bass.ds(2 * pair, 2), :]
                else:
                    factor = near_is_type[:]
                dve.tensor_tensor(near_outer[:, 0:count], row[:, :, 0:F][:, :, None, :].to_broadcast([EP, count, RELATIONS, F]),
                                  factor[:, :, :, None].to_broadcast([EP, count, RELATIONS, F]),
                                  ALU.mult).then_inc(near_outers, 1)
                if ph != "l1":
                    fill(3, 1 + GROUPS)
                else:
                    dve.wait_ge(near_counted, 3 * pair + 1)
                    dve.tensor_reduce(near_count[:], near_is_type[:, 0:count], AX.X, ALU.add).then_inc(near_counted, 1)
                    fill(3, 4)
                    dve.wait_ge(near_counted, 3 * pair + 2)
                    dve.tensor_scalar(near_count[:], near_count[:], 1.0, None, ALU.max).then_inc(near_counted, 1)
                    fill(4, 5)
                    dve.wait_ge(near_counted, 3 * pair + 3)
                    dve.reciprocal(edge_norm[:, bass.ds(pair * 2 * T, 2 * T)].rearrange("p (s t) -> p s t", s=2)[:, :, FAR1:T],
                                   near_count[:].rearrange("p (s t) -> p s t", s=2))

            def with_near(ph, chunk_body):
                near_finish(ph, 0)
                near_begin(ph, 1)

                def body(pair, ahead1, ahead2):
                    chunk_body(2 * pair, pair, 0)
                    if ahead1:
                        near_finish(ph, pair + 1, pair + 2 if ahead2 else None)
                    chunk_body(2 * pair + 1, pair, 1)
                near_pairs(dve, body)

            dve.wait_ge(added, before("l0") + CHUNKS)
            dve.tensor_copy(aggT[:].rearrange("p a b -> p (a b)"), acc[:, :]).then_inc(ev("l0_aggT"), 1)
            dve.tensor_copy(cntT[:].rearrange("p a b -> p (a b)"), counts[:, 0:WIDE_HI]).then_inc(ev("cntT_ready"), 1)
            dve.wait_ge(ev("l0_agg"), 1)
            dve.wait_ge(ev("l0_rooted"), 1)
            link(dve.tensor_tensor(flat(t1), bank[1][0:NP, :], flat(rooted), ALU.add))

            def channels(v):
                return v[:, None, :].to_broadcast([NP, LOCAL, F])

            def by_channel(v):
                return v[:].rearrange("p l f -> p f l")

            link(dve.tensor_reduce(chan[:], by_channel(t1), AX.X, ALU.add), "bn_mean_in")
            dve.wait_ge(ev("bn_mean_sum"), 1)
            link(dve.tensor_scalar(chan2[:], bank[0][0:NP, 0:F], 1.0 / N_NODES, None, ALU.mult))
            link(dve.tensor_tensor(t0[:], t1[:], channels(chan2), ALU.subtract))
            link(dve.tensor_tensor(rooted[:], t0[:], over(valid), ALU.mult))
            link(dve.tensor_tensor(t1[:], rooted[:], rooted[:], ALU.mult))
            link(dve.tensor_reduce(chan[:], by_channel(t1), AX.X, ALU.add), "bn_var_in")
            dve.wait_ge(ev("bn_var_sum"), 1)
            link(dve.tensor_scalar(chan2[:], bank[0][0:NP, 0:F], 1.0 / N_NODES, EPS, ALU.mult, ALU.add), "bn_var")
            dve.wait_ge(ev("bn_std"), 1)
            link(dve.reciprocal(chan2[:], chan[:]))
            link(dve.tensor_tensor(chan[:], chan2[:], rows16[:, GAMMA, :], ALU.mult))
            link(dve.tensor_tensor(t1[:], t0[:], channels(chan), ALU.mult))
            link(dve.tensor_tensor(t0[:], t1[:], row(BETA), ALU.add))
            link(dve.scalar_tensor_tensor(x[:], t0[:], 0.0, x[:], ALU.max, ALU.add))
            layernorm("ln1", turned_as="l1")
            dve.wait_ge(ev("cnt_turned"), 1)
            link(dve.tensor_copy(cnt[:], bank[4][0:NP, 0:LOCAL * RELATIONS]))
            by_relation = cnt[:].rearrange("p (l r) -> p l r", r=RELATIONS)
            dve.tensor_copy(node_rows1[0:NP, :, 0:F], h[:])
            link(dve.tensor_copy(node_rows1[0:NP, :, F:ROW1], by_relation))
            link(dve.tensor_reduce(stat[:], by_relation, AX.X, ALU.add))
            link(dve.tensor_scalar(cnt[:], cnt[:], 1.0, None, ALU.max))
            dve.reciprocal(stage1[:, :, RELATIONS * F:], by_relation).then_inc(ev("inverse_counts"), 1)
            split_nodes(node_rows1[0:NP].rearrange("p l f -> p (l f)"), node_parts1,
                        gated[:].rearrange("p a b c d -> p (a b c d)")[:, 0:LOCAL * ROW1], "l1_parts_ready")
            near_begin("l1", 0)
            inverse_root("in_degree", in_scale)

            def l1(chunk, pair, s):
                st = Steps("l1", chunk, s)
                dve.wait_ge(fields_in[s], fields_in_by("l1", pair))
                slot_free("l1", chunk)
                st.mark(matches(is_lo[:, s], count_lo, s, SRC_LO, LO))
                dve.wait_ge(S["l1"]["rows_in"][s], 16 * FAR1 * (pair + 1))
                dve.wait_ge(ea8_in[s], 16 * (pair + 1))
                dve.tensor_tensor(product1[:, 0:FAR1].rearrange("p t (j h) -> p t j h", h=F),
                                  gathered1[:, s, 0:FAR1, 0:RELATIONS * F].rearrange("p t (j h) -> p t j h", h=F),
                                  ea8[:, s, 0:FAR1][:, :, :, None].to_broadcast([EP, FAR1, RELATIONS, F]), ALU.mult
                                  ).then_inc(ev("l1_products"), 1)
                one_hots("l1", s, (0,))
                dve.wait_ge(ev("l1_products"), chunk + 1)
                st.mark(dve.tensor_reduce(raw[:, s, 0:FAR1], product1[:, 0:FAR1].rearrange("p t (j h) -> p t h j", h=F), AX.X, ALU.add))
                st.mark(matches(is_type[:], count_lo, s, TYPE, RELATIONS))
                one_hots("l1", s, (1, 2))
                dve.wait_ge(silu_ready, chunk + 1)

                def edge_norms(k):
                    if k == 0:
                        st.wait("typed")
                        st.mark(dve.tensor_tensor(is_type[:, 0:FAR1], is_type[:, 0:FAR1], gathered1[:, s, 0:FAR1, RELATIONS * F:], ALU.mult))
                    if k == 1:
                        st.wait("weighed")
                        st.mark(dve.tensor_reduce(edge_norm[:, bass.ds(chunk * T, FAR1)], is_type[:, 0:FAR1], AX.X, ALU.add))

                split(st, msg[:, s], edge_norms)
                to_stationary("l1", chunk, s, parts, lambda: st.wait("low"))

            with_near("l1", l1)
            dve.wait_ge(added, before("l1") + CHUNKS)
            link(dve.tensor_copy(sT[:].rearrange("p a b -> p (a b)"), acc[:, :]), "l1_sT")
            link(dve.tensor_copy(degT[:].rearrange("p a b -> p (a b)"), counts[0:LO, :]), "degT_ready")
            link(dve.tensor_tensor(rooted[:], x[:], h[:], ALU.add))

            def gate(i):
                dve.wait_ge(ev("upd_made"), i + 1)
                if i >= 2:
                    dve.wait_ge(ev("upd_summed"), i - 1)
                dve.tensor_tensor(gated[:, i % 2], bank[2 + i % 2][0:NP, :].rearrange("p (l i k) -> p l i k", l=2, i=F),
                                  h[:, 2 * i:2 * i + 2, :][:, :, :, None].to_broadcast([NP, 2, F, F]), ALU.mult
                                  ).then_inc(ev("upd_read"), 1)

            gate(0)
            for i in range(4 * GROUPS):
                if i + 1 < 4 * GROUPS:
                    gate(i + 1)
                dve.wait_ge(ev("upd_read"), i + 1)
                dve.tensor_reduce(t0[:, 2 * i:2 * i + 2, :], gated[:, i % 2].rearrange("p l i k -> p l k i"), AX.X, ALU.add
                                  ).then_inc(ev("upd_summed"), 1)
            dve.wait_ge(ev("u_lin"), 1)
            link(dve.scalar_tensor_tensor(flat(x), bank[1][0:NP, :], float(1.0 / np.float32(np.sqrt(F))), flat(rooted),
                                          ALU.mult, ALU.add))
            layernorm("ln2", turned_as="l2a")

            for k, bias in (("a", B1), ("b", B2)):
                ph = "l2" + k
                split_nodes(flat(h), node_parts, flat(t1), f"{ph}_parts_ready")
                near_begin(ph, 0)
                if k == "a":
                    dve.wait_ge(ev("deg_turned"), 1)
                    link(dve.tensor_copy(stat[:], bank[4][0:NP, 0:LOCAL]))
                    inverse_root("out_degree", out_scale)
                dve.wait_ge(ev(f"{ph}_root_made"), 1)
                link(dve.tensor_tensor(rooted[:], bank[1][0:NP, :].rearrange("p (l f) -> p l f", f=F), row(bias), ALU.add),
                     f"{ph}_rooted")

                def l2(chunk, pair, s):
                    st = Steps(ph, chunk, s)
                    dve.wait_ge(fields_in[s], fields_in_by(ph, pair))
                    slot_free(ph, chunk)
                    st.mark(matches(is_lo[:, s], count_lo, s, DST_LO, LO))
                    one_hots(ph, s, (0,))
                    if s == 0:
                        dve.wait_ge(near_done, pairs_before(ph) + pair + 1)
                        dve.tensor_tensor(msg[:, :, FAR:T, :],
                                          bank[4][0:EP, 0:NEARS * F].rearrange("p (s t f) -> p s t f", s=2, t=NEAR),
                                          edge_norm[:, bass.ds(chunk * T, 2 * T)].rearrange("p (s t) -> p s t", s=2)[
                                              :, :, FAR:T, None].to_broadcast([EP, 2, NEAR, F]), ALU.mult)
                    dve.wait_ge(S[ph]["rows_in"][s], 16 * FAR * (pair + 1))
                    st.mark(dve.tensor_tensor(msg[:, s, 0:FAR, :], gathered2[:, s, 0:FAR, :],
                                              edge_norm[:, bass.ds(chunk * T, FAR)][:, :, None].to_broadcast([EP, FAR, F]), ALU.mult))
                    one_hots(ph, s, (1,))
                    st.wait("msg")
                    split(st, msg[:, s], lambda k: one_hots(ph, s, ((2, 3), (4, 5), (6, 7), ())[k]))
                    to_stationary(ph, chunk, s, parts, lambda: st.wait("low"))

                with_near(ph, l2)
                dve.wait_ge(added, before(ph) + CHUNKS)
                link(dve.tensor_copy(aggT[:].rearrange("p a b -> p (a b)"), acc[:, :]), f"{ph}_aggT")
                dve.wait_ge(ev(f"{ph}_agg"), 1)
                link(dve.tensor_tensor(flat(t0), bank[1][0:NP, :], flat(rooted), ALU.add))
                if k == "a":
                    link(dve.tensor_scalar(h[:], t0[:], 0.0, None, ALU.max), h_ready, turn("l2b"))
            link(dve.tensor_reduce(stat[:], t0[:], AX.X, ALU.max))
            link(dve.tensor_tensor(t0[:], t0[:], over(stat), ALU.subtract), "shifted")
            dve.wait_ge(ev("exp_done"), 1)
            link(dve.tensor_reduce(stat[:], t1[:], AX.X, ALU.add), "exp_sum")
            dve.wait_ge(ev("log_done"), 1)
            link(dve.tensor_tensor(t1[:], t0[:], over(stat2), ALU.subtract))
            link(dve.tensor_tensor(x[:], x[:], t1[:], ALU.add))
            layernorm("ln3")
            link(dve.tensor_tensor(t0[:], h[:], over(out_scale), ALU.mult), "l3_stage_ready")
            split_nodes(flat(t0), node_parts, flat(t1), "l3_parts_ready")
            near_begin("l3", 0)

            def l3(chunk, pair, s):
                st = Steps("l3", chunk, s)
                dve.wait_ge(fields_in[s], fields_in_by("l3", pair))
                slot_free("l3", chunk)
                st.mark(matches(is_lo[:, s], count_lo, s, DST_LO, LO))
                if s == 0:
                    dve.wait_ge(near_summed, pairs_before("l3") + pair + 1)
                    dve.tensor_copy(gathered2[:, :, FAR:T, :], near_row[:].rearrange("p (s t) f -> p s t f", s=2)
                                    ).then_inc(ev("l3_near_placed"), 1)
                one_hots("l3", s, (0, 1))
                dve.wait_ge(S["l3"]["rows_in"][s], 16 * FAR * (pair + 1))
                dve.wait_ge(ev("l3_near_placed"), pair + 1)
                split(st, gathered2[:, s], lambda k: one_hots("l3", s, ((2, 3), (4, 5), (6, 7), ())[k]))
                to_stationary("l3", chunk, s, parts, lambda: st.wait("low"))

            with_near("l3", l3)
            dve.wait_ge(added, before("l3") + CHUNKS)
            link(dve.tensor_copy(aggT[:].rearrange("p a b -> p (a b)"), acc[:, :]), "l3_aggT")
            dve.wait_ge(ev("l3_agg"), 1)
            link(dve.tensor_tensor(t0[:], bank[1][0:NP, :].rearrange("p (l f) -> p l f", f=F), over(in_scale), ALU.mult))
            link(dve.tensor_tensor(t1[:], t0[:], x[:], ALU.add), "result_ready")


_INS = ["x", "src", "dst", "edge_attr_16", "edge_attr_8", "edge_type_8",
        "L0_gnn_W1", "L0_gnn_b1", "L0_gnn_W2", "L0_gnn_b2", "L0_gnn_root", "L0_gnn_bias", "L0_gnn_gamma", "L0_gnn_beta",
        "L1_gnn_W_msg_tp", "L1_gnn_W_msg_lin", "L1_gnn_W_upd_tp", "L1_gnn_W_upd_lin",
        "L2_gnn_W1", "L2_gnn_root1", "L2_gnn_b1", "L2_gnn_W2", "L2_gnn_root2", "L2_gnn_b2"]


def constants():
    part = np.arange(128)[:, None] // F % 3 == np.arange(3)[None, :]
    return {
        "c_valid": (np.arange(SLOTS) < N_NODES).reshape(NP, LOCAL).astype(np.float32),
        "c_ident": np.eye(128, dtype=np.float32),
        "c_hi": np.tile(np.arange(HI, dtype=np.float16), (EP, 1)),
        "c_key": np.tile(np.arange(WIDE_LO * RELATIONS, dtype=np.float32), (EP, 1)),
        "c_part": part.astype(np.float32),
        "c_diagonal": (np.arange(128)[:, None] // F == np.arange(LO)[None, :]).astype(np.float32),
        "c_node_hi": np.arange(HI, dtype=np.float32).reshape(NP, GROUPS),
    }


def kernel(**inputs):
    import concourse.bacc as _bacc
    from concourse.bass_utils import run_bass_kernel_spmd as _run

    nc = _bacc.Bacc("TRN2", target_bir_lowering=False, num_devices=1)
    arrays, aps = {}, {}
    given = {k: np.ascontiguousarray(inputs[k]) for k in _INS}
    for name, a in {**given, **constants()}.items():
        arrays[f"in_{name}"] = a
        aps[name] = nc.dram_tensor(f"in_{name}", a.shape, mybir.dt.from_np(a.dtype), kind="ExternalInput").ap()
    out = nc.dram_tensor("out_0", (N_NODES, F), F32, kind="ExternalOutput").ap()
    build(nc, aps, out)
    r = _run(nc, [arrays], core_ids=[0])
    return r.results[0]["out_0"]
```
